# Optimizing a Trainium2 kernel written in Bass

```python
import numpy as np
import jax
import jax.numpy as jnp

def _softmax(x, axis=-1):
    return jax.nn.softmax(x, axis=axis)

def _gelu(x):
    return jax.nn.gelu(x, approximate=True)

def _silu(x):
    return jax.nn.silu(x)

def _sigmoid(x):
    return jax.nn.sigmoid(x)

def _layernorm(x, axis=-1, eps=1e-05):
    m = jnp.mean(x, axis=axis, keepdims=True)
    v = jnp.var(x, axis=axis, keepdims=True)
    return (x - m) / jnp.sqrt(v + eps)

def _scatter_add(tgt, idx, src, axis=0):
    return tgt.at[idx].add(src)

def _segment_sum(src, seg, n):
    return jax.ops.segment_sum(src, seg, n)
kernel_name = 'mk_decoder_preln_d4_seqx_r4_317585'

def setup_inputs(seed: int=0):
    np.random.seed(seed)
    _w = jnp.asarray

    def _rec_inputs():
        import jax
        import jax.numpy as jnp
        _rk = jax.random.key(seed)
        x = -0.0003929 + 0.9999 * jax.random.normal(jax.random.fold_in(_rk, 1), (8, 112, 256), jnp.float32)
        _lenS = 112 - jax.random.randint(jax.random.fold_in(_rk, 7), (8,), 0, max(1, 112 // 4) + 1, jnp.int32)
        _lenS2 = 375 - jax.random.randint(jax.random.fold_in(_rk, 8), (8,), 0, max(1, 375 // 4) + 1, jnp.int32)
        _ctx_512P = jax.random.normal(jax.random.fold_in(_rk, 11), (8, 16, 128), jnp.float32)
        _ctx_512c = jax.random.dirichlet(jax.random.fold_in(_rk, 511), 0.3 * jnp.ones((16,), jnp.float32), (8, 375))
        _ctx_512t = jnp.einsum('bsk,bkd->bsd', _ctx_512c, _ctx_512P)
        _ctx_512t = _ctx_512t * jax.lax.rsqrt(jnp.mean(jnp.square(_ctx_512t)) + 1e-12) * 0.953939
        ctx_512 = 4.13588e-05 + 0.999923 * (_ctx_512t + 0.3 * jax.random.normal(jax.random.fold_in(_rk, 611), (8, 375, 128), jnp.float32))
        return (x, ctx_512)
    x, ctx_512 = _rec_inputs()

    def _L0_attn_setup():
        import jax, jax.numpy as jnp
        import numpy as np
        B, S, D = (4, 256, 256)
        H, HKV, HD = (16, 4, 64)
        QD, KD, OH = (H * HD, HKV * HD, 64)

        def _lstm(x, Wih, Whh, b):
            xW = jnp.einsum('bsd,gd->sbg', x, Wih) + b
            h0 = jnp.zeros((x.shape[0], Whh.shape[1]), x.dtype)

            def step(carry, xt):
                h, c = carry
                gates = xt + h @ Whh.T
                i, f, g, o = jnp.split(gates, 4, axis=-1)
                c = jax.nn.sigmoid(f) * c + jax.nn.sigmoid(i) * jnp.tanh(g)
                h = jax.nn.sigmoid(o) * jnp.tanh(c)
                return ((h, c), h)
            _, hs = jax.lax.scan(step, (h0, h0), xW)
            return jnp.swapaxes(hs, 0, 1)

        def _mlp(h, W1, b1, W2, b2):
            return jax.nn.relu(h @ W1.T + b1) @ W2.T + b2
        key = jax.random.key(seed)
        ks = iter(jax.random.split(key, 32))
        n = lambda shape, s=0.02: jax.random.normal(next(ks), shape, dtype=jnp.float32) * s
        return {'hidden_states': jax.random.normal(next(ks), (B, S, D), dtype=jnp.float32), 'Wih_q': n((4 * D, D)), 'Whh_q': n((4 * D, D)), 'b_q': n((4 * D,)), 'Wih_k': n((4 * D, D)), 'Whh_k': n((4 * D, D)), 'b_k': n((4 * D,)), 'Wq1': n((OH, D)), 'bq1': n((OH,)), 'Wq2': n((QD, OH)), 'bq2': n((QD,)), 'Wk1': n((OH, D)), 'bk1': n((OH,)), 'Wk2': n((KD, OH)), 'bk2': n((KD,)), 'Wv': n((KD, D)), 'bv': n((KD,)), 'Wo': n((D, QD))}
    _L0_attn_all = _L0_attn_setup()
    _L0_attn_in = {k: v for k, v in _L0_attn_all.items() if k in ('Wih_q', 'Whh_q', 'b_q', 'Wih_k', 'Whh_k', 'b_k', 'Wq1', 'bq1', 'Wq2', 'bq2', 'Wk1', 'bk1', 'Wk2', 'bk2', 'Wv', 'bv', 'Wo')}
    del _L0_attn_all

    def _L0_xattn_setup():
        import jax, jax.numpy as jnp
        import numpy as np
        B, LQ, LK = (8, 512, 512)
        QD, KD, VD = (256, 128, 128)
        key = jax.random.key(seed)
        ks = jax.random.split(key, 9)
        s = 0.02
        return {'query': jax.random.normal(ks[0], (B, LQ, QD), jnp.float32), 'key': jax.random.normal(ks[1], (B, LK, KD), jnp.float32), 'value': jax.random.normal(ks[2], (B, LK, VD), jnp.float32), 'Wq': jax.random.normal(ks[3], (QD, QD), jnp.float32) * s, 'bq': jnp.zeros((QD,), jnp.float32), 'Wk': jax.random.normal(ks[4], (KD, QD), jnp.float32) * s, 'bk': jnp.zeros((QD,), jnp.float32), 'Wv': jax.random.normal(ks[5], (VD, QD), jnp.float32) * s, 'bv': jnp.zeros((QD,), jnp.float32)}
    _L0_xattn_all = _L0_xattn_setup()
    _L0_xattn_in = {k: v for k, v in _L0_xattn_all.items() if k in ('Wq', 'bq', 'Wk', 'bk', 'Wv', 'bv')}
    del _L0_xattn_all

    def _L0_ffn_setup():
        import jax, jax.numpy as jnp
        import numpy as np
        DIM = 256
        HIDDEN = 768
        SCALE = 1.0 / 127.0

        def _dequant(w_int, dtype):
            return w_int.astype(dtype) * jnp.asarray(SCALE, dtype)
        key = jax.random.key(seed)
        k_x, k_g, k_u, k_d = jax.random.split(key, 4)
        x = jax.random.normal(k_x, (4, 512, DIM), dtype=jnp.float32)
        w_gate = jax.random.randint(k_g, (HIDDEN, DIM), -127, 128, dtype=jnp.int32)
        w_up = jax.random.randint(k_u, (HIDDEN, DIM), -127, 128, dtype=jnp.int32)
        w_down = jax.random.randint(k_d, (DIM, HIDDEN), -127, 128, dtype=jnp.int32)
        return {'x': x, 'w_gate': w_gate, 'w_up': w_up, 'w_down': w_down}
    _L0_ffn_all = _L0_ffn_setup()
    _L0_ffn_in = {k: v for k, v in _L0_ffn_all.items() if k in ('w_gate', 'w_up', 'w_down')}
    del _L0_ffn_all

    def _L1_attn_setup():
        import jax, jax.numpy as jnp
        import numpy as np
        DIM = 256
        NUM_HEADS = 16
        HEAD_DIM = DIM // NUM_HEADS
        TAU = 1.0
        LAMBDA_JUMP = 0.6
        LAMBDA_LOCAL = 0.4
        MIN_ENTROPY = 0.5
        WINDOW = 3
        EPS = 1e-10

        def local_diffusion_kernel(seq_len, strength, window=WINDOW):
            i = jnp.arange(seq_len)
            d = i[:, None] - i[None, :]
            k = jnp.where(jnp.abs(d) <= window, jnp.exp(-d.astype(jnp.float32) ** 2 / (2.0 * strength ** 2)), 0.0)
            return k / (k.sum(axis=-1, keepdims=True) + EPS)
        key = jax.random.key(seed)
        ks = jax.random.split(key, 9)
        scale = 0.02
        x = jax.random.normal(ks[0], (2, 512, DIM), dtype=jnp.float32)
        Wq = jax.random.normal(ks[1], (DIM, DIM), dtype=jnp.float32) * scale
        bq = jax.random.normal(ks[2], (DIM,), dtype=jnp.float32) * scale
        Wk = jax.random.normal(ks[3], (DIM, DIM), dtype=jnp.float32) * scale
        bk = jax.random.normal(ks[4], (DIM,), dtype=jnp.float32) * scale
        Wv = jax.random.normal(ks[5], (DIM, DIM), dtype=jnp.float32) * scale
        bv = jax.random.normal(ks[6], (DIM,), dtype=jnp.float32) * scale
        Wo = jax.random.normal(ks[7], (DIM, DIM), dtype=jnp.float32) * scale
        bo = jax.random.normal(ks[8], (DIM,), dtype=jnp.float32) * scale
        return {'x': x, 'Wq': Wq, 'bq': bq, 'Wk': Wk, 'bk': bk, 'Wv': Wv, 'bv': bv, 'Wo': Wo, 'bo': bo}
    _L1_attn_all = _L1_attn_setup()
    _L1_attn_in = {k: v for k, v in _L1_attn_all.items() if k in ('Wq', 'bq', 'Wk', 'bk', 'Wv', 'bv', 'Wo', 'bo')}
    del _L1_attn_all

    def _L1_xattn_setup():
        import jax, jax.numpy as jnp
        import numpy as np
        HEADS = 16
        D_MODEL = 256
        IMG_MODEL = 128
        D_K = D_MODEL // HEADS
        key = jax.random.key(seed)
        ks = jax.random.split(key, 12)
        B, LQ, LKV = (8, 512, 256)
        s_dm = 1.0 / np.sqrt(D_MODEL)
        s_im = 1.0 / np.sqrt(IMG_MODEL)
        return {'q': jax.random.normal(ks[0], (B, LQ, D_MODEL), jnp.float32), 'k': jax.random.normal(ks[1], (B, LKV, IMG_MODEL), jnp.float32), 'v': jax.random.normal(ks[2], (B, LKV, IMG_MODEL), jnp.float32), 'Wq': jax.random.normal(ks[3], (D_MODEL, D_MODEL), jnp.float32) * s_dm, 'bq': jnp.zeros((D_MODEL,), jnp.float32), 'Wk': jax.random.normal(ks[4], (IMG_MODEL, D_MODEL), jnp.float32) * s_im, 'bk': jnp.zeros((D_MODEL,), jnp.float32), 'Wv': jax.random.normal(ks[5], (IMG_MODEL, D_MODEL), jnp.float32) * s_im, 'bv': jnp.zeros((D_MODEL,), jnp.float32), 'Wo': jax.random.normal(ks[6], (D_MODEL, D_MODEL), jnp.float32) * s_dm, 'bo': jnp.zeros((D_MODEL,), jnp.float32)}
    _L1_xattn_all = _L1_xattn_setup()
    _L1_xattn_in = {k: v for k, v in _L1_xattn_all.items() if k in ('Wq', 'bq', 'Wk', 'bk', 'Wv', 'bv', 'Wo', 'bo')}
    del _L1_xattn_all

    def _L1_ffn_setup():
        import jax, jax.numpy as jnp
        import numpy as np
        B, S, H = (2, 512, 256)
        E_DYN, E_FIX = (8, 1)
        I_DYN, I_FIX = (128, 512)
        TOP_K = 4
        TOP_P = 0.75
        JITTER_EPS = 0.1
        CAPACITY_FACTOR = 1.25
        MIN_CAPACITY = 4

        def _sparse_mixer(scores):
            T = scores.shape[0]
            rows = jnp.arange(T)
            masked_scores = scores
            mults, sels = ([], [])
            for _ in range(TOP_K):
                thr = jnp.max(masked_scores, axis=-1, keepdims=True)
                sel = jnp.argmax(masked_scores, axis=-1)
                factor = jnp.maximum(jnp.abs(scores), jnp.abs(thr))
                jmask = (thr - scores) / factor > 2.0 * JITTER_EPS
                gates = jax.nn.softmax(jnp.where(jmask, -jnp.inf, masked_scores), axis=-1)
                mult = jnp.take_along_axis(gates, sel[:, None], axis=-1)[:, 0]
                masked_scores = masked_scores.at[rows, sel].set(-jnp.inf)
                mults.append(mult)
                sels.append(sel)
            return (jnp.stack(mults, axis=-1), jnp.stack(sels, axis=-1))
        key = jax.random.key(seed)
        k = jax.random.split(key, 8)
        sc = 0.02
        return {'hidden_states': jax.random.normal(k[0], (B, S, H), jnp.float32), 'gate_w': jax.random.normal(k[1], (E_DYN + E_FIX, H), jnp.float32) * sc, 'dyn_gate_w': jax.random.normal(k[2], (E_DYN, I_DYN, H), jnp.float32) * sc, 'dyn_up_w': jax.random.normal(k[3], (E_DYN, I_DYN, H), jnp.float32) * sc, 'dyn_down_w': jax.random.normal(k[4], (E_DYN, H, I_DYN), jnp.float32) * sc, 'sh_gate_w': jax.random.normal(k[5], (E_FIX, I_FIX, H), jnp.float32) * sc, 'sh_up_w': jax.random.normal(k[6], (E_FIX, I_FIX, H), jnp.float32) * sc, 'sh_down_w': jax.random.normal(k[7], (E_FIX, H, I_FIX), jnp.float32) * sc}
    _L1_ffn_all = _L1_ffn_setup()
    _L1_ffn_in = {k: v for k, v in _L1_ffn_all.items() if k in ('gate_w', 'dyn_gate_w', 'dyn_up_w', 'dyn_down_w', 'sh_gate_w', 'sh_up_w', 'sh_down_w')}
    del _L1_ffn_all

    def _L2_attn_setup():
        import jax, jax.numpy as jnp
        import numpy as np
        B, T, HID = (16, 128, 256)
        NH, NKV, D = (8, 4, 128)
        THETA = 10000.0

        def _rotate_half(x):
            x1, x2 = (x[..., :x.shape[-1] // 2], x[..., x.shape[-1] // 2:])
            return jnp.concatenate((-x2, x1), axis=-1)
        key = jax.random.key(seed)
        k0, k1, k2, k3, k4 = jax.random.split(key, 5)
        s = 0.02
        return {'hidden_states': jax.random.normal(k0, (B, T, HID), dtype=jnp.float32), 'Wq': s * jax.random.normal(k1, (HID, NH * D), dtype=jnp.float32), 'Wk': s * jax.random.normal(k2, (HID, NKV * D), dtype=jnp.float32), 'Wv': s * jax.random.normal(k3, (HID, NKV * D), dtype=jnp.float32), 'Wo': s * jax.random.normal(k4, (NH * D, HID), dtype=jnp.float32)}
    _L2_attn_all = _L2_attn_setup()
    _L2_attn_in = {k: v for k, v in _L2_attn_all.items() if k in ('Wq', 'Wk', 'Wv', 'Wo')}
    del _L2_attn_all

    def _L2_xattn_setup():
        import jax, jax.numpy as jnp
        import numpy as np
        H, D, C1, C2, S, M, B, W = (16, 32, 256, 128, 512, 128, 2, 4)

        def _ln(x, g, b):
            m = jnp.mean(x, -1, keepdims=True)
            v = jnp.var(x, -1, keepdims=True)
            return (x - m) * jax.lax.rsqrt(v + 1e-05) * g + b

        def _mha(x, y, wq, wk, wv, li1_w, li1_b, lnx_g, lnx_b, lny_g, lny_b, ln3_g, ln3_b, li2_w, li2_b, li3_w, li3_b, causal):
            xn = _ln(x, lnx_g, lnx_b)
            yn = _ln(y, lny_g, lny_b)
            q = jnp.einsum('bsc,hcd->bhsd', xn, wq)
            k = jnp.einsum('btc,hcd->bhtd', yn, wk)
            v = jnp.einsum('btc,hcd->bhtd', yn, wv)
            a = jax.nn.softmax(jnp.einsum('bhsd,bhtd->bhst', q, k) * D ** (-0.5), axis=-1)
            if causal:
                s, t = (a.shape[-2], a.shape[-1])
                mask = (jnp.arange(t)[None, :] > jnp.arange(s)[:, None]).astype(a.dtype)
                a = a * mask
            o = jnp.einsum('bhst,bhtd->bhsd', a, v)
            o = o.transpose(0, 2, 1, 3).reshape(x.shape[0], x.shape[1], H * D)
            x_out = x + o @ li1_w + li1_b
            h = jax.nn.gelu(_ln(x_out, ln3_g, ln3_b) @ li2_w + li2_b, approximate=False)
            return x_out + h @ li3_w + li3_b
        key = jax.random.key(seed)
        ks = iter(jax.random.split(key, 64))

        def w(shape, scale=0.02):
            return jax.random.normal(next(ks), shape, jnp.float32) * scale
        inp = {'xx': jax.random.normal(next(ks), (B, S, C1), jnp.float32), 'ee': jax.random.normal(next(ks), (B, M, C2), jnp.float32), 'ln1_g': jnp.ones(C1, jnp.float32), 'ln1_b': jnp.zeros(C1, jnp.float32), 'ln2_g': jnp.ones(C1, jnp.float32), 'ln2_b': jnp.zeros(C1, jnp.float32)}
        for pfx, cy in (('a1', C1), ('a2', C2)):
            inp[pfx + '_wq'] = w((H, C1, D))
            inp[pfx + '_wk'] = w((H, cy, D))
            inp[pfx + '_wv'] = w((H, cy, D))
            inp[pfx + '_li1_w'] = w((H * D, C1))
            inp[pfx + '_li1_b'] = jnp.zeros(C1, jnp.float32)
            inp[pfx + '_lnx_g'] = jnp.ones(C1, jnp.float32)
            inp[pfx + '_lnx_b'] = jnp.zeros(C1, jnp.float32)
            inp[pfx + '_lny_g'] = jnp.ones(cy, jnp.float32)
            inp[pfx + '_lny_b'] = jnp.zeros(cy, jnp.float32)
            inp[pfx + '_ln3_g'] = jnp.ones(C1, jnp.float32)
            inp[pfx + '_ln3_b'] = jnp.zeros(C1, jnp.float32)
            inp[pfx + '_li2_w'] = w((C1, C1 * W))
            inp[pfx + '_li2_b'] = jnp.zeros(C1 * W, jnp.float32)
            inp[pfx + '_li3_w'] = w((C1 * W, C1))
            inp[pfx + '_li3_b'] = jnp.zeros(C1, jnp.float32)
        inp['training'] = 0
        return inp
    _L2_xattn_all = _L2_xattn_setup()
    _L2_xattn_in = {k: v for k, v in _L2_xattn_all.items() if k in ('ln1_g', 'ln1_b', 'ln2_g', 'ln2_b', 'a1_wq', 'a1_wk', 'a1_wv', 'a1_li1_w', 'a1_li1_b', 'a1_lnx_g', 'a1_lnx_b', 'a1_lny_g', 'a1_lny_b', 'a1_ln3_g', 'a1_ln3_b', 'a1_li2_w', 'a1_li2_b', 'a1_li3_w', 'a1_li3_b', 'a2_wq', 'a2_wk', 'a2_wv', 'a2_li1_w', 'a2_li1_b', 'a2_lnx_g', 'a2_lnx_b', 'a2_lny_g', 'a2_lny_b', 'a2_ln3_g', 'a2_ln3_b', 'a2_li2_w', 'a2_li2_b', 'a2_li3_w', 'a2_li3_b')}
    del _L2_xattn_all

    def _L2_ffn_setup():
        import jax, jax.numpy as jnp
        import numpy as np
        D_IN, D_HID = (256, 1024)

        def _ternary(key, shape):
            return jax.random.randint(key, shape, -1, 2).astype(jnp.float32)

        def _tlin(x, w, s):
            return jnp.einsum('bsi,oi->bso', x, w) * s
        key = jax.random.key(seed)
        ks = jax.random.split(key, 12)
        inv = lambda fan: 1.0 / np.sqrt(fan).astype(np.float32)
        return {'x': jax.random.normal(ks[0], (4, 512, D_IN), dtype=jnp.float32), 'w1_w': _ternary(ks[1], (D_HID, D_IN)), 'w1_s': jax.random.uniform(ks[2], (D_HID,), dtype=jnp.float32) * inv(D_IN), 'w2_w': _ternary(ks[3], (D_HID, D_IN)), 'w2_s': jax.random.uniform(ks[4], (D_HID,), dtype=jnp.float32) * inv(D_IN), 'h1_w': _ternary(ks[5], (D_HID, D_HID)), 'h1_s': jax.random.uniform(ks[6], (D_HID,), dtype=jnp.float32) * inv(D_HID), 'h2_w': _ternary(ks[7], (D_HID, D_HID)), 'h2_s': jax.random.uniform(ks[8], (D_HID,), dtype=jnp.float32) * inv(D_HID), 'w3_w': _ternary(ks[9], (D_IN, D_HID)), 'w3_s': jax.random.uniform(ks[10], (D_IN,), dtype=jnp.float32) * inv(D_HID)}
    _L2_ffn_all = _L2_ffn_setup()
    _L2_ffn_in = {k: v for k, v in _L2_ffn_all.items() if k in ('w1_w', 'w1_s', 'w2_w', 'w2_s', 'h1_w', 'h1_s', 'h2_w', 'h2_s', 'w3_w', 'w3_s')}
    del _L2_ffn_all

    def _L3_attn_setup():
        import jax, jax.numpy as jnp
        import numpy as np
        B, T, D_MODEL = (2, 256, 256)
        H, DEPTH = (8, 5)
        DH = D_MODEL // H
        key = jax.random.key(seed)
        k_x, k_wp, k_bp, k_wv, k_wo = jax.random.split(key, 5)
        x = jax.random.normal(k_x, (B, T, D_MODEL), dtype=jnp.float32)
        Wp = jax.random.normal(k_wp, (D_MODEL, H * DEPTH), dtype=jnp.float32) * 0.02
        bp = jnp.zeros((H * DEPTH,), dtype=jnp.float32)
        Wv = jax.random.normal(k_wv, (D_MODEL, D_MODEL), dtype=jnp.float32) * 0.02
        Wo = jax.random.normal(k_wo, (D_MODEL, D_MODEL), dtype=jnp.float32) * 0.02
        return {'x': x, 'Wp': Wp, 'bp': bp, 'Wv': Wv, 'Wo': Wo}
    _L3_attn_all = _L3_attn_setup()
    _L3_attn_in = {k: v for k, v in _L3_attn_all.items() if k in ('Wp', 'bp', 'Wv', 'Wo')}
    del _L3_attn_all

    def _L3_xattn_setup():
        import jax, jax.numpy as jnp
        import numpy as np
        DIM = 256
        LATENT_DIM = 128
        NUM_HEADS = 16
        HEAD_DIM = DIM // NUM_HEADS
        SCALE = HEAD_DIM ** (-0.5)
        key = jax.random.key(seed)
        k1, k2, k3, k4, k5 = jax.random.split(key, 5)
        B, xN, zN = (2, 512, 512)
        x = jax.random.normal(k1, (B, xN, DIM), dtype=jnp.float32)
        z = jax.random.normal(k2, (B, zN, LATENT_DIM), dtype=jnp.float32)
        Wq = jax.random.normal(k3, (DIM, DIM), dtype=jnp.float32) * DIM ** (-0.5)
        Wkv = jax.random.normal(k4, (2 * DIM, LATENT_DIM), dtype=jnp.float32) * LATENT_DIM ** (-0.5)
        Wo = jax.random.normal(k5, (DIM, DIM), dtype=jnp.float32) * DIM ** (-0.5)
        return {'x': x, 'z': z, 'Wq': Wq, 'Wkv': Wkv, 'Wo': Wo}
    _L3_xattn_all = _L3_xattn_setup()
    _L3_xattn_in = {k: v for k, v in _L3_xattn_all.items() if k in ('Wq', 'Wkv', 'Wo')}
    del _L3_xattn_all

    def _L3_ffn_setup():
        import jax, jax.numpy as jnp
        import numpy as np
        FP4_MAX = 6.0
        FP8_MAX = 448.0
        BLOCK = 16
        _FP4_VALS = jnp.array([0.0, 0.5, 1.0, 1.5, 2.0, 3.0, 4.0, 6.0], dtype=jnp.float32)
        _FP4_MIDS = jnp.array([0.25, 0.75, 1.25, 1.75, 2.5, 3.5, 5.0], dtype=jnp.float32)

        def fp4_global_scale(w):
            return FP8_MAX * FP4_MAX / jnp.max(jnp.abs(w))

        def fake_quant_nvfp4(x, global_scale):
            sh = x.shape
            xb = x.reshape(sh[:-1] + (sh[-1] // BLOCK, BLOCK))
            amax = jnp.max(jnp.abs(xb), axis=-1, keepdims=True)
            sc = jnp.clip(amax / FP4_MAX * global_scale, 0.0, FP8_MAX)
            sc8 = sc.astype(jnp.float8_e4m3fn).astype(jnp.float32)
            dq = sc8 / global_scale
            safe_dq = jnp.where(dq == 0.0, 1.0, dq)
            a = jnp.clip(jnp.abs(xb) / safe_dq, 0.0, FP4_MAX)
            q = jnp.sign(xb) * _FP4_VALS[jnp.digitize(a, _FP4_MIDS)]
            return (q * dq).reshape(sh)

        def nvfp4_linear(x, w, s_in):
            s_w = fp4_global_scale(w)
            xq = fake_quant_nvfp4(x, s_in)
            wq = fake_quant_nvfp4(w, s_w)
            return jnp.einsum('bsh,oh->bso', xq, wq)
        key = jax.random.key(seed)
        ks = jax.random.split(key, 6)
        B, S, H, I = (4, 512, 256, 1024)
        x = jax.random.normal(ks[0], (B, S, H), dtype=jnp.float32)
        gate_w = 0.05 * jax.random.normal(ks[1], (I, H), dtype=jnp.float32)
        up_w = 0.05 * jax.random.normal(ks[2], (I, H), dtype=jnp.float32)
        down_w = 0.05 * jax.random.normal(ks[3], (H, I), dtype=jnp.float32)
        s_in = (FP8_MAX * FP4_MAX / jnp.max(jnp.abs(jax.random.normal(ks[4], (1, H), dtype=jnp.float32)))).reshape(1)
        s_in_down = (FP8_MAX * FP4_MAX / jnp.max(jnp.abs(jax.random.normal(ks[5], (1, I), dtype=jnp.float32)))).reshape(1)
        return {'x': x, 'gate_w': gate_w, 'up_w': up_w, 'down_w': down_w, 's_in': s_in, 's_in_down': s_in_down}
    _L3_ffn_all = _L3_ffn_setup()
    _L3_ffn_in = {k: v for k, v in _L3_ffn_all.items() if k in ('gate_w', 'up_w', 'down_w', 's_in', 's_in_down')}
    del _L3_ffn_all
    return {'x': x, 'ctx_512': ctx_512, 'L0_attn_Wih_q': _L0_attn_in['Wih_q'], 'L0_attn_Whh_q': _L0_attn_in['Whh_q'], 'L0_attn_b_q': _L0_attn_in['b_q'], 'L0_attn_Wih_k': _L0_attn_in['Wih_k'], 'L0_attn_Whh_k': _L0_attn_in['Whh_k'], 'L0_attn_b_k': _L0_attn_in['b_k'], 'L0_attn_Wq1': _L0_attn_in['Wq1'], 'L0_attn_bq1': _L0_attn_in['bq1'], 'L0_attn_Wq2': _L0_attn_in['Wq2'], 'L0_attn_bq2': _L0_attn_in['bq2'], 'L0_attn_Wk1': _L0_attn_in['Wk1'], 'L0_attn_bk1': _L0_attn_in['bk1'], 'L0_attn_Wk2': _L0_attn_in['Wk2'], 'L0_attn_bk2': _L0_attn_in['bk2'], 'L0_attn_Wv': _L0_attn_in['Wv'], 'L0_attn_bv': _L0_attn_in['bv'], 'L0_attn_Wo': _L0_attn_in['Wo'], 'L0_xattn_Wq': _L0_xattn_in['Wq'], 'L0_xattn_bq': _L0_xattn_in['bq'], 'L0_xattn_Wk': _L0_xattn_in['Wk'], 'L0_xattn_bk': _L0_xattn_in['bk'], 'L0_xattn_Wv': _L0_xattn_in['Wv'], 'L0_xattn_bv': _L0_xattn_in['bv'], 'L0_ffn_w_gate': _L0_ffn_in['w_gate'], 'L0_ffn_w_up': _L0_ffn_in['w_up'], 'L0_ffn_w_down': _L0_ffn_in['w_down'], 'L1_attn_Wq': _L1_attn_in['Wq'], 'L1_attn_bq': _L1_attn_in['bq'], 'L1_attn_Wk': _L1_attn_in['Wk'], 'L1_attn_bk': _L1_attn_in['bk'], 'L1_attn_Wv': _L1_attn_in['Wv'], 'L1_attn_bv': _L1_attn_in['bv'], 'L1_attn_Wo': _L1_attn_in['Wo'], 'L1_attn_bo': _L1_attn_in['bo'], 'L1_xattn_Wq': _L1_xattn_in['Wq'], 'L1_xattn_bq': _L1_xattn_in['bq'], 'L1_xattn_Wk': _L1_xattn_in['Wk'], 'L1_xattn_bk': _L1_xattn_in['bk'], 'L1_xattn_Wv': _L1_xattn_in['Wv'], 'L1_xattn_bv': _L1_xattn_in['bv'], 'L1_xattn_Wo': _L1_xattn_in['Wo'], 'L1_xattn_bo': _L1_xattn_in['bo'], 'L1_ffn_gate_w': _L1_ffn_in['gate_w'], 'L1_ffn_dyn_gate_w': _L1_ffn_in['dyn_gate_w'], 'L1_ffn_dyn_up_w': _L1_ffn_in['dyn_up_w'], 'L1_ffn_dyn_down_w': _L1_ffn_in['dyn_down_w'], 'L1_ffn_sh_gate_w': _L1_ffn_in['sh_gate_w'], 'L1_ffn_sh_up_w': _L1_ffn_in['sh_up_w'], 'L1_ffn_sh_down_w': _L1_ffn_in['sh_down_w'], 'L2_attn_Wq': _L2_attn_in['Wq'], 'L2_attn_Wk': _L2_attn_in['Wk'], 'L2_attn_Wv': _L2_attn_in['Wv'], 'L2_attn_Wo': _L2_attn_in['Wo'], 'L2_xattn_ln1_g': _L2_xattn_in['ln1_g'], 'L2_xattn_ln1_b': _L2_xattn_in['ln1_b'], 'L2_xattn_ln2_g': _L2_xattn_in['ln2_g'], 'L2_xattn_ln2_b': _L2_xattn_in['ln2_b'], 'L2_xattn_a1_wq': _L2_xattn_in['a1_wq'], 'L2_xattn_a1_wk': _L2_xattn_in['a1_wk'], 'L2_xattn_a1_wv': _L2_xattn_in['a1_wv'], 'L2_xattn_a1_li1_w': _L2_xattn_in['a1_li1_w'], 'L2_xattn_a1_li1_b': _L2_xattn_in['a1_li1_b'], 'L2_xattn_a1_lnx_g': _L2_xattn_in['a1_lnx_g'], 'L2_xattn_a1_lnx_b': _L2_xattn_in['a1_lnx_b'], 'L2_xattn_a1_lny_g': _L2_xattn_in['a1_lny_g'], 'L2_xattn_a1_lny_b': _L2_xattn_in['a1_lny_b'], 'L2_xattn_a1_ln3_g': _L2_xattn_in['a1_ln3_g'], 'L2_xattn_a1_ln3_b': _L2_xattn_in['a1_ln3_b'], 'L2_xattn_a1_li2_w': _L2_xattn_in['a1_li2_w'], 'L2_xattn_a1_li2_b': _L2_xattn_in['a1_li2_b'], 'L2_xattn_a1_li3_w': _L2_xattn_in['a1_li3_w'], 'L2_xattn_a1_li3_b': _L2_xattn_in['a1_li3_b'], 'L2_xattn_a2_wq': _L2_xattn_in['a2_wq'], 'L2_xattn_a2_wk': _L2_xattn_in['a2_wk'], 'L2_xattn_a2_wv': _L2_xattn_in['a2_wv'], 'L2_xattn_a2_li1_w': _L2_xattn_in['a2_li1_w'], 'L2_xattn_a2_li1_b': _L2_xattn_in['a2_li1_b'], 'L2_xattn_a2_lnx_g': _L2_xattn_in['a2_lnx_g'], 'L2_xattn_a2_lnx_b': _L2_xattn_in['a2_lnx_b'], 'L2_xattn_a2_lny_g': _L2_xattn_in['a2_lny_g'], 'L2_xattn_a2_lny_b': _L2_xattn_in['a2_lny_b'], 'L2_xattn_a2_ln3_g': _L2_xattn_in['a2_ln3_g'], 'L2_xattn_a2_ln3_b': _L2_xattn_in['a2_ln3_b'], 'L2_xattn_a2_li2_w': _L2_xattn_in['a2_li2_w'], 'L2_xattn_a2_li2_b': _L2_xattn_in['a2_li2_b'], 'L2_xattn_a2_li3_w': _L2_xattn_in['a2_li3_w'], 'L2_xattn_a2_li3_b': _L2_xattn_in['a2_li3_b'], 'L2_ffn_w1_w': _L2_ffn_in['w1_w'], 'L2_ffn_w1_s': _L2_ffn_in['w1_s'], 'L2_ffn_w2_w': _L2_ffn_in['w2_w'], 'L2_ffn_w2_s': _L2_ffn_in['w2_s'], 'L2_ffn_h1_w': _L2_ffn_in['h1_w'], 'L2_ffn_h1_s': _L2_ffn_in['h1_s'], 'L2_ffn_h2_w': _L2_ffn_in['h2_w'], 'L2_ffn_h2_s': _L2_ffn_in['h2_s'], 'L2_ffn_w3_w': _L2_ffn_in['w3_w'], 'L2_ffn_w3_s': _L2_ffn_in['w3_s'], 'L3_attn_Wp': _L3_attn_in['Wp'], 'L3_attn_bp': _L3_attn_in['bp'], 'L3_attn_Wv': _L3_attn_in['Wv'], 'L3_attn_Wo': _L3_attn_in['Wo'], 'L3_xattn_Wq': _L3_xattn_in['Wq'], 'L3_xattn_Wkv': _L3_xattn_in['Wkv'], 'L3_xattn_Wo': _L3_xattn_in['Wo'], 'L3_ffn_gate_w': _L3_ffn_in['gate_w'], 'L3_ffn_up_w': _L3_ffn_in['up_w'], 'L3_ffn_down_w': _L3_ffn_in['down_w'], 'L3_ffn_s_in': _L3_ffn_in['s_in'], 'L3_ffn_s_in_down': _L3_ffn_in['s_in_down']}

def reference(x, ctx_512, L0_attn_Wih_q, L0_attn_Whh_q, L0_attn_b_q, L0_attn_Wih_k, L0_attn_Whh_k, L0_attn_b_k, L0_attn_Wq1, L0_attn_bq1, L0_attn_Wq2, L0_attn_bq2, L0_attn_Wk1, L0_attn_bk1, L0_attn_Wk2, L0_attn_bk2, L0_attn_Wv, L0_attn_bv, L0_attn_Wo, L0_xattn_Wq, L0_xattn_bq, L0_xattn_Wk, L0_xattn_bk, L0_xattn_Wv, L0_xattn_bv, L0_ffn_w_gate, L0_ffn_w_up, L0_ffn_w_down, L1_attn_Wq, L1_attn_bq, L1_attn_Wk, L1_attn_bk, L1_attn_Wv, L1_attn_bv, L1_attn_Wo, L1_attn_bo, L1_xattn_Wq, L1_xattn_bq, L1_xattn_Wk, L1_xattn_bk, L1_xattn_Wv, L1_xattn_bv, L1_xattn_Wo, L1_xattn_bo, L1_ffn_gate_w, L1_ffn_dyn_gate_w, L1_ffn_dyn_up_w, L1_ffn_dyn_down_w, L1_ffn_sh_gate_w, L1_ffn_sh_up_w, L1_ffn_sh_down_w, L2_attn_Wq, L2_attn_Wk, L2_attn_Wv, L2_attn_Wo, L2_xattn_ln1_g, L2_xattn_ln1_b, L2_xattn_ln2_g, L2_xattn_ln2_b, L2_xattn_a1_wq, L2_xattn_a1_wk, L2_xattn_a1_wv, L2_xattn_a1_li1_w, L2_xattn_a1_li1_b, L2_xattn_a1_lnx_g, L2_xattn_a1_lnx_b, L2_xattn_a1_lny_g, L2_xattn_a1_lny_b, L2_xattn_a1_ln3_g, L2_xattn_a1_ln3_b, L2_xattn_a1_li2_w, L2_xattn_a1_li2_b, L2_xattn_a1_li3_w, L2_xattn_a1_li3_b, L2_xattn_a2_wq, L2_xattn_a2_wk, L2_xattn_a2_wv, L2_xattn_a2_li1_w, L2_xattn_a2_li1_b, L2_xattn_a2_lnx_g, L2_xattn_a2_lnx_b, L2_xattn_a2_lny_g, L2_xattn_a2_lny_b, L2_xattn_a2_ln3_g, L2_xattn_a2_ln3_b, L2_xattn_a2_li2_w, L2_xattn_a2_li2_b, L2_xattn_a2_li3_w, L2_xattn_a2_li3_b, L2_ffn_w1_w, L2_ffn_w1_s, L2_ffn_w2_w, L2_ffn_w2_s, L2_ffn_h1_w, L2_ffn_h1_s, L2_ffn_h2_w, L2_ffn_h2_s, L2_ffn_w3_w, L2_ffn_w3_s, L3_attn_Wp, L3_attn_bp, L3_attn_Wv, L3_attn_Wo, L3_xattn_Wq, L3_xattn_Wkv, L3_xattn_Wo, L3_ffn_gate_w, L3_ffn_up_w, L3_ffn_down_w, L3_ffn_s_in, L3_ffn_s_in_down):
    import jax
    import jax.numpy as jnp

    def _L0_attn_ref(hidden_states, Wih_q, Whh_q, b_q, Wih_k, Whh_k, b_k, Wq1, bq1, Wq2, bq2, Wk1, bk1, Wk2, bk2, Wv, bv, Wo):
        import jax, jax.numpy as jnp
        import numpy as np
        B, S, D = (4, 256, 256)
        H, HKV, HD = (16, 4, 64)
        QD, KD, OH = (H * HD, HKV * HD, 64)

        def _lstm(x, Wih, Whh, b):
            xW = jnp.einsum('bsd,gd->sbg', x, Wih) + b
            h0 = jnp.zeros((x.shape[0], Whh.shape[1]), x.dtype)

            def step(carry, xt):
                h, c = carry
                gates = xt + h @ Whh.T
                i, f, g, o = jnp.split(gates, 4, axis=-1)
                c = jax.nn.sigmoid(f) * c + jax.nn.sigmoid(i) * jnp.tanh(g)
                h = jax.nn.sigmoid(o) * jnp.tanh(c)
                return ((h, c), h)
            _, hs = jax.lax.scan(step, (h0, h0), xW)
            return jnp.swapaxes(hs, 0, 1)

        def _mlp(h, W1, b1, W2, b2):
            return jax.nn.relu(h @ W1.T + b1) @ W2.T + b2
        bsz, q_len, _ = hidden_states.shape
        v = (hidden_states @ Wv.T + bv).reshape(bsz, q_len, HKV, HD).transpose(0, 2, 1, 3)
        hq = _lstm(hidden_states, Wih_q, Whh_q, b_q)
        hk = _lstm(hidden_states, Wih_k, Whh_k, b_k)
        q = _mlp(hq, Wq1, bq1, Wq2, bq2).reshape(bsz, q_len, H, HD).transpose(0, 2, 1, 3)
        k = _mlp(hk, Wk1, bk1, Wk2, bk2).reshape(bsz, q_len, HKV, HD).transpose(0, 2, 1, 3)
        groups = H // HKV
        k = jnp.repeat(k, groups, axis=1)
        v = jnp.repeat(v, groups, axis=1)
        scale = 1.0 / np.sqrt(HD)
        scores = jnp.einsum('bhsd,bhtd->bhst', q, k) * scale
        causal = jnp.tril(jnp.ones((q_len, q_len), dtype=bool))
        scores = jnp.where(causal, scores, jnp.finfo(scores.dtype).min)
        attn = jax.nn.softmax(scores, axis=-1)
        out = jnp.einsum('bhst,bhtd->bhsd', attn, v)
        out = out.transpose(0, 2, 1, 3).reshape(bsz, q_len, H * HD)
        return out @ Wo.T

    def _L0_xattn_ref(query, key, value, Wq, bq, Wk, bk, Wv, bv):
        import jax, jax.numpy as jnp
        import numpy as np
        B, LQ, LK = (8, 512, 512)
        QD, KD, VD = (256, 128, 128)
        q = jnp.einsum('bld,de->ble', query, Wq) + bq
        k = jnp.einsum('bld,de->ble', key, Wk) + bk
        v = jnp.einsum('bld,de->ble', value, Wv) + bv
        scores = jnp.einsum('bqe,bke->bqk', q, k)
        attn = jax.nn.softmax(scores, axis=-1)
        out = jnp.einsum('bqk,bke->bqe', attn, v)
        return out

    def _L0_ffn_ref(x, w_gate, w_up, w_down):
        import jax, jax.numpy as jnp
        import numpy as np
        DIM = 256
        HIDDEN = 768
        SCALE = 1.0 / 127.0

        def _dequant(w_int, dtype):
            return w_int.astype(dtype) * jnp.asarray(SCALE, dtype)
        wg = _dequant(w_gate, x.dtype)
        wu = _dequant(w_up, x.dtype)
        wd = _dequant(w_down, x.dtype)
        gate = jnp.einsum('bsd,hd->bsh', x, wg)
        up = jnp.einsum('bsd,hd->bsh', x, wu)
        h = jax.nn.silu(gate) * up
        return jnp.einsum('bsh,dh->bsd', h, wd)

    def _L1_attn_ref(x, Wq, bq, Wk, bk, Wv, bv, Wo, bo):
        import jax, jax.numpy as jnp
        import numpy as np
        DIM = 256
        NUM_HEADS = 16
        HEAD_DIM = DIM // NUM_HEADS
        TAU = 1.0
        LAMBDA_JUMP = 0.6
        LAMBDA_LOCAL = 0.4
        MIN_ENTROPY = 0.5
        WINDOW = 3
        EPS = 1e-10

        def local_diffusion_kernel(seq_len, strength, window=WINDOW):
            i = jnp.arange(seq_len)
            d = i[:, None] - i[None, :]
            k = jnp.where(jnp.abs(d) <= window, jnp.exp(-d.astype(jnp.float32) ** 2 / (2.0 * strength ** 2)), 0.0)
            return k / (k.sum(axis=-1, keepdims=True) + EPS)
        B, S, D = x.shape
        H, hd = (NUM_HEADS, HEAD_DIM)
        Q = (x @ Wq.T + bq).reshape(B, S, H, hd).transpose(0, 2, 1, 3)
        K = (x @ Wk.T + bk).reshape(B, S, H, hd).transpose(0, 2, 1, 3)
        V = (x @ Wv.T + bv).reshape(B, S, H, hd).transpose(0, 2, 1, 3)
        scores = jnp.einsum('bhqd,bhkd->bhqk', Q, K) / (TAU * np.sqrt(hd).astype(np.float32))
        A = jax.nn.softmax(scores, axis=-1)
        entropy = -jnp.sum(A * jnp.log(A + EPS), axis=-1, keepdims=True)
        stable = jax.lax.stop_gradient((entropy >= MIN_ENTROPY).astype(A.dtype))
        A = stable * A + (1.0 - stable) * jax.lax.stop_gradient(A)
        L = local_diffusion_kernel(S, LAMBDA_LOCAL)
        A_stable = LAMBDA_JUMP * A + (1.0 - LAMBDA_JUMP) * L[None, None, :, :]
        out = jnp.einsum('bhqk,bhkd->bhqd', A_stable, V)
        out = out.transpose(0, 2, 1, 3).reshape(B, S, D)
        return out @ Wo.T + bo

    def _L1_xattn_ref(q, k, v, Wq, bq, Wk, bk, Wv, bv, Wo, bo):
        import jax, jax.numpy as jnp
        import numpy as np
        HEADS = 16
        D_MODEL = 256
        IMG_MODEL = 128
        D_K = D_MODEL // HEADS
        B, LQ, _ = q.shape
        LKV = k.shape[1]
        qh = (q @ Wq + bq).reshape(B, LQ, HEADS, D_K).transpose(0, 2, 1, 3)
        kh = (k @ Wk + bk).reshape(B, LKV, HEADS, D_K).transpose(0, 2, 1, 3)
        vh = (v @ Wv + bv).reshape(B, LKV, HEADS, D_K).transpose(0, 2, 1, 3)
        scale = 1.0 / np.sqrt(D_K)
        scores = jnp.einsum('bhqd,bhkd->bhqk', qh, kh) * scale
        attn = jax.nn.softmax(scores, axis=-1)
        out = jnp.einsum('bhqk,bhkd->bhqd', attn, vh)
        concat = out.transpose(0, 2, 1, 3).reshape(B, LQ, D_MODEL)
        return concat @ Wo + bo

    def _L1_ffn_ref(hidden_states, gate_w, dyn_gate_w, dyn_up_w, dyn_down_w, sh_gate_w, sh_up_w, sh_down_w):
        import jax, jax.numpy as jnp
        import numpy as np
        B, S, H = (2, 512, 256)
        E_DYN, E_FIX = (8, 1)
        I_DYN, I_FIX = (128, 512)
        TOP_K = 4
        TOP_P = 0.75
        JITTER_EPS = 0.1
        CAPACITY_FACTOR = 1.25
        MIN_CAPACITY = 4

        def _sparse_mixer(scores):
            T = scores.shape[0]
            rows = jnp.arange(T)
            masked_scores = scores
            mults, sels = ([], [])
            for _ in range(TOP_K):
                thr = jnp.max(masked_scores, axis=-1, keepdims=True)
                sel = jnp.argmax(masked_scores, axis=-1)
                factor = jnp.maximum(jnp.abs(scores), jnp.abs(thr))
                jmask = (thr - scores) / factor > 2.0 * JITTER_EPS
                gates = jax.nn.softmax(jnp.where(jmask, -jnp.inf, masked_scores), axis=-1)
                mult = jnp.take_along_axis(gates, sel[:, None], axis=-1)[:, 0]
                masked_scores = masked_scores.at[rows, sel].set(-jnp.inf)
                mults.append(mult)
                sels.append(sel)
            return (jnp.stack(mults, axis=-1), jnp.stack(sels, axis=-1))
        Bv, Sv, Hv = hidden_states.shape
        T = Bv * Sv
        x = hidden_states.reshape(T, Hv)
        full_logits = x @ gate_w.T
        dyn_logits = full_logits[:, :E_DYN]
        probs = jax.nn.softmax(dyn_logits, axis=-1)
        sorted_p = jnp.sort(probs, axis=-1)[:, ::-1]
        csum = jnp.cumsum(sorted_p, axis=-1)
        dyn_k = jnp.minimum(jnp.sum(csum < TOP_P, axis=-1) + 1, TOP_K)
        mult, sel = _sparse_mixer(dyn_logits)
        slot_valid = jnp.arange(TOP_K)[None, :] < dyn_k[:, None]
        mult = jnp.where(slot_valid, mult, 0.0)
        rows = jnp.arange(T)
        rw = jnp.zeros((T, E_DYN), x.dtype).at[rows[:, None], sel].add(mult)
        rw = rw / jnp.sum(rw, axis=-1, keepdims=True)
        mask_dyn = (rw > 0).astype(jnp.int32)
        cap = max(int(np.ceil(T / E_DYN * CAPACITY_FACTOR)), MIN_CAPACITY)
        mask_dyn = mask_dyn * (jnp.cumsum(mask_dyn, axis=0) <= cap)
        expert_mask = jnp.concatenate([mask_dyn, jnp.ones((T, E_FIX), jnp.int32)], axis=-1)
        maskf = expert_mask.astype(x.dtype)
        gw = jax.nn.softmax(jnp.where(expert_mask == 0, -jnp.inf, full_logits), axis=-1)
        gd = rw * jnp.sum(gw[:, :E_DYN], axis=-1, keepdims=True)
        global_w = jnp.concatenate([gd, gw[:, E_DYN:]], axis=-1) * maskf
        g = jnp.einsum('th,eih->tei', x, dyn_gate_w)
        u = jnp.einsum('th,eih->tei', x, dyn_up_w)
        y_dyn = jnp.einsum('tei,ehi->teh', jax.nn.silu(g) * u, dyn_down_w)
        out = jnp.einsum('te,teh->th', global_w[:, :E_DYN], y_dyn)
        gs = jnp.einsum('th,fih->tfi', x, sh_gate_w)
        us = jnp.einsum('th,fih->tfi', x, sh_up_w)
        y_sh = jnp.einsum('tfi,fhi->tfh', jax.nn.silu(gs) * us, sh_down_w)
        out = out + jnp.einsum('tf,tfh->th', global_w[:, E_DYN:], y_sh)
        return out.reshape(Bv, Sv, Hv)

    def _L2_attn_ref(hidden_states, Wq, Wk, Wv, Wo):
        import jax, jax.numpy as jnp
        import numpy as np
        B, T, HID = (16, 128, 256)
        NH, NKV, D = (8, 4, 128)
        THETA = 10000.0

        def _rotate_half(x):
            x1, x2 = (x[..., :x.shape[-1] // 2], x[..., x.shape[-1] // 2:])
            return jnp.concatenate((-x2, x1), axis=-1)
        b, t, _ = hidden_states.shape
        q = (hidden_states @ Wq).reshape(b, t, NH, D).transpose(0, 2, 1, 3)
        k = (hidden_states @ Wk).reshape(b, t, NKV, D).transpose(0, 2, 1, 3)
        v = (hidden_states @ Wv).reshape(b, t, NKV, D).transpose(0, 2, 1, 3)
        inv_freq = 1.0 / THETA ** (jnp.arange(0, D, 2, dtype=jnp.float32) / D)
        freqs = jnp.outer(jnp.arange(t, dtype=jnp.float32), inv_freq)
        emb = jnp.concatenate((freqs, freqs), axis=-1)
        cos, sin = (jnp.cos(emb), jnp.sin(emb))
        q = q * cos + _rotate_half(q) * sin
        k = k * cos + _rotate_half(k) * sin
        groups = NH // NKV
        k = jnp.repeat(k, groups, axis=1)
        v = jnp.repeat(v, groups, axis=1)
        scale = 1.0 / jnp.sqrt(jnp.float32(D))
        attn = jnp.einsum('bhtd,bhsd->bhts', q, k) * scale
        causal = jnp.triu(jnp.ones((t, t), dtype=bool), k=1)
        attn = jnp.where(causal, -jnp.inf, attn)
        attn = jax.nn.softmax(attn, axis=-1)
        out = jnp.einsum('bhts,bhsd->bhtd', attn, v)
        out = out.transpose(0, 2, 1, 3).reshape(b, t, NH * D)
        return out @ Wo

    def _L2_xattn_ref(xx, ee, ln1_g, ln1_b, ln2_g, ln2_b, a1_wq, a1_wk, a1_wv, a1_li1_w, a1_li1_b, a1_lnx_g, a1_lnx_b, a1_lny_g, a1_lny_b, a1_ln3_g, a1_ln3_b, a1_li2_w, a1_li2_b, a1_li3_w, a1_li3_b, a2_wq, a2_wk, a2_wv, a2_li1_w, a2_li1_b, a2_lnx_g, a2_lnx_b, a2_lny_g, a2_lny_b, a2_ln3_g, a2_ln3_b, a2_li2_w, a2_li2_b, a2_li3_w, a2_li3_b, training):
        import jax, jax.numpy as jnp
        import numpy as np
        H, D, C1, C2, S, M, B, W = (16, 32, 256, 128, 512, 128, 2, 4)

        def _ln(x, g, b):
            m = jnp.mean(x, -1, keepdims=True)
            v = jnp.var(x, -1, keepdims=True)
            return (x - m) * jax.lax.rsqrt(v + 1e-05) * g + b

        def _mha(x, y, wq, wk, wv, li1_w, li1_b, lnx_g, lnx_b, lny_g, lny_b, ln3_g, ln3_b, li2_w, li2_b, li3_w, li3_b, causal):
            xn = _ln(x, lnx_g, lnx_b)
            yn = _ln(y, lny_g, lny_b)
            q = jnp.einsum('bsc,hcd->bhsd', xn, wq)
            k = jnp.einsum('btc,hcd->bhtd', yn, wk)
            v = jnp.einsum('btc,hcd->bhtd', yn, wv)
            a = jax.nn.softmax(jnp.einsum('bhsd,bhtd->bhst', q, k) * D ** (-0.5), axis=-1)
            if causal:
                s, t = (a.shape[-2], a.shape[-1])
                mask = (jnp.arange(t)[None, :] > jnp.arange(s)[:, None]).astype(a.dtype)
                a = a * mask
            o = jnp.einsum('bhst,bhtd->bhsd', a, v)
            o = o.transpose(0, 2, 1, 3).reshape(x.shape[0], x.shape[1], H * D)
            x_out = x + o @ li1_w + li1_b
            h = jax.nn.gelu(_ln(x_out, ln3_g, ln3_b) @ li2_w + li2_b, approximate=False)
            return x_out + h @ li3_w + li3_b
        x = _ln(xx, ln1_g, ln1_b)
        x = x + _mha(x, x, a1_wq, a1_wk, a1_wv, a1_li1_w, a1_li1_b, a1_lnx_g, a1_lnx_b, a1_lny_g, a1_lny_b, a1_ln3_g, a1_ln3_b, a1_li2_w, a1_li2_b, a1_li3_w, a1_li3_b, causal=True)
        x = _ln(x, ln2_g, ln2_b)
        return x + _mha(x, ee, a2_wq, a2_wk, a2_wv, a2_li1_w, a2_li1_b, a2_lnx_g, a2_lnx_b, a2_lny_g, a2_lny_b, a2_ln3_g, a2_ln3_b, a2_li2_w, a2_li2_b, a2_li3_w, a2_li3_b, causal=False)

    def _L2_ffn_ref(x, w1_w, w1_s, w2_w, w2_s, h1_w, h1_s, h2_w, h2_s, w3_w, w3_s):
        import jax, jax.numpy as jnp
        import numpy as np
        D_IN, D_HID = (256, 1024)

        def _ternary(key, shape):
            return jax.random.randint(key, shape, -1, 2).astype(jnp.float32)

        def _tlin(x, w, s):
            return jnp.einsum('bsi,oi->bso', x, w) * s
        h = jax.nn.silu(_tlin(x, w1_w, w1_s)) * _tlin(x, w2_w, w2_s)
        h = jax.nn.gelu(_tlin(h, h1_w, h1_s), approximate=False)
        h = jax.nn.gelu(_tlin(h, h2_w, h2_s), approximate=False)
        return _tlin(h, w3_w, w3_s)

    def _L3_attn_ref(x, Wp, bp, Wv, Wo):
        import jax, jax.numpy as jnp
        import numpy as np
        B, T, D_MODEL = (2, 256, 256)
        H, DEPTH = (8, 5)
        DH = D_MODEL // H
        Bx, Tx, d = x.shape
        paths = jax.nn.sigmoid(x @ Wp + bp)
        paths = paths.reshape(Bx, Tx, H, DEPTH).transpose(0, 2, 1, 3)
        pq = paths[:, :, :, None, :]
        pk = paths[:, :, None, :, :]
        agree = pq * pk + (1.0 - pq) * (1.0 - pk)
        sim = jnp.cumprod(agree, axis=-1).sum(axis=-1) / DEPTH
        mask = jnp.triu(jnp.ones((Tx, Tx), dtype=bool), k=1)
        sim = jnp.where(mask[None, None], -jnp.inf, sim)
        attn = jax.nn.softmax(sim, axis=-1)
        V = (x @ Wv).reshape(Bx, Tx, H, DH).transpose(0, 2, 1, 3)
        ctx = jnp.einsum('bhqk,bhkd->bhqd', attn, V)
        ctx = ctx.transpose(0, 2, 1, 3).reshape(Bx, Tx, d)
        return ctx @ Wo

    def _L3_xattn_ref(x, z, Wq, Wkv, Wo):
        import jax, jax.numpy as jnp
        import numpy as np
        DIM = 256
        LATENT_DIM = 128
        NUM_HEADS = 16
        HEAD_DIM = DIM // NUM_HEADS
        SCALE = HEAD_DIM ** (-0.5)
        B, xN, _ = x.shape
        _, zN, _ = z.shape
        Q = (x @ Wq.T).reshape(B, xN, NUM_HEADS, HEAD_DIM)
        KV = (z @ Wkv.T).reshape(B, zN, 2, NUM_HEADS, HEAD_DIM)
        K = KV[:, :, 0]
        V = KV[:, :, 1]
        attn = jnp.einsum('bqhd,bkhd->bhqk', Q, K) * SCALE
        attn = jax.nn.softmax(attn, axis=-1)
        O = jnp.einsum('bhqk,bkhd->bqhd', attn, V).reshape(B, xN, DIM)
        return O @ Wo.T

    def _L3_ffn_ref(x, gate_w, up_w, down_w, s_in, s_in_down):
        import jax, jax.numpy as jnp
        import numpy as np
        FP4_MAX = 6.0
        FP8_MAX = 448.0
        BLOCK = 16
        _FP4_VALS = jnp.array([0.0, 0.5, 1.0, 1.5, 2.0, 3.0, 4.0, 6.0], dtype=jnp.float32)
        _FP4_MIDS = jnp.array([0.25, 0.75, 1.25, 1.75, 2.5, 3.5, 5.0], dtype=jnp.float32)

        def fp4_global_scale(w):
            return FP8_MAX * FP4_MAX / jnp.max(jnp.abs(w))

        def fake_quant_nvfp4(x, global_scale):
            sh = x.shape
            xb = x.reshape(sh[:-1] + (sh[-1] // BLOCK, BLOCK))
            amax = jnp.max(jnp.abs(xb), axis=-1, keepdims=True)
            sc = jnp.clip(amax / FP4_MAX * global_scale, 0.0, FP8_MAX)
            sc8 = sc.astype(jnp.float8_e4m3fn).astype(jnp.float32)
            dq = sc8 / global_scale
            safe_dq = jnp.where(dq == 0.0, 1.0, dq)
            a = jnp.clip(jnp.abs(xb) / safe_dq, 0.0, FP4_MAX)
            q = jnp.sign(xb) * _FP4_VALS[jnp.digitize(a, _FP4_MIDS)]
            return (q * dq).reshape(sh)

        def nvfp4_linear(x, w, s_in):
            s_w = fp4_global_scale(w)
            xq = fake_quant_nvfp4(x, s_in)
            wq = fake_quant_nvfp4(w, s_w)
            return jnp.einsum('bsh,oh->bso', xq, wq)
        gate_out = nvfp4_linear(x, gate_w, s_in[0])
        up_out = nvfp4_linear(x, up_w, s_in[0])
        hidden = jax.nn.silu(gate_out) * up_out
        return nvfp4_linear(hidden, down_w, s_in_down[0])
    x = x + _L0_attn_ref(_layernorm(x, axis=-1), L0_attn_Wih_q, L0_attn_Whh_q, L0_attn_b_q, L0_attn_Wih_k, L0_attn_Whh_k, L0_attn_b_k, L0_attn_Wq1, L0_attn_bq1, L0_attn_Wq2, L0_attn_bq2, L0_attn_Wk1, L0_attn_bk1, L0_attn_Wk2, L0_attn_bk2, L0_attn_Wv, L0_attn_bv, L0_attn_Wo)
    x = x + _L0_xattn_ref(_layernorm(x, axis=-1), ctx_512, ctx_512, L0_xattn_Wq, L0_xattn_bq, L0_xattn_Wk, L0_xattn_bk, L0_xattn_Wv, L0_xattn_bv)
    x = x + _L0_ffn_ref(_layernorm(x, axis=-1), L0_ffn_w_gate, L0_ffn_w_up, L0_ffn_w_down)
    x = x + _L1_attn_ref(_layernorm(x, axis=-1), L1_attn_Wq, L1_attn_bq, L1_attn_Wk, L1_attn_bk, L1_attn_Wv, L1_attn_bv, L1_attn_Wo, L1_attn_bo)
    x = x + _L1_xattn_ref(_layernorm(x, axis=-1), ctx_512, ctx_512, L1_xattn_Wq, L1_xattn_bq, L1_xattn_Wk, L1_xattn_bk, L1_xattn_Wv, L1_xattn_bv, L1_xattn_Wo, L1_xattn_bo)
    x = x + _L1_ffn_ref(_layernorm(x, axis=-1), L1_ffn_gate_w, L1_ffn_dyn_gate_w, L1_ffn_dyn_up_w, L1_ffn_dyn_down_w, L1_ffn_sh_gate_w, L1_ffn_sh_up_w, L1_ffn_sh_down_w)
    x = x + _L2_attn_ref(_layernorm(x, axis=-1), L2_attn_Wq, L2_attn_Wk, L2_attn_Wv, L2_attn_Wo)
    x = x + _L2_xattn_ref(_layernorm(x, axis=-1), ctx_512, L2_xattn_ln1_g, L2_xattn_ln1_b, L2_xattn_ln2_g, L2_xattn_ln2_b, L2_xattn_a1_wq, L2_xattn_a1_wk, L2_xattn_a1_wv, L2_xattn_a1_li1_w, L2_xattn_a1_li1_b, L2_xattn_a1_lnx_g, L2_xattn_a1_lnx_b, L2_xattn_a1_lny_g, L2_xattn_a1_lny_b, L2_xattn_a1_ln3_g, L2_xattn_a1_ln3_b, L2_xattn_a1_li2_w, L2_xattn_a1_li2_b, L2_xattn_a1_li3_w, L2_xattn_a1_li3_b, L2_xattn_a2_wq, L2_xattn_a2_wk, L2_xattn_a2_wv, L2_xattn_a2_li1_w, L2_xattn_a2_li1_b, L2_xattn_a2_lnx_g, L2_xattn_a2_lnx_b, L2_xattn_a2_lny_g, L2_xattn_a2_lny_b, L2_xattn_a2_ln3_g, L2_xattn_a2_ln3_b, L2_xattn_a2_li2_w, L2_xattn_a2_li2_b, L2_xattn_a2_li3_w, L2_xattn_a2_li3_b, 0)
    x = x + _L2_ffn_ref(_layernorm(x, axis=-1), L2_ffn_w1_w, L2_ffn_w1_s, L2_ffn_w2_w, L2_ffn_w2_s, L2_ffn_h1_w, L2_ffn_h1_s, L2_ffn_h2_w, L2_ffn_h2_s, L2_ffn_w3_w, L2_ffn_w3_s)
    x = x + _L3_attn_ref(_layernorm(x, axis=-1), L3_attn_Wp, L3_attn_bp, L3_attn_Wv, L3_attn_Wo)
    x = x + _L3_xattn_ref(_layernorm(x, axis=-1), ctx_512, L3_xattn_Wq, L3_xattn_Wkv, L3_xattn_Wo)
    x = x + _L3_ffn_ref(_layernorm(x, axis=-1), L3_ffn_gate_w, L3_ffn_up_w, L3_ffn_down_w, L3_ffn_s_in, L3_ffn_s_in_down)
    return x

_drawn_inputs = setup_inputs


def setup_inputs(seed=0):
    import zlib

    import numpy as np

    out = dict(_drawn_inputs(seed))
    spreads = {'L0_xattn_bq': (0.0, 0.1),
     'L0_xattn_bk': (0.0, 0.1),
     'L0_xattn_bv': (0.0, 0.1),
     'L1_xattn_bq': (0.0, 0.1),
     'L1_xattn_bk': (0.0, 0.1),
     'L1_xattn_bv': (0.0, 0.1),
     'L1_xattn_bo': (0.0, 0.1),
     'L2_xattn_ln1_g': (1.0, 0.2),
     'L2_xattn_ln1_b': (0.0, 0.1),
     'L2_xattn_ln2_g': (1.0, 0.2),
     'L2_xattn_ln2_b': (0.0, 0.1),
     'L2_xattn_a1_li1_b': (0.0, 0.1),
     'L2_xattn_a1_lnx_g': (1.0, 0.2),
     'L2_xattn_a1_lnx_b': (0.0, 0.1),
     'L2_xattn_a1_lny_g': (1.0, 0.2),
     'L2_xattn_a1_lny_b': (0.0, 0.1),
     'L2_xattn_a1_ln3_g': (1.0, 0.2),
     'L2_xattn_a1_ln3_b': (0.0, 0.1),
     'L2_xattn_a1_li2_b': (0.0, 0.1),
     'L2_xattn_a1_li3_b': (0.0, 0.1),
     'L2_xattn_a2_li1_b': (0.0, 0.1),
     'L2_xattn_a2_lnx_g': (1.0, 0.2),
     'L2_xattn_a2_lnx_b': (0.0, 0.1),
     'L2_xattn_a2_lny_g': (1.0, 0.2),
     'L2_xattn_a2_lny_b': (0.0, 0.1),
     'L2_xattn_a2_ln3_g': (1.0, 0.2),
     'L2_xattn_a2_ln3_b': (0.0, 0.1),
     'L2_xattn_a2_li2_b': (0.0, 0.1),
     'L2_xattn_a2_li3_b': (0.0, 0.1),
     'L3_attn_bp': (0.0, 0.1)}
    factors = {}
    for name, (base, spread) in spreads.items():
        noise = np.random.default_rng([zlib.crc32(name.encode()), seed]).standard_normal(out[name].shape)
        drawn = base * np.exp(spread * noise) if base else spread * noise
        out[name] = jnp.asarray(drawn.astype(out[name].dtype))
    for name, factor in factors.items():
        out[name] = (out[name] * factor).astype(out[name].dtype)
    return out
```

```python
import numpy as np
import concourse.bass as bass
import concourse.mybir as mybir
from concourse.alu_op_type import AluOpType as ALU

F32 = mybir.dt.float32
BF16 = mybir.dt.bfloat16
I32 = mybir.dt.int32
ACT = mybir.ActivationFunctionType
AX = mybir.AxisListType.X

P = 128
B, S, D = 8, 112, 256
T = B * S
KD = D // P
CK, CD = 375, 128
CC = 3
CR = CK // CC
HALF = B // 2
HT = HALF * S
EPS = 1e-5
MASKED = -1e30


class Lane:

    def __init__(self, prog, name, engine, step=1):
        self.prog, self.name, self.engine, self.step = prog, name, engine, step
        self.sem = prog.stack.enter_context(prog.nc.semaphore(name))
        self.n = 0
        self.base = 0
        self.seen = {}
        prog.lanes.append(self)

    def do(self, ins):
        self.n += self.step
        return ins.then_inc(self.sem, self.step)

    def mark(self):
        return (self, self.n, self.prog.turn)

    def after(self, *points):
        for pt in points:
            lane, k, turn = pt.mark() if isinstance(pt, Lane) else pt
            if self.seen.get((lane.name, turn), -1) >= k:
                continue
            self.seen[(lane.name, turn)] = k
            if turn is None or turn is not self.prog.turn:
                if k:
                    self.engine.wait_ge(lane.sem, k)
            else:
                per = self.prog.per_turn.get((turn.name, lane.name), 0)
                if per:
                    self.engine.wait_ge(lane.sem, turn.i * per + (lane.base + k))
                elif lane.base + k:
                    self.engine.wait_ge(lane.sem, lane.base + k)


class Turn:
    def __init__(self, name, i, times):
        self.name, self.i, self.times = name, i, times


class Prog:

    def __init__(self, nc, stack, per_turn):
        self.nc, self.stack, self.per_turn = nc, stack, per_turn
        self.lanes, self.turn, self.counted = [], None, {}

    def loop(self, name, times, body):
        for lane in self.lanes:
            lane.base, lane.n, lane.seen = lane.n, 0, {}
        with self.nc.Fori(0, times) as i:
            self.turn = Turn(name, i, times)
            body(i)
        for lane in self.lanes:
            self.counted[(name, lane.name)] = lane.n
            lane.n, lane.base, lane.seen = lane.base + times * lane.n, 0, {}
        self.turn = None


class Region:

    def __init__(self, mem, start, words):
        self.mem, self.start, self.at, self.end = mem, start, start, start + words

    def take(self, *dims, dt=F32, parts=P):
        n = int(np.prod(dims))
        words = n if dt in (F32, I32) else (n + 1) // 2
        a = self.mem[0:parts, self.at:self.at + words]
        self.at += words
        assert self.at <= self.end, (self.at, self.end)
        if dt is not F32:
            a = a.bitcast(dt)
        names = "abcde"[:len(dims)]
        if len(dims) > 1:
            a = a.rearrange(f"p ({' '.join(names)}) -> p {' '.join(names)}",
                            **{c: d for c, d in zip(names, dims)})
        return a

    def rest(self):
        return Region(self.mem, self.at, self.end - self.at)


class Decoder:

    def __init__(self, nc, stack, ins, layouts, out, per_turn):
        self.nc, self.ins, self.layouts, self.out = nc, ins, layouts, out
        self.prog = Prog(nc, stack, per_turn)
        lane = lambda name, engine, step=1: Lane(self.prog, name, engine, step)
        self.PE = lane("pe_done", nc.tensor)
        self.ACT = lane("act_done", nc.scalar)
        self.DVE = lane("dve_done", nc.vector)
        self.POOL = lane("pool_done", nc.gpsimd)
        self.SP = lane("sp_done", nc.sync)
        self.CTX = lane("ctx_landed", nc.sync, 16)
        self.compute = (self.PE, self.ACT, self.DVE, self.POOL)
        self.landed = {}

        words = 53100
        mem = stack.enter_context(nc.sbuf_tensor("memory", [P, words], F32))
        self.mem = mem
        ps = stack.enter_context(nc.psum_tensor("banks", [P, 8, 512], F32))
        self.bank = lambda n, parts=P, cols=512: ps[0:parts, n, 0:cols]
        self.banks = ps
        whole = Region(mem, 0, words)
        self.x = whole.take(B, D, parts=S)
        self.xnT = whole.take(KD, B, S)
        self.small = Region(mem, whole.at, 800)
        whole.at += 800
        self.biases = Region(mem, whole.at, 2700)
        whole.at += 2700
        self.A = Region(mem, whole.at, 22528)
        whole.at += 22528
        self.Bm = Region(mem, whole.at, 15360)
        whole.at += 15360
        self.work = whole.rest()
        self.a_start, self.packs = self.A.start, {}
        self.stats = self.small.take(16, parts=S)
        self.minus_half = self.small.take(1)

    def load(self, pack, region, after=()):
        self.SP.after(*after)
        lane = Lane(self.prog, f"{pack}_landed", self.nc.sync, 16)
        self.landed[pack] = lane
        first, arrays = region.at, {}
        dt = self.ins[pack].dtype
        for name, shape in self.layouts[pack]:
            arrays[name] = region.take(*shape, dt=dt)
        dst = self.mem[:, first:region.at]
        lane.do(self.nc.sync.dma_start(dst if dt is F32 else dst.bitcast(dt), self.ins[pack]))
        return arrays

    def need(self, pack, *lanes):
        for lane in lanes:
            lane.after(self.landed[pack])

    def mm(self, out, lhsT, rhs, start=True, stop=True, count=False):
        ins = self.nc.tensor.matmul(out, lhsT, rhs, start=start, stop=stop)
        if count:
            self.PE.do(ins)

    def project(self, out, weights, acts, count=True):
        n = len(weights)
        for k in range(n):
            self.mm(out, weights[k], acts[k], k == 0, k == n - 1, count and k == n - 1)

    def tp(self, out, in_, count=True):
        n = in_.shape[0]
        ins = self.nc.tensor.transpose(out, in_, self.ident[0:n, 0:n])
        if count:
            self.PE.do(ins)

    def tt(self, out, a, b, op, lane=None):
        lane = lane or self.DVE
        lane.do(lane.engine.tensor_tensor(out, a, b, op))

    def ts(self, out, a, s1, s2, op0, op1=None, lane=None):
        lane = lane or self.DVE
        lane.do(lane.engine.tensor_scalar(out, a, s1, s2, op0, op1) if op1 is not None
                else lane.engine.tensor_scalar(out, a, s1, None, op0))

    def stt(self, out, a, s, b, op0, op1):
        self.DVE.do(self.nc.vector.scalar_tensor_tensor(out=out, in0=a, scalar=s, in1=b, op0=op0, op1=op1))

    def act(self, out, in_, func, **kw):
        self.ACT.do(self.nc.scalar.activation(out, in_, func, **kw))

    def copy(self, out, in_, lane):
        lane.do(lane.engine.copy(out, in_) if lane is self.ACT else lane.engine.tensor_copy(out, in_))

    def norm(self, src, dst):
        DVE, POOL, st = self.DVE, self.POOL, self.stats
        DVE.do(self.nc.vector.bn_stats(st[:, 0:6], src))
        DVE.after(DVE)
        DVE.do(self.nc.vector.memset(st[:, 10:11], 0.0))
        DVE.do(self.nc.vector.bn_aggr(st[:, 6:8], st[:, 0:6]))
        DVE.after(DVE)
        self.ts(st[:, 8:9], st[:, 7:8], EPS, None, ALU.add)
        POOL.after(DVE)
        self.tt(st[:, 9:10], st[:, 8:9], self.minus_half[0:S, :], ALU.pow, POOL)
        DVE.after(POOL)
        self.ts(dst, src, st[:, 6:7], st[:, 9:10], ALU.subtract, ALU.mult)

    def turn_features(self, src, dst, bank, gain=None, shift=None):
        PE, DVE = self.PE, self.DVE
        PE.after(DVE)
        pt = self.bank(bank, P, KD * S).rearrange("p (k s) -> p k s", k=KD)
        for k in range(KD):
            self.tp(pt[:, k, :], src[:, k * P:(k + 1) * P], k == KD - 1)
        DVE.after(PE)
        if gain is None:
            self.copy(dst, pt, DVE)
        else:
            for k in range(KD):
                self.ts(dst[:, k, :], pt[:, k, :], gain[:, k:k + 1], shift[:, k:k + 1], ALU.mult, ALU.add)

    def attention(self, H, nk, hd, score, value, o, *, P_sb, PT_sb, mask=None, keepT=None, fill=None,
                  o_banks=(7,), share=1.0, plus=None, vals=None):
        PE, A, V, nc = self.PE, self.ACT, self.DVE, self.nc
        G = min(4, H)
        wide = nk > S
        chunks = [(c * CR, CR) for c in range(CC)] if wide else [(0, nk)]
        per_bank = 512 // hd
        spread = hd < 64 and vals is not None
        nmax, total = self.nmax, self.total
        sread, tread = [(PE.mark()[0], 0, None)] * 2, {}

        def s_bank(g):
            return self.banks[0:S, 0:G, 0:nk]

        def scores(g):
            for h in range(G):
                pairs = score(G * g + h)
                self.project(s_bank(g)[:, h, :], [q for q, _ in pairs], [k for _, k in pairs], h == G - 1)

        def weights(g):
            src = s_bank(g)
            if fill is not None:
                V.after(PE)
                fill(g, P_sb)
                src = P_sb
            elif mask is not None:
                V.after(PE)
                self.tt(P_sb, src, mask[0:S, :].unsqueeze(1).broadcast_to([S, G, nk]), ALU.add)
                src = P_sb
            V.after(PE, V, A)
            V.do(nc.vector.tensor_reduce(nmax[:, G * g:G * g + G], src, AX, ALU.max, negate=True))
            A.after(V, PE)
            for h in range(G):
                n = G * g + h
                self.act(P_sb[:, h, :], src[:, h, :], ACT.Exp, bias=nmax[:, n:n + 1], scale=1.0,
                         accum_out=total[:, n:n + 1])

        def turn(g):
            PE.after(A, V)
            for c, (at, rows) in enumerate(chunks):
                bank = 4 + c if wide else 4 + g % 2
                pt = self.bank(bank, rows, G * S)
                for h in range(G):
                    self.tp(pt[:, h * S:(h + 1) * S], P_sb[:, h, at:at + rows], h == G - 1)
                lane = A if c % 2 else V
                lane.after(PE)
                if keepT is not None:
                    self.tt(PT_sb[0:rows, c, :].rearrange("p (h s) -> p h s", h=G),
                            pt.rearrange("p (h s) -> p h s", h=G),
                            keepT[0:rows, :].unsqueeze(1).broadcast_to([rows, G, S]), ALU.mult)
                else:
                    self.copy(PT_sb[0:rows, c, :], pt, lane)

        def values(g):
            PE.after(V, A)
            for h in range(G):
                n = G * g + h
                if spread:
                    out = self.bank(7, S)[:, h * G * hd:(h + 1) * G * hd]
                    vs = [vals[0:r, c, G * g * hd:G * (g + 1) * hd] for c, (_, r) in enumerate(chunks)]
                else:
                    out = self.bank(o_banks[n // per_bank], S)[:, (n % per_bank) * hd:(n % per_bank + 1) * hd]
                    vs = [value(n, c) for c in range(len(chunks))]
                self.project(out, [PT_sb[0:r, c, h * S:(h + 1) * S] for c, (_, r) in enumerate(chunks)],
                             vs, h == G - 1)
            if spread:
                V.after(PE)
                step = G * hd + hd
                own = self.bank(7, S, 512).rearrange("p (h x) -> p h x", x=hd)
                own = own[:, 0:G * (G + 1):G + 1, :] if G * (G + 1) <= 512 // hd else None
                if own is not None:
                    self.copy(o[:, G * g * hd:G * (g + 1) * hd].rearrange("p (h d) -> p h d", h=G), own, V)
                else:
                    blk = self.bank(7, S, 512)
                    for h in range(G):
                        self.copy(o[:, (G * g + h) * hd:(G * g + h + 1) * hd],
                                  blk[:, h * G * hd + h * hd:h * G * hd + (h + 1) * hd], V)

        groups = H // G
        PE.after(A, V, self.POOL)
        if fill is None:
            scores(0)
        weights(0)
        for g in range(groups):
            if g + 1 < groups and fill is None:
                PE.after(A, V)
                scores(g + 1)
            turn(g)
            if g + 1 < groups:
                weights(g + 1)
            values(g)
        V.after(A)
        V.do(nc.vector.reciprocal(self.inv[:, 0:H], total[:, 0:H]))
        if share != 1.0:
            V.after(V)
            self.ts(self.inv[:, 0:H], self.inv[:, 0:H], share, None, ALU.mult)
        V.after(V, PE)
        each = min(per_bank, H)
        for n in range(0, 0 if spread else H, each):
            ob = self.bank(o_banks[n // per_bank], S, each * hd).rearrange("p (h d) -> p h d", h=each)
            self.tt(o[:, n * hd:(n + each) * hd].rearrange("p (h d) -> p h d", h=each), ob,
                    self.inv[:, n:n + each].unsqueeze(2).broadcast_to([S, each, hd]), ALU.mult)
        if spread:
            ov = o.rearrange("p (h d) -> p h d", h=H)
            self.tt(ov, ov, self.inv[:, 0:H].unsqueeze(2).broadcast_to([S, H, hd]), ALU.mult)
        if plus is not None:
            V.after(V)
            self.tt(o, o, plus, ALU.add)

    def out_project(self, o, oT, w, bank_t, bank_o):
        tiles = w.shape[1]
        PE, V = self.PE, self.DVE
        PE.after(V, self.ACT)
        for t0 in range(0, tiles, 4):
            n = min(4, tiles - t0)
            pt = self.bank(bank_t + t0 // 4, P, n * S)
            for t in range(n):
                self.tp(pt[:, t * S:(t + 1) * S], o[:, (t0 + t) * P:(t0 + t + 1) * P], t == n - 1)
            V.after(PE)
            self.copy(oT[:, t0:t0 + n, :], pt.rearrange("p (t s) -> p t s", t=n), V)
        PE.after(V)
        y = self.bank(bank_o, S, D)
        self.project(y, [oT[:, t, :] for t in range(tiles)], [w[:, t, :] for t in range(tiles)])
        return y

    def start(self):
        SP, nc = self.SP, self.nc
        self.load_x = Lane(self.prog, "x_landed", nc.sync, 16)
        self.load_x.do(nc.sync.dma_start(self.x, self.ins["x"]))
        c = self.load("consts", self.small)
        self.ident, self.causal, self.upperT, self.spread = c["ident"], c["causal"], c["upperT"], c["spread"]
        self.rows16, self.rows32, self.prefix = c["rows16"], c["rows32"], c["prefix"]
        self.ones, self.turn8 = c["ones"], c["turn8"]
        self.nmax = self.small.take(16, parts=S)
        self.total = self.small.take(16, parts=S)
        self.inv = self.small.take(16, parts=S)
        self.POOL.do(nc.gpsimd.memset(self.minus_half, -0.5))
        for lane in self.compute:
            lane.after(self.load_x, self.landed["consts"], self.POOL)
        self.tp(self.bank(0, P, P), self.ident)
        self.copy(self.nmax, self.ident[0:S, 0:16], self.ACT)
        self.copy(self.total, self.ident[0:S, 0:16], self.DVE)

    def l0_attn(self):
        nc, PE, A, V, G = self.nc, self.PE, self.ACT, self.DVE, self.POOL
        GT = 8
        w = self.load("l0a", self.A)
        whh = self.A.take(3, 2, KD, GT * P, dt=BF16)
        raw = self.load("l0a_whh", self.A)["whh"]
        bias = self.load("l0a_bias", self.biases)
        x, xnT = self.x, self.xnT
        xW = Region(self.mem, self.Bm.start, 15360).take(2, S, GT, B)
        wk = self.work.rest()
        hs = wk.take(2, KD, B, S)
        xn = wk.take(D, parts=S)

        def norm_batch(b):
            self.norm(x[:, b, :], xn)
            V.after(V)
            self.turn_features(xn, xnT[:, :, b, :], 0)
        self.prog.loop("l0_norm", B, norm_batch)

        self.need("l0a_whh", V, A, G)
        for l in range(2):
            self.copy(whh[:, 0, l], raw[:, l], A)
            G.after(A)
            self.tt(raw[:, l], raw[:, l], whh[:, 0, l], ALU.subtract, G)
            A.after(G)
            self.copy(whh[:, 1, l], raw[:, l], A)
            G.after(A, G)
            self.tt(whh[:, 2, l], raw[:, l], whh[:, 1, l], ALU.subtract, G)
        self.need("l0a", PE, V)
        self.need("l0a_bias", PE, A, V)

        PE.after(V)
        def input_gates(half):
            free = [None] * 4
            for n in range(2 * GT):
                l, g = divmod(n, GT)
                ps = self.bank(n % 4, P, HT)
                if free[n % 4]:
                    PE.after(free[n % 4])
                else:
                    PE.after(A, V)
                self.project(ps, [w["wih"][:, l, k, g * P:(g + 1) * P] for k in range(KD)],
                             [xnT[:, k, bass.ds(half * HALF, HALF), :] for k in range(KD)])
                dst = xW[:, l, :, g, bass.ds(half * HALF, HALF)].rearrange("p t b -> p b t")
                src = ps.rearrange("p (b t) -> p b t", b=HALF)
                lane = A if n % 2 else V
                lane.after(PE)
                if lane is A:
                    self.act(dst, src, ACT.Identity, bias=bias["b_lstm"][:, n:n + 1], scale=1.0)
                else:
                    self.ts(dst, src, bias["b_lstm"][:, n:n + 1], None, ALU.add)
                free[n % 4] = lane.mark()
        self.prog.loop("l0_input", 2, input_gates)

        gates = wk.take(2, GT, B)
        cell = wk.take(2, KD, B)
        prod = wk.take(2, 2, KD, B)
        tc = wk.take(2, KD, B)
        h = wk.take(2, KD, B)
        left = wk.take(2, KD, B)
        hp = wk.take(2, 2, 3, KD, B, dt=BF16)
        V.do(nc.vector.memset(cell, 0.0))
        V.do(nc.vector.memset(hp, 0.0))
        UN = 8
        V.after(A, V, G)
        PE.after(A, V, G)
        G.after(V)

        def steps(i):
            hmark = [V.mark(), V.mark()]
            pmark = [G.mark(), G.mark()]
            for u in range(UN):
                t = i * UN + u
                new, old = (u + 1) % 2, u % 2
                for l in range(2):
                    ps = self.bank(l, P, 3 * GT * B).rearrange("p (s g b) -> p s g b", s=3, g=GT)
                    PE.after(hmark[l])
                    for g in range(GT):
                        for k in range(KD):
                            for part in range(3):
                                ins = nc.tensor.matmul(
                                    ps[:, part:3, g, :], whh[:, part, l, k, g * P:(g + 1) * P],
                                    hp[:, old, l, 0:3 - part, k, :],
                                    start=(g == 0 and k == 0 and part == 0), stop=(k == KD - 1 and part == 2),
                                    skip_group_check=True)
                    PE.do(ins)
                    V.after(PE)
                    V.do(nc.vector.tensor_reduce(gates[:, l].rearrange("p g b -> p (g b)"),
                                                 ps.rearrange("p s g b -> p (g b) s"), AX, ALU.add))
                    V.after(V)
                    self.tt(gates[:, l], gates[:, l],
                            xW[:, l, bass.ds(t, 1), :, :].rearrange("p o g b -> p (o g) b"), ALU.add)
                    A.after(V)
                    self.act(gates[:, l, 0:6, :], gates[:, l, 0:6, :], ACT.Sigmoid)
                    m_sig = A.mark()
                    self.act(gates[:, l, 6:8, :], gates[:, l, 6:8, :], ACT.Tanh)
                    m_tanh = A.mark()
                    V.after(m_sig, V)
                    self.tt(prod[:, l, 0], gates[:, l, 2:4, :], cell[:, l], ALU.mult)
                    V.after(m_tanh)
                    self.tt(prod[:, l, 1], gates[:, l, 0:2, :], gates[:, l, 6:8, :], ALU.mult)
                    V.after(V)
                    self.tt(cell[:, l], prod[:, l, 0], prod[:, l, 1], ALU.add)
                    A.after(V)
                    self.act(tc[:, l], cell[:, l], ACT.Tanh)
                    V.after(A, pmark[l])
                    self.tt(hp[:, new, l, 0], gates[:, l, 4:6, :], tc[:, l], ALU.mult)
                    self.tt(h[:, l], gates[:, l, 4:6, :], tc[:, l], ALU.mult)
                    V.after(V)
                    self.tt(hp[:, new, l, 1], h[:, l], hp[:, new, l, 0], ALU.subtract)
                    self.tt(left[:, l], h[:, l], hp[:, new, l, 0], ALU.subtract)
                    V.after(V)
                    self.tt(hp[:, new, l, 2], left[:, l], hp[:, new, l, 1], ALU.subtract)
                    hmark[l] = V.mark()
                    G.after(hmark[l])
                    self.copy(hs[:, l, :, :, bass.ds(t, 1)].rearrange("p k b o -> p k (b o)"), h[:, l], G)
                    pmark[l] = G.mark()
        self.prog.loop("l0_lstm", S // UN, steps)
        self.fetch_l0_l1()

        wk2 = Region(self.mem, self.Bm.start, 15360)
        xb = wk2.take(KD, S)
        r1 = wk2.take(2, S, parts=64)
        qT = wk2.take(8, S)
        kT = wk2.take(4, S)
        v = wk2.take(D, parts=S)
        o = wk2.take(4 * D, parts=S)
        oT = wk2.take(8, S)
        P_sb = wk2.take(4, S, parts=S)
        PT_sb = wk2.take(1, 4 * S)
        bq2s = wk2.take(8)
        V.after(PE, A, G, V)
        self.ts(bq2s, bias["bq2"], 0.125, None, ALU.mult)
        for lane in self.compute:
            lane.after(*self.compute)

        def batch(b):
            G.after(PE)
            self.copy(xb, xnT[:, :, b, :], G)
            for l, (w1, b1) in enumerate((("wq1", "bq1"), ("wk1", "bk1"))):
                PE.after(V)
                ps = self.bank(2 + l, 64, S)
                self.project(ps, [w[w1][:, k, :] for k in range(KD)],
                             [hs[:, l, k, b, :] for k in range(KD)])
                V.after(PE)
                self.ts(r1[:, l, :], ps, bias[b1][0:64, :], 0.0, ALU.add, ALU.max)
            PE.after(V, A)
            for part in range(2):
                ps = self.bank(part, P, 4 * S).rearrange("p (t s) -> p t s", t=4)
                for t in range(4):
                    c = 4 * part + t
                    self.mm(ps[:, t, :], w["wq2"][0:64, c * P:(c + 1) * P], r1[:, 0, :], count=t == 3)
                V.after(PE)
                self.stt(qT[:, 4 * part:4 * part + 4, :], ps, 0.125,
                         bq2s[:, 4 * part:4 * part + 4].unsqueeze(2).broadcast_to([P, 4, S]), ALU.mult, ALU.add)
            ps = self.bank(4, P, 4 * S).rearrange("p (t s) -> p t s", t=4)
            for t in range(4):
                self.mm(ps[:, t, :], w["wk2"][0:64, t * P:(t + 1) * P], r1[:, 1, :], count=t == 3)
            V.after(PE)
            self.tt(kT, ps, bias["bk2"].unsqueeze(2).broadcast_to([P, 4, S]), ALU.add)
            PE.after(G)
            self.project(self.bank(5, S, D), [xb[:, k, :] for k in range(KD)], [w["wv"][:, k, :] for k in range(KD)])
            V.after(PE)
            self.tt(v, self.bank(5, S, D), bias["bv"][0:S, :], ALU.add)
            self.attention(16, S, 64,
                           lambda n: [(qT[64 * (n % 2):64 * (n % 2) + 64, n // 2, :],
                                       kT[64 * (n % 2):64 * (n % 2) + 64, n // 4, :])],
                           lambda n, c: v[:, 64 * (n // 4):64 * (n // 4) + 64],
                           o, P_sb=P_sb, PT_sb=PT_sb, mask=self.causal, o_banks=(6, 7))
            y = self.out_project(o, oT, w["wo"], 0, 2)
            V.after(PE)
            self.tt(x[:, b, :], x[:, b, :], y, ALU.add)
        self.prog.loop("l0_attn", B, batch)
        self.fetch_l1_l2()

    def fetch_l0_l1(self):
        upper = Region(self.mem, self.Bm.start + 5000, 15360 - 5000)
        for pack in ("l0x", "l0f", "l1a"):
            self.packs[pack] = self.load(pack, upper, self.compute)

    def fetch_l1_l2(self):
        a = Region(self.mem, self.a_start, 22528)
        for pack in ("l1x", "l1f", "l2a"):
            self.packs[pack] = self.load(pack, a, self.compute)
        self.extra = a.rest()
        self.extra_b = Region(self.mem, self.Bm.start, 5000)

    def settle(self):
        for lane in self.compute:
            lane.after(*self.compute, self.CTX)

    def buffers(self, *regions):
        regions = [r.rest() for r in regions]

        def take(*dims, dt=F32, parts=P):
            n = int(np.prod(dims))
            n = n if dt is not BF16 else (n + 1) // 2
            for r in regions:
                if r.at + n <= r.end:
                    return r.take(*dims, dt=dt, parts=parts)
            raise AssertionError(("no room for", dims))
        return take

    def load_context(self, i, dst, which="ctxT"):
        self.SP.after(self.PE, self.DVE)
        src = self.ins[which][i] if isinstance(i, int) else \
            self.ins[which][bass.ds(i, 1)].rearrange("o p n -> (o p) n")
        self.CTX.do(self.nc.sync.dma_start(dst, src))

    def queries(self, q, qm, src, w, bias, scale, rows, bank=0):
        PE, V, G = self.PE, self.DVE, self.POOL
        tiles = w.shape[2] // P
        ps = self.bank(bank, P, tiles * S).rearrange("p (t s) -> p t s", t=tiles)
        for t in range(tiles):
            self.project(ps[:, t, :], [w[:, k, t * P:(t + 1) * P] for k in range(KD)],
                         [src[:, k, :] for k in range(KD)], t == tiles - 1)
        V.after(PE, G)
        if bias is None:
            self.ts(q, ps, scale, None, ALU.mult)
        else:
            self.stt(q, ps, scale, bias.unsqueeze(2).broadcast_to([P, tiles, S]), ALU.mult, ALU.add)
        if qm is None:
            return
        per = rows.shape[1]
        V.after(V)
        G.after(V, PE)
        for t in range(tiles):
            self.tt(qm[:, t * per:(t + 1) * per, :], q[:, t, :].unsqueeze(1).broadcast_to([P, per, S]),
                    rows.unsqueeze(2).broadcast_to([P, per, S]), ALU.mult, V if t % 2 else G)

    def keys(self, kT, src, w, bias, bank):
        PE, A = self.PE, self.ACT
        nk = kT.shape[2]
        for t in range(kT.shape[1]):
            ps = self.bank(bank + t, P, nk)
            self.project(ps, [w[:, k, t * P:(t + 1) * P] for k in range(len(src))], src)
            A.after(PE)
            if bias is None:
                self.copy(kT[:, t, :], ps, A)
            else:
                self.act(kT[:, t, :], ps, ACT.Identity, bias=bias[:, t:t + 1], scale=1.0)

    def values_of(self, v, src, w, bias, bank, chunks):
        PE, V = self.PE, self.DVE
        F = w.shape[2]
        for c, (at, rows) in enumerate(chunks):
            ps = self.bank(bank + c, rows, F)
            self.project(ps, [s[:, at:at + rows] for s in src], [w[:, k, :] for k in range(len(src))])
            V.after(PE)
            if bias is None:
                self.copy(v[0:rows, c, :], ps, V)
            else:
                self.tt(v[0:rows, c, :], ps, bias[0:rows, :], ALU.add)

    CHUNKS = [(c * CR, CR) for c in range(CC)]

    def l0_xattn(self):
        PE, A, V, G = self.PE, self.ACT, self.DVE, self.POOL
        self.settle()
        w, x = self.packs["l0x"], self.x
        take = self.buffers(self.work, self.extra, self.extra_b)
        xn, xT = take(D, parts=S), take(KD, S)
        q, kT, v = take(KD, S), take(KD, CK), take(CC, D)
        ctx, P_sb, PT_sb, o = take(CK), take(1, CK, parts=S), take(CC, S), take(D, parts=S)
        self.load_context(0, ctx)
        self.need("l0x", PE, V, A)

        def batch(b):
            for e in (PE, A, V):
                e.after(self.CTX)
            self.norm(x[:, b, :], xn)
            self.keys(kT, [ctx], w["wk"], w["bk"], 4)
            self.values_of(v, [ctx], w["wv"], w["bv"], 1, self.CHUNKS)
            self.load_context(b + 1, ctx)
            V.after(V)
            self.turn_features(xn, xT, 0)
            PE.after(V)
            self.queries(q, None, xT, w["wq"], w["bq"], 1.0, None, bank=7)
            self.attention(1, CK, D, lambda n: [(q[:, k, :], kT[:, k, :]) for k in range(KD)],
                           lambda n, c: v[0:CR, c, :], o, P_sb=P_sb, PT_sb=PT_sb)
            V.after(V)
            self.tt(x[:, b, :], x[:, b, :], o, ALU.add)
        self.prog.loop("l0_xattn", B, batch)

    def cross(self, name, pack, hd, scale, rows):
        PE, A, V, G = self.PE, self.ACT, self.DVE, self.POOL
        self.settle()
        w, x = self.packs[pack], self.x
        H = D // hd
        take = self.buffers(self.work, self.extra, self.extra_b)
        xn, xT = take(D, parts=S), take(KD, S)
        q, qm, kT, v = take(KD, S), take(H, S), take(KD, CK), take(CC, D)
        ctx, P_sb, PT_sb, o = take(CK), take(4, CK, parts=S), take(CC, 4 * S), take(D, parts=S)
        oT = take(KD, S)
        self.load_context(0, ctx)
        self.need(pack, PE, V, A)
        per = P // hd
        bq = w.get("bq")
        if bq is not None:
            bqs = take(KD)
            self.ts(bqs, bq, scale, None, ALU.mult)
            bq = bqs

        def batch(b):
            for e in (PE, A, V):
                e.after(self.CTX)
            self.norm(x[:, b, :], xn)
            self.keys(kT, [ctx], w["wk"], w.get("bk"), 4)
            self.values_of(v, [ctx], w["wv"], w.get("bv"), 1, self.CHUNKS)
            self.load_context(b + 1, ctx)
            V.after(V)
            self.turn_features(xn, xT, 0)
            PE.after(V)
            self.queries(q, qm, xT, w["wq"], bq, scale, rows, bank=7)
            self.narrow_attention(H, CK, hd, qm, kT, v, o, P_sb, PT_sb)
            y = self.out_project(o, oT, w["wo"], 4, 0)
            V.after(PE)
            if "bo" in w:
                self.tt(xn, y, w["bo"][0:S, :], ALU.add)
                V.after(V)
                y = xn
            self.tt(x[:, b, :], x[:, b, :], y, ALU.add)
        self.prog.loop(name, B, batch)

    def narrow_attention(self, H, nk, hd, qm, kT, v, o, P_sb, PT_sb, **more):
        per = P // hd
        self.attention(H, nk, hd, lambda n: [(qm[:, n, :], kT[:, n // per, :])],
                       lambda n, c: v[0:(CR if nk > S else S), c, hd * n:hd * n + hd],
                       o, P_sb=P_sb, PT_sb=PT_sb, vals=v, **more)

    def l1_attn(self):
        PE, A, V, G = self.PE, self.ACT, self.DVE, self.POOL
        self.settle()
        w, x, H, hd = self.packs["l1a"], self.x, 16, 16
        take = self.buffers(self.work, self.extra, self.extra_b)
        xn, xT = take(D, parts=S), take(KD, S)
        q, qm, kT, v = take(KD, S), take(H, S), take(KD, S), take(1, D, parts=S)
        P_sb, PT_sb, o, oT = take(4, S, parts=S), take(1, 4 * S), take(D, parts=S), take(KD, S)
        near, bqs = take(D, parts=S), take(KD)
        self.need("l1a", PE, V, A)
        self.ts(bqs, w["bq"], 0.25, None, ALU.mult)

        def batch(b):
            PE.after(V, A)
            self.norm(x[:, b, :], xn)
            V.after(V)
            self.turn_features(xn, xT, 0)
            PE.after(V)
            src = [xT[:, k, :] for k in range(KD)]
            self.keys(kT, src, w["wk"], w["bk"], 4)
            self.values_of(v, src, w["wv"], w["bv"], 2, [(0, S)])
            self.queries(q, qm, xT, w["wq"], bqs, 0.25, self.rows16, bank=1)
            PE.after(V)
            self.mm(self.bank(3, S, D), self.spread[0:S, :], v[:, 0, :], count=True)
            V.after(PE)
            self.copy(near, self.bank(3, S, D), V)
            self.narrow_attention(H, S, hd, qm, kT, v, o, P_sb, PT_sb, share=0.6, plus=near)
            y = self.out_project(o, oT, w["wo"], 4, 0)
            V.after(PE)
            self.tt(xn, y, w["bo"][0:S, :], ALU.add)
            V.after(V)
            self.tt(x[:, b, :], x[:, b, :], xn, ALU.add)
        self.prog.loop("l1_attn", B, batch)

    def l1_xattn(self):
        self.cross("l1_xattn", "l1x", 16, 0.25, self.rows16)

    def l3_xattn(self):
        self.cross("l3_xattn", "l3x", 16, 0.25, self.rows16)

    def norm_half(self, half, src, xn2, xT, gain=None, shift=None):
        V = self.DVE
        for j in range(HALF):
            self.norm(src[:, bass.ds(half * HALF + j, 1), :].rearrange("p o d -> p (o d)"), xn2)
            V.after(V)
            self.turn_features(xn2, xT[:, :, j, :], j % 2, gain, shift)

    def tile_stream(self, n, banks, fill, drain, free):
        PE = self.PE
        for u in range(n):
            bk = banks[u % len(banks)]
            if bk in free:
                PE.after(*free[bk])
            fill(u, bk)
            free[bk] = drain(u, bk)

    def gated(self, tiles, xT, wg, wu, h, g_sb, free, scales=None):
        PE, A, V = self.PE, self.ACT, self.DVE
        flat = [xT[:, k].rearrange("p b s -> p (b s)") for k in range(KD)]

        def fill(u, bk):
            for o, wt in ((0, wg), (1, wu)):
                self.project(self.bank(bk + o, P, HT), [wt[:, k, u * P:(u + 1) * P] for k in range(KD)], flat)

        def drain(u, bk):
            A.after(PE, V)
            sg = {} if scales is None else dict(scale=scales[0][:, u:u + 1])
            self.act(g_sb[:, u % 2, :], self.bank(bk, P, HT), ACT.Silu, **sg)
            V.after(A, PE)
            if scales is None:
                self.tt(h[:, u, :], g_sb[:, u % 2, :], self.bank(bk + 1, P, HT), ALU.mult)
            else:
                self.stt(h[:, u, :], self.bank(bk + 1, P, HT), scales[1][:, u:u + 1], g_sb[:, u % 2, :],
                         ALU.mult, ALU.mult)
            return (A.mark(), V.mark())
        self.tile_stream(tiles, (0, 2, 4), fill, drain, free)

    def down(self, half, h, w, free, finish):
        PE, V = self.PE, self.DVE
        PE.after(V)
        tiles = w.shape[1]

        def fill(j, bk):
            self.project(self.bank(bk, S, D), [h[:, t, j * S:(j + 1) * S] for t in range(tiles)],
                         [w[:, t, :] for t in range(tiles)])

        def drain(j, bk):
            V.after(PE)
            finish(j, bass.ds(half * HALF + j, 1), self.bank(bk, S, D))
            return (V.mark(),)
        self.tile_stream(HALF, (6, 7), fill, drain, free)

    def xs(self, a, at):
        return a[:, at, :].rearrange("p o d -> p (o d)")

    def l0_ffn(self):
        PE, A, V, G = self.PE, self.ACT, self.DVE, self.POOL
        self.settle()
        wi, x = self.packs["l0f"], self.x
        take = self.buffers(self.work, self.extra, self.extra_b)
        xn, xT = take(D, parts=S), take(KD, HALF, S)
        h, g_sb = take(6, HT), take(2, HT)
        self.need("l0f", A, V, G)
        w = {}
        for name, lane in (("wg", A), ("wu", V), ("wd", G)):
            w[name] = wi[name].bitcast(F32)
            if lane is A:
                self.act(w[name], wi[name], ACT.Copy, scale=1.0 / 127.0)
            else:
                self.ts(w[name], wi[name], 1.0 / 127.0, None, ALU.mult, lane=lane)
        PE.after(A, V, G)

        def half_turn(i):
            free = {}
            PE.after(V, A)
            self.norm_half(i, x, xn, xT)
            PE.after(V)
            self.gated(6, xT, w["wg"], w["wu"], h, g_sb, free)
            self.down(i, h, w["wd"], free,
                      lambda j, at, y: self.tt(self.xs(x, at), self.xs(x, at), y, ALU.add))
        self.prog.loop("l0_ffn", 2, half_turn)

    def l1_ffn(self):
        nc, PE, A, V, G = self.nc, self.PE, self.ACT, self.DVE, self.POOL
        self.settle()
        self.fetch_l2x()
        w, x, xnT = self.packs["l1f"], self.x, self.xnT
        E, TOP, CAP = 8, 4, 140
        take = self.buffers(self.work, self.extra)
        xn, logits = take(D, parts=S), take(B, E + 1, parts=S)
        free = {}
        self.need("l1f", PE)

        def norm_batch(b):
            PE.after(V)
            self.norm(x[:, b, :], xn)
            V.after(V)
            xb = xb_buf
            self.turn_features(xn, xb, 0)
            PE.after(V)
            self.project(self.bank(1, S, E + 1), [xb[:, k, :] for k in range(KD)],
                         [w["router"][:, k, :] for k in range(KD)])
            V.after(PE, G)
            self.copy(logits[:, b, :], self.bank(1, S, E + 1), V)
            G.after(V)
            self.copy(xnT[:, :, b, :], xb, G)
        xb_buf = take(KD, S)
        self.prog.loop("l1_router", B, norm_batch)

        e3 = lambda: take(B, E, parts=S)
        e1 = lambda: take(B, parts=S)
        wide = lambda a: a.unsqueeze(2).broadcast_to([S, B, E])
        s, rest, t1, t2, t3, pick, rw = logits[:, :, 0:E], e3(), e3(), e3(), e3(), e3(), e3()
        size, prob, cum, a1, first, total = e3(), e1(), e1(), e1(), e1(), e1()
        turn, weight = self.turn8[0:S, :].unsqueeze(1).broadcast_to([S, B, E]), take(B, E + 1, parts=S)

        def do(f, *a, **k):
            V.after(V)
            f(*a, **k)

        def red(out, a, op):
            V.after(V)
            V.do(nc.vector.tensor_reduce(out, a, AX, op))

        def exp(out, a):
            A.after(V)
            self.act(out, a, ACT.Exp)
            V.after(A)
        do(self.copy, rest, s, V)
        do(self.ts, rw, s, 0.0, None, ALU.mult)
        do(self.ts, t1, s, -1.0, None, ALU.mult)
        do(self.tt, size, s, t1, ALU.max)
        for r in range(TOP):
            red(a1, rest, ALU.max)
            if r == 0:
                do(self.copy, first, a1, V)
                do(self.tt, t1, s, wide(first), ALU.subtract)
                exp(t1, t1)
                red(total, t1, ALU.add)
                do(lambda: V.do(nc.vector.reciprocal(total, total)))
            do(self.tt, t1, rest, wide(a1), ALU.is_equal)
            do(self.tt, t1, t1, turn, ALU.mult)
            red(prob, t1, ALU.max)
            do(self.tt, pick, t1, wide(prob), ALU.is_equal)
            do(self.ts, prob, a1, -1.0, None, ALU.mult)
            do(self.tt, prob, prob, a1, ALU.max)
            do(self.tt, t1, size, wide(prob), ALU.max)
            do(self.ts, t1, t1, 0.2, None, ALU.mult)
            do(self.tt, t2, wide(a1), s, ALU.subtract)
            do(self.tt, t2, t2, t1, ALU.is_le)
            do(self.tt, t3, rest, wide(a1), ALU.subtract)
            exp(t3, t3)
            do(self.tt, t3, t3, t2, ALU.mult)
            red(prob, t3, ALU.add)
            do(lambda: V.do(nc.vector.reciprocal(prob, prob)))
            if r:
                do(self.ts, t1[:, :, 0], cum, 0.75, None, ALU.is_lt)
                do(self.tt, prob, prob, t1[:, :, 0], ALU.mult)
            do(self.tt, t1, pick, wide(prob), ALU.mult)
            do(self.tt, rw, rw, t1, ALU.add)
            if r < TOP - 1:
                do(self.ts, t1, pick, MASKED, None, ALU.mult)
                do(self.tt, rest, rest, t1, ALU.add)
                do(self.tt, a1, a1, first, ALU.subtract)
                exp(a1, a1)
                do(self.tt, a1, a1, total, ALU.mult)
                if r:
                    do(self.tt, cum, cum, a1, ALU.add)
                else:
                    do(self.copy, cum, a1, V)
        red(a1, rw, ALU.add)
        do(lambda: V.do(nc.vector.reciprocal(a1, a1)))
        do(self.tt, rw, rw, wide(a1), ALU.mult)
        do(self.ts, t1, rw, 0.0, None, ALU.is_gt)
        PE.after(V)
        flat = t1.rearrange("p b e -> p (b e)")
        self.mm(self.bank(2, S, B * E), self.prefix[0:S, :], flat)
        self.mm(self.bank(3, S, B * E), self.ones[0:S, 0:S], flat, count=True)
        V.after(PE)
        do(self.copy, t2.rearrange("p b e -> p (b e)"), self.bank(2, S, B * E), V)
        do(self.copy, t3.rearrange("p b e -> p (b e)"), self.bank(3, S, B * E), V)
        for b in range(1, B):
            do(self.tt, t2[:, b, :], t2[:, b, :], t3[:, b - 1, :], ALU.add)
            if b < B - 1:
                do(self.tt, t3[:, b, :], t3[:, b, :], t3[:, b - 1, :], ALU.add)
        do(self.ts, t2, t2, float(CAP), None, ALU.is_le)
        do(self.tt, t1, t1, t2, ALU.mult)
        do(self.ts, weight[:, :, 0:E], t1, -1.0, -MASKED, ALU.add, ALU.mult)
        do(self.tt, weight[:, :, 0:E], weight[:, :, 0:E], s, ALU.add)
        do(self.copy, weight[:, :, E:E + 1], logits[:, :, E:E + 1], V)
        red(a1, weight, ALU.max)
        w9 = lambda a: a.unsqueeze(2).broadcast_to([S, B, E + 1])
        do(self.tt, weight, weight, w9(a1), ALU.subtract)
        exp(weight, weight)
        red(a1, weight, ALU.add)
        do(lambda: V.do(nc.vector.reciprocal(a1, a1)))
        do(self.tt, weight, weight, w9(a1), ALU.mult)
        red(a1, weight[:, :, 0:E], ALU.add)
        do(self.tt, rw, rw, wide(a1), ALU.mult)
        do(self.tt, weight[:, :, 0:E], rw, t1, ALU.mult)

        h, g_sb, wt = take(4, HT), take(2, HT), take(HALF, E + 1, parts=S)
        self.settle()

        def experts(i):
            free = {}
            V.after(V)
            self.copy(wt, weight[:, bass.ds(i * HALF, HALF), :], V)
            flat = [xnT[:, k, bass.ds(i * HALF, HALF), :].rearrange("p b s -> p (b s)") for k in range(KD)]
            PE.after(V, A)

            def unit(u, bk):
                wg, wu, c = (w["dg"], w["du"], u) if u < E else (w["sg"], w["su"], u - E)
                for o, ww in ((0, wg), (1, wu)):
                    self.project(self.bank(bk + o, P, HT), [ww[:, k, c * P:(c + 1) * P] for k in range(KD)], flat)

            def activate(u, bk):
                slot = u % 4
                A.after(PE, V)
                self.act(g_sb[:, u % 2, :], self.bank(bk, P, HT), ACT.Silu)
                V.after(A, PE)
                self.tt(h[:, slot, :], g_sb[:, u % 2, :], self.bank(bk + 1, P, HT), ALU.mult)
                return (A.mark(), V.mark())

            def give(e):
                tiles = [e % 4] if e < E else [0, 1, 2, 3]
                dd = [w["dd"][:, e, :]] if e < E else [w["sd"][:, t, :] for t in range(4)]

                def fill(j, bk):
                    self.project(self.bank(bk, S, D), [h[:, t, j * S:(j + 1) * S] for t in tiles], dd)

                def drain(j, bk):
                    V.after(PE, V)
                    xb = self.xs(x, bass.ds(i * HALF + j, 1))
                    self.stt(xb, self.bank(bk, S, D), wt[:, j, e:e + 1], xb, ALU.mult, ALU.add)
                    return (V.mark(),)
                self.tile_stream(HALF, (6, 7), fill, drain, free)
            ready = {}
            for u in range(E + 4 + 1):
                if u < E + 4:
                    self.tile_stream(1, ((0, 2, 4)[u % 3],), lambda _, bk: unit(u, bk),
                                     lambda _, bk: activate(u, bk), free)
                    ready[u] = V.mark()
                if 1 <= u <= E:
                    PE.after(ready[u - 1])
                    give(u - 1)
            PE.after(V)
            give(E)
        self.prog.loop("l1_experts", 2, experts)

    def fetch_l2x(self):
        self.packs["l2x"] = self.load("l2x", Region(self.mem, self.Bm.start, 15360), self.compute)

    def l2_attn(self):
        PE, A, V, G = self.PE, self.ACT, self.DVE, self.POOL
        self.settle()
        w, x, H, KV = self.packs["l2a"], self.x, 8, 4
        take = self.buffers(self.work, self.extra)
        xn, xT = take(D, parts=S), take(KD, S)
        q, kT, v, o = take(H, S), take(KV, S), take(KV * P, parts=S), take(H * P, parts=S)
        oT, P_sb, PT_sb, tmp = take(H, S), take(4, S, parts=S), take(1, 4 * S), take(2, 4, S)
        self.need("l2a", PE)
        self.SP.after(*self.compute)
        rb = Region(self.mem, self.biases.start, 2700)
        rope = self.load("rope", rb)
        self.need("rope", V)

        def batch(b):
            PE.after(V, A)
            self.norm(x[:, b, :], xn)
            V.after(V)
            self.turn_features(xn, xT, 6)
            PE.after(V)
            for g, (wa, wb, c0, dst, cos, sin) in enumerate((
                    ("wq", "wqs", 0, q[:, 0:4], "cosq", "sinq"), ("wq", "wqs", 4, q[:, 4:8], "cosq", "sinq"),
                    ("wk", "wks", 0, kT, "cos", "sin"))):
                pa = self.bank(2 * g, P, 4 * S).rearrange("p (h s) -> p h s", h=4)
                pb = self.bank(2 * g + 1, P, 4 * S).rearrange("p (h s) -> p h s", h=4)
                for ps, ww in ((pa, w[wa]), (pb, w[wb])):
                    for h in range(4):
                        c = c0 + h
                        self.project(ps[:, h, :], [ww[:, k, c * P:(c + 1) * P] for k in range(KD)],
                                     [xT[:, k, :] for k in range(KD)], h == 3)
                V.after(PE, V)
                cs = lambda n: rope[n].unsqueeze(1).broadcast_to([P, 4, S])
                self.tt(dst, pa, cs(cos), ALU.mult)
                self.tt(tmp[:, g % 2], pb, cs(sin), ALU.mult)
                G.after(V)
                self.tt(dst, dst, tmp[:, g % 2], ALU.add, G)
                V.after(G)
            self.project(self.bank(7, S, KV * P), [xT[:, k, :] for k in range(KD)], [w["wv"][:, k, :] for k in range(KD)])
            A.after(PE)
            self.copy(v, self.bank(7, S, KV * P), A)
            self.attention(H, S, P, lambda n: [(q[:, n, :], kT[:, n // 2, :])],
                           lambda n, c: v[:, P * (n // 2):P * (n // 2) + P],
                           o, P_sb=P_sb, PT_sb=PT_sb, mask=self.causal, o_banks=(6, 7))
            y = self.out_project(o, oT, w["wo"], 0, 2)
            V.after(PE)
            self.tt(x[:, b, :], x[:, b, :], y, ALU.add)
        self.prog.loop("l2_attn", B, batch)
        self.fetch_l2f()

    def fetch_l2f(self):
        a = Region(self.mem, self.a_start, 22528)
        self.packs["l2f"] = self.load("l2f", a, self.compute)
        self.a_hi = a.rest()

    def fetch_l2f_rest(self):
        self.packs["l2f2"] = self.load("l2f2", Region(self.mem, self.a_hi.start, 8192), self.compute)

    def fetch_l3(self):
        b = Region(self.mem, self.Bm.start, 15360)
        for pack in ("l3a", "l3x", "l3f"):
            self.packs[pack] = self.load(pack, b, self.compute)
        self.b_hi = b.rest()
        self.extra = self.extra_b = Region(self.mem, self.a_start, 22528)

    def l2_xattn(self):
        PE, A, V, G = self.PE, self.ACT, self.DVE, self.POOL
        self.settle()
        w, x, xnT = self.packs["l2x"], self.x, self.xnT
        H, hd, HT4 = 16, 32, 4
        scale = float(np.float32(hd) ** np.float32(-0.5))
        c = self.load("l2x_rows", Region(self.mem, self.biases.start, 2700), self.compute)
        take = self.buffers(self.work, self.a_hi)
        acc = take(B, D, parts=S)
        xn, xT, xm = take(D, parts=S), take(KD, S), take(D, parts=S)
        q, qm, v = take(HT4, S), take(H, S), take(1, 512, parts=S)
        kT, yT = take(HT4, S), take(KD, S)
        P_sb, PT_sb, o, oT = take(4, S, parts=S), take(1, 4 * S), take(512, parts=S), take(HT4, S)
        self.need("l2x", PE, V, A)
        self.need("l2x_rows", V, A)
        row = lambda n: c["rows"][0:S, n, :]
        f = c["cols"]

        def col(n, k=KD):
            return f[:, n:n + k]

        def affine_norm(src, dst, g, b):
            self.norm(src, dst)
            V.after(V)
            self.tt(dst, dst, row(g), ALU.mult)
            V.after(V)
            self.tt(dst, dst, row(b), ALU.add)
            V.after(V)

        def close(b, y, base, lib, ln3):
            V.after(PE)
            self.tt(xn, y, row(lib), ALU.add)
            V.after(V)
            self.tt(xn, xn, base, ALU.add)
            V.after(V)
            self.tt(acc[:, b, :], xn, base, ALU.add)
            self.norm(xn, xm)
            V.after(V)
            self.turn_features(xm, xT, 0, col(ln3), col(ln3 + 2))
            G.after(V)
            self.copy(xnT[:, :, b, :], xT, G)
            V.after(G)

        def block1(b):
            PE.after(V, A)
            self.norm(x[:, b, :], xm)
            V.after(V)
            affine_norm(xm, xm, 0, 1)
            self.norm(xm, xn)
            V.after(V)
            self.turn_features(xn, xT, 0, col(0), col(2))
            V.after(PE)
            for k in range(KD):
                self.ts(yT[:, k, :], self.bank(0, P, KD * S)[:, k * S:(k + 1) * S],
                        f[:, 4 + k:5 + k], f[:, 6 + k:7 + k], ALU.mult, ALU.add)
            PE.after(V)
            src = [yT[:, k, :] for k in range(KD)]
            self.keys(kT, src, w["a1_wk"], None, 4)
            self.values_of(v, src, w["a1_wv"], None, 2, [(0, S)])
            self.queries(q, qm, xT, w["a1_wq"], None, scale, self.rows32, bank=1)
            self.narrow_attention(H, S, hd, qm, kT, v, o, P_sb, PT_sb, keepT=self.upperT)
            y = self.out_project(o, oT, w["a1_li1"], 4, 0)
            close(b, y, xm, 4, 8)
        self.prog.loop("l2_block1", B, lambda b: block1(b))
        self.settle()
        self.gelu_block("l2_block1_mlp", w["a1_li2"], w["a1_li3"], f[:, 32:40], row(5), acc, (w, take))

        self.settle()
        take = self.buffers(Region(self.mem, self.work.at + B * D, self.work.end - self.work.at - B * D), self.a_hi)
        xn, xT, xm = take(D, parts=S), take(KD, S), take(D, parts=S)
        q, qm, kT = take(HT4, S), take(H, S), take(HT4, CK)
        v, P_sb, PT_sb = take(CC, 512), take(4, CK, parts=S), take(CC, 4 * S)
        o, oT, ctx, cn, cT = take(512, parts=S), take(HT4, S), take(CC, P), take(P), take(CK)
        cst = take(12)
        self.load_context(0, ctx[0:CR].rearrange("p c n -> p (c n)"), "ctxN")

        def block2(b):
            for e in (PE, A, V):
                e.after(self.CTX)
            PE.after(V, A)
            for k in range(CC):
                V.after(V)
                V.do(self.nc.vector.bn_stats(cst[0:CR, 0:6], ctx[0:CR, k, :]))
                V.after(V)
                V.do(self.nc.vector.memset(cst[0:CR, 10:11], 0.0))
                V.do(self.nc.vector.bn_aggr(cst[0:CR, 6:8], cst[0:CR, 0:6]))
                V.after(V)
                self.ts(cst[0:CR, 8:9], cst[0:CR, 7:8], EPS, None, ALU.add)
                G.after(V)
                self.tt(cst[0:CR, 9:10], cst[0:CR, 8:9], self.minus_half[0:CR, :], ALU.pow, G)
                V.after(G, PE)
                self.ts(cn[0:CR, :], ctx[0:CR, k, :], cst[0:CR, 6:7], cst[0:CR, 9:10], ALU.subtract, ALU.mult)
                PE.after(V)
                self.tp(self.bank(k % 2, P, CR), cn[0:CR, :])
                V.after(PE)
                self.ts(cT[:, k * CR:(k + 1) * CR], self.bank(k % 2, P, CR), f[:, 20:21], f[:, 21:22], ALU.mult, ALU.add)
            self.load_context(b + 1, ctx[0:CR].rearrange("p c n -> p (c n)"), "ctxN")
            PE.after(V)
            self.keys(kT, [cT], w["a2_wk"], None, 4)
            self.values_of(v, [cT], w["a2_wv"], None, 1, self.CHUNKS)
            affine_norm(acc[:, b, :], xm, 2, 3)
            self.norm(xm, xn)
            V.after(V)
            self.turn_features(xn, xT, 0, col(12), col(14))
            PE.after(V, A)
            self.queries(q, qm, xT, w["a2_wq"], None, scale, self.rows32, bank=7)
            self.narrow_attention(H, CK, hd, qm, kT, v, o, P_sb, PT_sb)
            y = self.out_project(o, oT, w["a2_li1"], 4, 0)
            close(b, y, xm, 6, 16)
        self.prog.loop("l2_block2", B, lambda b: block2(b))
        self.settle()
        for half in range(2):
            self.tt(x[:, half * HALF:(half + 1) * HALF, :], x[:, half * HALF:(half + 1) * HALF, :],
                    acc[:, half * HALF:(half + 1) * HALF, :], ALU.add)
        V.after(V)
        self.gelu_block("l2_block2_mlp", w["a2_li2"], w["a2_li3"], f[:, 40:48], row(7), x, (w, take))

    def gelu_block(self, name, w2, w3, b2, b3, into, _):
        PE, A, V = self.PE, self.ACT, self.DVE
        xnT = self.xnT
        h = Region(self.mem, self.a_hi.start, 8192).take(8, HT)

        def turn(i):
            free = {}
            PE.after(V, A)
            flat = [xnT[:, k, bass.ds(i * HALF, HALF), :].rearrange("p b s -> p (b s)") for k in range(KD)]

            def fill(u, bk):
                self.project(self.bank(bk, P, HT), [w2[:, k, u * P:(u + 1) * P] for k in range(KD)], flat)

            def drain(u, bk):
                A.after(PE)
                self.act(h[:, u, :], self.bank(bk, P, HT), ACT.Gelu, bias=b2[:, u:u + 1], scale=1.0)
                return (A.mark(),)
            self.tile_stream(8, (0, 1, 2, 3), fill, drain, free)
            PE.after(A)

            def finish(j, at, y):
                dst = self.xs(into, at)
                V.after(V)
                self.tt(dst, dst, y, ALU.add)
                V.after(V)
                self.tt(dst, dst, b3, ALU.add)
            self.down(i, h, w3, free, finish)
        self.prog.loop(name, 2, turn)

    def l2_ffn(self):
        PE, A, V, G = self.PE, self.ACT, self.DVE, self.POOL
        self.settle()
        self.fetch_l2f_rest()
        self.fetch_l3()
        w, w2, x = self.packs["l2f"], self.packs["l2f2"], self.x
        s = self.load("l2f_scales", Region(self.mem, self.biases.start, 2700), self.compute)
        take = self.buffers(self.b_hi, self.work)
        h1, h2 = take(8, HT), take(8, HT)
        xT, g_sb, xn = self.xnT[:, :, 0:HALF, :], take(2, HT), take(D, parts=S)
        self.need("l2f", PE)
        self.need("l2f_scales", A, V)

        def turn(i):
            free = {}
            PE.after(V, A)
            self.norm_half(i, x, xn, xT)
            PE.after(V)
            self.gated(8, xT, w["w1"], w["w2"], h1, g_sb, free, (s["s1"], s["s2"]))

            def dense(src, dst, ww, sc):
                PE.after(A, V)

                def fill(u, bk):
                    self.project(self.bank(bk, P, HT), [ww[:, k, u * P:(u + 1) * P] for k in range(8)],
                                 [src[:, k, :] for k in range(8)])

                def drain(u, bk):
                    A.after(PE)
                    self.act(dst[:, u, :], self.bank(bk, P, HT), ACT.Gelu, scale=sc[:, u:u + 1])
                    return (A.mark(),)
                self.tile_stream(8, (0, 1, 2, 3, 4, 5), fill, drain, free)
            dense(h1, h2, w["h1"], s["h1s"])
            self.need("l2f2", PE)
            dense(h2, h1, w2["h2"], s["h2s"])
            PE.after(A)

            def finish(j, at, y):
                V.after(V)
                self.tt(xn, y, s["s3"][0:S, :], ALU.mult)
                V.after(V)
                self.tt(self.xs(x, at), self.xs(x, at), xn, ALU.add)
            self.down(i, h1, w["w3"], free, finish)
        self.prog.loop("l2_ffn", 2, turn)

    def l3_attn(self):
        nc, PE, A, V, G = self.nc, self.PE, self.ACT, self.DVE, self.POOL
        self.settle()
        w, x = self.packs["l3a"], self.x
        H, DEPTH, hd = 8, 5, 32
        R = H * DEPTH
        take = self.buffers(self.work, self.extra)
        xn, xT = take(D, parts=S), take(KD, S)
        left, right = take(S, parts=65), take(R, S, parts=65)
        v, P_sb, PT_sb = take(1, D, parts=S), take(4, S, parts=S), take(1, 4 * S)
        o, oT, bp = take(D, parts=S), take(KD, S), take(1)
        self.need("l3a", PE, V, A)
        self.ts(bp, w["bp"], 0.5, None, ALU.mult)
        V.do(nc.vector.memset(left, 0.0))
        V.do(nc.vector.memset(right, 0.0))
        V.after(V)
        V.do(nc.vector.memset(left[64:65, :], 1.0))
        V.do(nc.vector.memset(right[64:65], 0.5))
        V.after(V)

        def batch(b):
            PE.after(V, A)
            self.norm(x[:, b, :], xn)
            V.after(V)
            self.turn_features(xn, xT, 0)
            PE.after(V)
            src = [xT[:, k, :] for k in range(KD)]
            self.project(self.bank(1, R, S), [w["wp"][:, k, :] for k in range(KD)], src)
            A.after(PE, V)
            self.act(left[0:R, :], self.bank(1, R, S), ACT.Tanh, bias=bp[0:R, :], scale=0.5)
            self.values_of(v, src, w["wv"], None, 2, [(0, S)])
            V.after(A, PE)
            self.tt(right[0:R], left[0:R, :].unsqueeze(1).broadcast_to([R, R, S]),
                    w["half_eye"][0:R, :].unsqueeze(2).broadcast_to([R, R, S]), ALU.mult)

            def fill(g, dst):
                for d in range(DEPTH - 1, -1, -1):
                    bk = d % 4
                    PE.after(V, A)
                    at = d * H + 4 * g
                    self.mm(self.bank(bk, S, 4 * S), left, right[:, at:at + 4, :], count=True)
                    V.after(PE, V)
                    agree = self.bank(bk, S, 4 * S).rearrange("p (h s) -> p h s", h=4)
                    if d == DEPTH - 1:
                        self.copy(dst, agree, V)
                    else:
                        self.stt(dst, dst, 1.0, agree, ALU.add, ALU.mult)
                V.after(V)
                self.stt(dst, dst, 1.0 / DEPTH, self.causal[0:S, :].unsqueeze(1).broadcast_to([S, 4, S]),
                         ALU.mult, ALU.add)
            self.attention(H, S, hd, None, lambda n, c: None, o, P_sb=P_sb, PT_sb=PT_sb, fill=fill, vals=v)
            y = self.out_project(o, oT, w["wo"], 4, 0)
            V.after(PE)
            self.tt(x[:, b, :], x[:, b, :], y, ALU.add)
        self.prog.loop("l3_attn", B, batch)

    def quantize(self, src, gs, dst, y, t, sc, blocks):
        V, nc = self.DVE, self.nc
        p = src.shape[0]
        b3 = lambda a: a.rearrange("p (n k) -> p n k", k=16)
        wide = lambda a: a.unsqueeze(2).broadcast_to([p, blocks, 16])
        top, s8, c8 = sc[:, 0], sc[:, 1], sc[:, 2]
        V.after(V)
        V.do(nc.vector.tensor_reduce(top, b3(src), AX, ALU.max, apply_absolute_value=True))
        V.after(V)
        self.ts(top, top, 1.0 / 6.0, gs, ALU.mult, ALU.mult)
        V.after(V)
        self.ts(top, top, 448.0, None, ALU.min)
        V.after(V)
        self.ts(c8.bitcast(I32), top.bitcast(I32), 0x7F800000, None, ALU.bitwise_and)
        V.after(V)
        self.ts(c8, c8, 2.0 ** -6, 1.5 * 2.0 ** 20, ALU.max, ALU.mult)
        V.after(V)
        self.tt(s8, top, c8, ALU.add)
        V.after(V)
        self.tt(s8, s8, c8, ALU.subtract)
        V.after(V)
        self.ts(c8, s8, 2.0 ** -9, None, ALU.max)
        V.after(V)
        V.do(nc.vector.reciprocal(c8, c8))
        V.after(V)
        self.ts(c8, c8, gs, 1.0 + 2.0 ** -22, ALU.mult, ALU.mult)
        V.after(V)
        self.tt(b3(y), b3(src), wide(c8), ALU.mult)
        V.after(V)
        self.ts(y, y, 6.0, -6.0, ALU.min, ALU.max)
        V.after(V)
        self.ts(t.bitcast(I32), y.bitcast(I32), 0x7F800000, None, ALU.bitwise_and)
        V.after(V)
        self.ts(t, t, 1.0, 1.5 * 2.0 ** 22, ALU.max, ALU.mult)
        V.after(V)
        self.tt(y, y, t, ALU.add)
        V.after(V)
        self.tt(y, y, t, ALU.subtract)
        V.after(V)
        self.tt(b3(dst), b3(y), wide(s8), ALU.mult)

    def tp16(self, src, dst, n, bank, lane):
        PE = self.PE
        rows = src.shape[0]
        PE.after(self.DVE, self.ACT)
        ps = self.banks[:, bank, :].bitcast(BF16)[:, 0:n * rows].rearrange("p (n r) -> p n r", n=n)
        for k in range(n):
            ins = self.nc.tensor.transpose(ps[:, k, :], src[:, k * P:(k + 1) * P], self.ident16[0:rows, 0:rows])
        PE.do(ins)
        lane.after(PE)
        self.copy(dst, ps, lane)

    def l3_ffn(self):
        nc, PE, A, V, G = self.nc, self.PE, self.ACT, self.DVE, self.POOL
        self.settle()
        w, x = self.packs["l3f"], self.x
        take = self.buffers(self.work, self.extra)
        self.ident16 = take(P, dt=BF16)
        self.copy(self.ident16, self.ident, V)
        self.need("l3f", V, A, G)
        HID = 1024
        big, gs = take(3), take(3)
        y, t, sc = take(2048), take(2048), take(3, P)
        wq = take(2048, dt=BF16)
        wT = {"gate": take(KD, HID, dt=BF16), "up": take(KD, HID, dt=BF16), "down": take(8, D, dt=BF16)}
        for n, name in enumerate(("gate", "up", "down")):
            V.do(nc.vector.tensor_reduce(big[:, n:n + 1], w[name].rearrange("p o i -> p (o i)"), AX, ALU.max,
                                         apply_absolute_value=True))
        G.after(V)
        top = take(3)
        G.do(nc.gpsimd.partition_all_reduce(top, big, P, bass.bass_isa.ReduceOp.max))
        V.after(G)
        V.do(nc.vector.reciprocal(gs, top))
        V.after(V)
        self.ts(gs, gs, 448.0 * 6.0, None, ALU.mult)
        inv = take(3)
        V.after(V)
        for n in range(3):
            self.tt(inv[:, n:n + 1], gs[:, n:n + 1], w["s_in"][:, (0, 0, 1)[n]:(0, 0, 1)[n] + 1], ALU.mult)
        V.after(V)
        V.do(nc.vector.reciprocal(inv, inv))
        for n, name in enumerate(("gate", "up", "down")):
            V.after(PE)
            self.quantize(w[name].rearrange("p o i -> p (o i)"), gs[:, n:n + 1], wq, y, t, sc, P)
            it = w[name].shape[2] // P
            for o in range(w[name].shape[1]):
                cols = wq[:, o * it * P:(o + 1) * it * P]
                self.tp16(cols, wT[name][:, :, o * P:(o + 1) * P], it, o % 4, A)
        xn, xq, xT = take(D, parts=S), take(D, dt=BF16, parts=S), take(KD, S, dt=BF16)
        sg, hid, hq = take(HID, parts=S), take(HID, parts=S), take(HID, dt=BF16, parts=S)
        hT, tmp = take(8, S, dt=BF16), take(D, parts=S)
        self.settle()

        def batch(b):
            PE.after(V, A)
            self.norm(x[:, b, :], xn)
            self.quantize(xn, w["s_in"][0:S, 0:1], xq, y[0:S, 0:D], t[0:S, 0:D], sc[0:S, :, 0:D // 16], D // 16)
            self.tp16(xq, xT, KD, 4, V)
            PE.after(V)
            for o, name in ((0, "gate"), (2, "up")):
                for half in range(2):
                    self.project(self.bank(o + half, S), [xT[:, k, :] for k in range(KD)],
                                 [wT[name][:, k, half * 512:(half + 1) * 512] for k in range(KD)])
            A.after(PE, V)
            self.act(sg.rearrange("p (h n) -> p h n", h=2), self.banks[0:S, 0:2, :], ACT.Silu, scale=inv[0:S, 0:1])
            V.after(A, PE)
            self.stt(hid.rearrange("p (h n) -> p h n", h=2), self.banks[0:S, 2:4, :], inv[0:S, 1:2],
                     sg.rearrange("p (h n) -> p h n", h=2), ALU.mult, ALU.mult)
            self.quantize(hid, w["s_in"][0:S, 1:2], hq, y[0:S, 0:HID], t[0:S, 0:HID], sc[0:S, :, 0:HID // 16], HID // 16)
            self.tp16(hq, hT, 8, 5, A)
            PE.after(A)
            self.project(self.bank(6, S, D), [hT[:, k, :] for k in range(8)], [wT["down"][:, k, :] for k in range(8)])
            V.after(PE, V)
            self.stt(x[:, b, :], self.bank(6, S, D), inv[0:S, 2:3], x[:, b, :], ALU.mult, ALU.add)
        self.prog.loop("l3_ffn", B, batch)

SUBLAYERS = (Decoder.l0_attn, Decoder.l0_xattn, Decoder.l0_ffn, Decoder.l1_attn, Decoder.l1_xattn, Decoder.l1_ffn,
             Decoder.l2_attn, Decoder.l2_xattn, Decoder.l2_ffn, Decoder.l3_attn, Decoder.l3_xattn, Decoder.l3_ffn)


def build(nc, ins, layouts, out, per_turn, stages=None):
    from contextlib import ExitStack
    with ExitStack() as stack:
        d = Decoder(nc, stack, ins, layouts, out, per_turn)
        d.start()
        for stage in stages or SUBLAYERS:
            stage(d)
        d.SP.after(*d.compute, d.CTX)
        done = Lane(d.prog, "out_stored", nc.sync, 16)
        done.do(nc.sync.dma_start(out, d.x))
        nc.sync.wait_ge(done.sem, 16)
        return d.prog.counted


def lay_out(i):
    f = lambda name: np.asarray(i[name])

    def inout(w):
        return w.reshape(-1, P, w.shape[1]).transpose(1, 0, 2)

    def col(b):
        return b.reshape(-1, P).T

    def row(b):
        return np.broadcast_to(b[None, :], (P, b.shape[0]))

    def pad(a):
        return np.concatenate([a, np.zeros((P - a.shape[0],) + a.shape[1:], a.dtype)], 0)

    packs = {}
    iota = np.arange(S)
    dist = iota[:, None] - iota[None, :]
    near = np.where(np.abs(dist) <= 3, np.exp(-(dist.astype(np.float32) ** 2) / np.float32(2.0 * 0.4 ** 2)), 0.0)
    near = near / (near.sum(-1, keepdims=True) + 1e-10)
    c32 = lambda a: np.ascontiguousarray(a, np.float32)
    packs["consts"] = {
        "ident": np.eye(P, dtype=np.float32),
        "causal": pad(c32(np.where(dist >= 0, 0.0, MASKED))),
        "upperT": pad(c32(dist > 0)),
        "rows16": c32(np.arange(P)[:, None] // 16 == np.arange(8)),
        "rows32": c32(np.arange(P)[:, None] // 32 == np.arange(4)),
        "prefix": pad(c32(dist.T >= 0)),
        "ones": np.ones((P, S), np.float32),
        "turn8": row(c32(8 - np.arange(8))),
        "spread": pad(c32((1.0 - 0.6) * near.T)),
    }
    order = [0, 1, 3, 2]
    gates = lambda w: w.reshape(4, D, -1)[order].reshape(4 * D, -1)
    both = lambda n: np.stack([inout(gates(f(f"L0_attn_{n}_q")).T), inout(gates(f(f"L0_attn_{n}_k")).T)], 1)
    wk2 = f("L0_attn_Wk2").reshape(4, 64, 64)
    packs["l0a"] = {
        "wih": both("Wih"),
        "wq1": inout(f("L0_attn_Wq1").T), "wk1": inout(f("L0_attn_Wk1").T),
        "wq2": pad(f("L0_attn_Wq2").T),
        "wk2": pad(np.stack([wk2, wk2], 1).reshape(512, 64).T),
        "wv": inout(f("L0_attn_Wv").T), "wo": inout(f("L0_attn_Wo").T),
    }
    bk2 = f("L0_attn_bk2").reshape(4, 64)
    packs["l0a_whh"] = {"whh": both("Whh")}
    packs["l0a_bias"] = {
        "b_lstm": np.concatenate([col(gates(f("L0_attn_b_q"))[:, 0]), col(gates(f("L0_attn_b_k"))[:, 0])], 1),
        "bq1": pad(f("L0_attn_bq1")[:, None]), "bk1": pad(f("L0_attn_bk1")[:, None]),
        "bq2": col(f("L0_attn_bq2")), "bk2": np.concatenate([bk2, bk2], 1).T,
        "bv": row(f("L0_attn_bv")),
    }
    packs["l0x"] = {"wq": inout(f("L0_xattn_Wq")), "wk": inout(f("L0_xattn_Wk")), "wv": inout(f("L0_xattn_Wv")),
                    "bq": col(f("L0_xattn_bq")), "bk": col(f("L0_xattn_bk")), "bv": row(f("L0_xattn_bv"))}
    packs["l0f"] = {"wg": inout(f("L0_ffn_w_gate").T), "wu": inout(f("L0_ffn_w_up").T),
                    "wd": inout(f("L0_ffn_w_down").T)}
    packs["l1a"] = {"wq": inout(f("L1_attn_Wq").T), "wk": inout(f("L1_attn_Wk").T), "wv": inout(f("L1_attn_Wv").T),
                    "wo": inout(f("L1_attn_Wo").T), "bq": col(f("L1_attn_bq")), "bk": col(f("L1_attn_bk")),
                    "bv": row(f("L1_attn_bv")), "bo": row(f("L1_attn_bo"))}
    packs["l1x"] = {"wq": inout(f("L1_xattn_Wq")), "wk": inout(f("L1_xattn_Wk")), "wv": inout(f("L1_xattn_Wv")),
                    "wo": inout(f("L1_xattn_Wo")), "bq": col(f("L1_xattn_bq")), "bk": col(f("L1_xattn_bk")),
                    "bv": row(f("L1_xattn_bv")), "bo": row(f("L1_xattn_bo"))}
    packs["l1f"] = {
        "router": inout(f("L1_ffn_gate_w").T),
        "dg": np.concatenate([inout(w.T) for w in f("L1_ffn_dyn_gate_w")], 2),
        "du": np.concatenate([inout(w.T) for w in f("L1_ffn_dyn_up_w")], 2),
        "dd": np.concatenate([inout(w.T) for w in f("L1_ffn_dyn_down_w")], 1),
        "sg": inout(f("L1_ffn_sh_gate_w")[0].T), "su": inout(f("L1_ffn_sh_up_w")[0].T),
        "sd": inout(f("L1_ffn_sh_down_w")[0].T),
    }
    swap = lambda w: w.reshape(D, -1, 2, 64)[:, :, ::-1].reshape(D, -1)
    packs["l2a"] = {"wq": inout(f("L2_attn_Wq")), "wqs": inout(swap(f("L2_attn_Wq"))),
                    "wk": inout(f("L2_attn_Wk")), "wks": inout(swap(f("L2_attn_Wk"))),
                    "wv": inout(f("L2_attn_Wv")), "wo": inout(f("L2_attn_Wo"))}
    inv_freq = (1.0 / np.float32(10000.0) ** (np.arange(0, P, 2, dtype=np.float32) / np.float32(P))).astype(np.float32)
    angle = np.outer(np.concatenate([inv_freq, inv_freq]), iota.astype(np.float32)).astype(np.float32)
    sign = np.where(np.arange(P) < P // 2, -1.0, 1.0)[:, None]
    unit = 1.0 / np.sqrt(np.float32(P))
    packs["rope"] = {"cosq": c32(np.cos(angle) * unit), "sinq": c32(np.sin(angle) * sign * unit),
                     "cos": c32(np.cos(angle)), "sin": c32(np.sin(angle) * sign)}
    x2 = lambda n: f(f"L2_xattn_{n}")
    heads = lambda w: inout(w.transpose(1, 0, 2).reshape(w.shape[1], -1))
    packs["l2x"] = {"a1_wq": heads(x2("a1_wq")), "a1_wk": heads(x2("a1_wk")), "a1_wv": heads(x2("a1_wv")),
                    "a1_li1": inout(x2("a1_li1_w")), "a1_li2": inout(x2("a1_li2_w")), "a1_li3": inout(x2("a1_li3_w")),
                    "a2_wq": heads(x2("a2_wq")), "a2_wk": heads(x2("a2_wk")), "a2_wv": heads(x2("a2_wv")),
                    "a2_li1": inout(x2("a2_li1_w")), "a2_li2": inout(x2("a2_li2_w")), "a2_li3": inout(x2("a2_li3_w"))}
    cols = [col(x2(n)) for n in ("a1_lnx_g", "a1_lnx_b", "a1_lny_g", "a1_lny_b", "a1_ln3_g", "a1_ln3_b",
                                 "a2_lnx_g", "a2_lnx_b", "a2_ln3_g", "a2_ln3_b", "a2_lny_g", "a2_lny_b")]
    packs["l2x_rows"] = {
        "rows": np.stack([row(x2(n)) for n in ("ln1_g", "ln1_b", "ln2_g", "ln2_b", "a1_li1_b", "a1_li3_b",
                                               "a2_li1_b", "a2_li3_b")], 1),
        "cols": np.concatenate(cols + [np.zeros((P, 10), np.float32), col(x2("a1_li2_b")), col(x2("a2_li2_b"))], 1)}
    l2 = lambda n: f(f"L2_ffn_{n}")
    packs["l2f"] = {"w1": inout(l2("w1_w").T), "w2": inout(l2("w2_w").T), "h1": inout(l2("h1_w").T),
                    "w3": inout(l2("w3_w").T)}
    packs["l2f2"] = {"h2": inout(l2("h2_w").T)}
    packs["l2f_scales"] = {"s1": col(l2("w1_s")), "s2": col(l2("w2_s")), "h1s": col(l2("h1_s")),
                           "h2s": col(l2("h2_s")), "s3": row(l2("w3_s"))}
    by_depth = lambda w: w.reshape(-1, 8, 5).transpose(0, 2, 1).reshape(-1, 40)
    packs["l3a"] = {"wp": inout(by_depth(f("L3_attn_Wp"))), "bp": pad(by_depth(f("L3_attn_bp")[None])[0][:, None]),
                    "half_eye": pad(c32(0.5 * np.eye(40))),
                    "wv": inout(f("L3_attn_Wv")), "wo": inout(f("L3_attn_Wo"))}
    wkv = f("L3_xattn_Wkv")
    packs["l3x"] = {"wq": inout(f("L3_xattn_Wq").T), "wk": inout(wkv[0:D].T), "wv": inout(wkv[D:2 * D].T),
                    "wo": inout(f("L3_xattn_Wo").T)}
    natural = lambda w: w.reshape(-1, P, w.shape[1]).transpose(1, 0, 2)
    packs["l3f"] = {"gate": natural(f("L3_ffn_gate_w")), "up": natural(f("L3_ffn_up_w")),
                    "down": natural(f("L3_ffn_down_w")),
                    "s_in": row(np.concatenate([f("L3_ffn_s_in"), f("L3_ffn_s_in_down")]))}
    arrays = {"x": np.ascontiguousarray(f("x").transpose(1, 0, 2))}
    ctx = f("ctx_512")
    ahead = np.concatenate([ctx, ctx[:1]], 0)
    arrays["ctxT"] = np.ascontiguousarray(ahead.transpose(0, 2, 1))
    arrays["ctxN"] = np.ascontiguousarray(ahead.reshape(B + 1, CC, CR, CD).transpose(0, 2, 1, 3).reshape(B + 1, CR, -1))
    layouts = {}
    for name, pack in packs.items():
        layouts[name] = [(k, a.shape[1:]) for k, a in pack.items()]
        arrays[name] = np.ascontiguousarray(np.concatenate([a.reshape(P, -1) for a in pack.values()], 1))
    return arrays, layouts


def kernel(**inputs):
    import concourse.bacc as bacc
    from concourse.bass_utils import run_bass_kernel_spmd

    arrays, layouts = lay_out(inputs)
    per_turn = {}
    for _ in range(2):
        nc = bacc.Bacc("TRN2", target_bir_lowering=False, num_devices=1)
        ins = {k: nc.dram_tensor(f"in_{k}", a.shape, mybir.dt.from_np(a.dtype), kind="ExternalInput").ap()
               for k, a in arrays.items()}
        out = nc.dram_tensor("out", (S, B, D), F32, kind="ExternalOutput").ap()
        per_turn = build(nc, ins, layouts, out, per_turn)
    r = run_bass_kernel_spmd(nc, [{f"in_{k}": a for k, a in arrays.items()}], core_ids=[0])
    return np.ascontiguousarray(r.results[0]["out"].transpose(1, 0, 2))
```

```python
import numpy as np
import concourse.bass as bass
import concourse.mybir as mybir
from concourse.alu_op_type import AluOpType as ALU

F32 = mybir.dt.float32
BF16 = mybir.dt.bfloat16
I32 = mybir.dt.int32
ACT = mybir.ActivationFunctionType
AX = mybir.AxisListType.X

P = 128
B, S, D = 8, 112, 256
T = B * S
KD = D // P
CK, CD = 375, 128
CC = 3
CR = CK // CC
HALF = B // 2
HT = HALF * S
EPS = 1e-5
MASKED = -1e30


class Lane:

    def __init__(self, prog, name, engine, step=1):
        self.prog, self.name, self.engine, self.step = prog, name, engine, step
        self.sem = prog.stack.enter_context(prog.nc.semaphore(name))
        self.n = 0
        self.base = 0
        self.seen = {}
        prog.lanes.append(self)

    def do(self, ins):
        self.n += self.step
        return ins.then_inc(self.sem, self.step)

    def mark(self):
        return (self, self.n, self.prog.turn)

    def after(self, *points):
        for pt in points:
            lane, k, turn = pt.mark() if isinstance(pt, Lane) else pt
            if self.seen.get((lane.name, turn), -1) >= k:
                continue
            self.seen[(lane.name, turn)] = k
            if turn is None or turn is not self.prog.turn:
                if k:
                    self.engine.wait_ge(lane.sem, k)
            else:
                per = self.prog.per_turn.get((turn.name, lane.name), 0)
                if per:
                    self.engine.wait_ge(lane.sem, turn.i * per + (lane.base + k))
                elif lane.base + k:
                    self.engine.wait_ge(lane.sem, lane.base + k)


class Turn:
    def __init__(self, name, i, times):
        self.name, self.i, self.times = name, i, times


class Prog:

    def __init__(self, nc, stack, per_turn):
        self.nc, self.stack, self.per_turn = nc, stack, per_turn
        self.lanes, self.turn, self.counted = [], None, {}

    def loop(self, name, times, body):
        for lane in self.lanes:
            lane.base, lane.n, lane.seen = lane.n, 0, {}
        with self.nc.Fori(0, times) as i:
            self.turn = Turn(name, i, times)
            body(i)
        for lane in self.lanes:
            self.counted[(name, lane.name)] = lane.n
            lane.n, lane.base, lane.seen = lane.base + times * lane.n, 0, {}
        self.turn = None


class Region:

    def __init__(self, mem, start, words):
        self.mem, self.start, self.at, self.end = mem, start, start, start + words

    def take(self, *dims, dt=F32, parts=P):
        n = int(np.prod(dims))
        words = n if dt in (F32, I32) else (n + 1) // 2
        a = self.mem[0:parts, self.at:self.at + words]
        self.at += words
        assert self.at <= self.end, (self.at, self.end)
        if dt is not F32:
            a = a.bitcast(dt)
        names = "abcde"[:len(dims)]
        if len(dims) > 1:
            a = a.rearrange(f"p ({' '.join(names)}) -> p {' '.join(names)}",
                            **{c: d for c, d in zip(names, dims)})
        return a

    def rest(self):
        return Region(self.mem, self.at, self.end - self.at)


class Decoder:

    def __init__(self, nc, stack, ins, layouts, out, per_turn):
        self.nc, self.ins, self.layouts, self.out = nc, ins, layouts, out
        self.prog = Prog(nc, stack, per_turn)
        lane = lambda name, engine, step=1: Lane(self.prog, name, engine, step)
        self.PE = lane("pe_done", nc.tensor)
        self.ACT = lane("act_done", nc.scalar)
        self.DVE = lane("dve_done", nc.vector)
        self.POOL = lane("pool_done", nc.gpsimd)
        self.SP = lane("sp_done", nc.sync)
        self.CTX = lane("ctx_landed", nc.sync, 16)
        self.compute = (self.PE, self.ACT, self.DVE, self.POOL)
        self.landed = {}

        words = 53100
        mem = stack.enter_context(nc.sbuf_tensor("memory", [P, words], F32))
        self.mem = mem
        ps = stack.enter_context(nc.psum_tensor("banks", [P, 8, 512], F32))
        self.bank = lambda n, parts=P, cols=512: ps[0:parts, n, 0:cols]
        self.banks = ps
        whole = Region(mem, 0, words)
        self.x = whole.take(B + 1, D, parts=S)
        self.xnT = whole.take(KD, B + 1, S)
        self.small = Region(mem, whole.at, 900)
        whole.at += 900
        self.biases = Region(mem, whole.at, 2700)
        whole.at += 2700
        self.A = Region(mem, whole.at, 22528)
        whole.at += 22528
        self.Bm = Region(mem, whole.at, 15360)
        whole.at += 15360
        self.work = whole.rest()
        self.a_start, self.packs = self.A.start, {}
        self.marks = {}
        self.stats = self.small.take(16, parts=S)
        self.minus_half = self.small.take(1)

    def load(self, pack, region, after=()):
        self.SP.after(*after)
        lane = Lane(self.prog, f"{pack}_landed", self.nc.sync, 16)
        self.landed[pack] = lane
        first, arrays = region.at, {}
        dt = self.ins[pack].dtype
        for name, shape in self.layouts[pack]:
            arrays[name] = region.take(*shape, dt=dt)
        dst = self.mem[:, first:region.at]
        lane.do(self.nc.sync.dma_start(dst if dt is F32 else dst.bitcast(dt), self.ins[pack]))
        return arrays

    def need(self, pack, *lanes):
        for lane in lanes:
            lane.after(self.landed[pack])

    def mm(self, out, lhsT, rhs, start=True, stop=True, count=False):
        ins = self.nc.tensor.matmul(out, lhsT, rhs, start=start, stop=stop)
        if count:
            self.PE.do(ins)

    def project(self, out, weights, acts, count=True):
        n = len(weights)
        for k in range(n):
            self.mm(out, weights[k], acts[k], k == 0, k == n - 1, count and k == n - 1)

    def tp(self, out, in_, count=True):
        n = in_.shape[0]
        ins = self.nc.tensor.transpose(out, in_, self.ident[0:n, 0:n])
        if count:
            self.PE.do(ins)

    def tt(self, out, a, b, op, lane=None):
        lane = lane or self.DVE
        lane.do(lane.engine.tensor_tensor(out, a, b, op))

    def ts(self, out, a, s1, s2, op0, op1=None, lane=None):
        lane = lane or self.DVE
        lane.do(lane.engine.tensor_scalar(out, a, s1, s2, op0, op1) if op1 is not None
                else lane.engine.tensor_scalar(out, a, s1, None, op0))

    def stt(self, out, a, s, b, op0, op1):
        self.DVE.do(self.nc.vector.scalar_tensor_tensor(out=out, in0=a, scalar=s, in1=b, op0=op0, op1=op1))

    def act(self, out, in_, func, **kw):
        self.ACT.do(self.nc.scalar.activation(out, in_, func, **kw))

    def copy(self, out, in_, lane):
        lane.do(lane.engine.copy(out, in_) if lane is self.ACT else lane.engine.tensor_copy(out, in_))

    def norm(self, src, dst):
        DVE, POOL, st = self.DVE, self.POOL, self.stats
        DVE.do(self.nc.vector.bn_stats(st[:, 0:6], src))
        DVE.after(DVE)
        DVE.do(self.nc.vector.memset(st[:, 10:11], 0.0))
        DVE.do(self.nc.vector.bn_aggr(st[:, 6:8], st[:, 0:6]))
        DVE.after(DVE)
        self.ts(st[:, 8:9], st[:, 7:8], EPS, None, ALU.add)
        POOL.after(DVE)
        self.tt(st[:, 9:10], st[:, 8:9], self.minus_half[0:S, :], ALU.pow, POOL)
        DVE.after(POOL)
        self.ts(dst, src, st[:, 6:7], st[:, 9:10], ALU.subtract, ALU.mult)

    def turn_features(self, src, dst, bank, gain=None, shift=None):
        PE, DVE = self.PE, self.DVE
        PE.after(DVE)
        pt = self.bank(bank, P, KD * S).rearrange("p (k s) -> p k s", k=KD)
        for k in range(KD):
            self.tp(pt[:, k, :], src[:, k * P:(k + 1) * P], k == KD - 1)
        DVE.after(PE)
        if gain is None:
            self.copy(dst, pt, DVE)
        else:
            for k in range(KD):
                self.ts(dst[:, k, :], pt[:, k, :], gain[:, k:k + 1], shift[:, k:k + 1], ALU.mult, ALU.add)

    def since(self, key, *lanes):
        return self.marks.get(key) or [(lane, 0, self.prog.turn) for lane in lanes]

    def via_misc(self, parts, cols, fill, drain, lane):
        n = self.next_misc()
        bk = self.bank(n, parts, cols)
        fill(bk)
        lane.after(self.PE)
        drain(bk)
        self.marks[("misc", n)] = [lane.mark()]

    def next_misc(self):
        n = self.misc_banks[self.misc_at % len(self.misc_banks)]
        self.misc_at += 1
        self.PE.after(*self.since(("misc", n), self.DVE, self.ACT))
        return n

    def attend_all(self, name, H, nk, hd, bufs, score, value, prologue, epilogue, *, o, P_sb, PT_sb,
                   mask=None, keepT=None, fill=None, spread=False, o_banks=(7,), share=1.0, plus=None,
                   side=None, late=None):
        PE, A, V, G, nc, M = self.PE, self.ACT, self.DVE, self.POOL, self.nc, self.marks
        Q = min(4, H)
        groups = H // Q
        wide = nk > S
        chunks = self.CHUNKS if wide else [(0, nk)]
        per_bank = 512 // hd
        ring = (0, 1, 2, 0)
        self.misc_banks, self.misc_at = side or ((3,) if wide and H > 1 else (1, 2, 3) if wide else (2, 3)), 0

        def scores(buf, g):
            if fill is not None:
                return
            for h in range(Q):
                n = Q * g + h
                if wide:
                    out = self.bank(ring[h], S, nk)
                    PE.after(*self.since(("s", ring[h]), A))
                else:
                    out = self.bank(g % 2, S, Q * nk)[:, h * nk:(h + 1) * nk]
                    if h == 0:
                        PE.after(*self.since(("s", g % 2), A, V))
                pairs = score(buf, n)
                self.project(out, [q for q, _ in pairs], [k for _, k in pairs])
                M[("sc", h)] = [PE.mark()]
                if wide:
                    weigh(buf, n, h, out)

        def weigh(buf, n, h, src):
            V.after(*M[("sc", h)])
            V.do(nc.vector.tensor_reduce(buf["nmax"][:, n:n + 1], src, AX, ALU.max, negate=True))
            A.after(V, *self.since("turn", PE))
            self.act(P_sb[:, h, :], src, ACT.Exp, bias=buf["nmax"][:, n:n + 1], scale=1.0,
                     accum_out=buf["total"][:, n:n + 1])
            M[("s", ring[h])] = [A.mark()]
            M["exp"] = [A.mark()]

        def weigh_group(buf, g):
            if wide:
                return
            src = self.bank(g % 2, S, Q * nk).rearrange("p (h k) -> p h k", h=Q)
            if fill is not None:
                V.after(*self.since("turn", PE))
                fill(buf, g, P_sb)
                src = P_sb
            else:
                V.after(*M[("sc", Q - 1)])
                if mask is not None:
                    V.after(*self.since("turn", PE))
                    self.tt(P_sb, src, mask[0:S, :].unsqueeze(1).broadcast_to([S, Q, nk]), ALU.add)
                    M[("s", g % 2)] = [V.mark()]
                    src = P_sb
            V.after(V)
            n = Q * g
            V.do(nc.vector.tensor_reduce(buf["nmax"][:, n:n + Q], src, AX, ALU.max, negate=True))
            A.after(V, *self.since("turn", PE))
            for h in range(Q):
                self.act(P_sb[:, h, :], src[:, h, :], ACT.Exp, bias=buf["nmax"][:, n + h:n + h + 1],
                         scale=1.0, accum_out=buf["total"][:, n + h:n + h + 1])
            if src is not P_sb:
                M[("s", g % 2)] = [A.mark()]
            M["exp"] = [A.mark()]

        def turn(g):
            PE.after(*self.since("exp", A))
            marks = []
            for c, (at, rows) in enumerate(chunks):
                bank = 4 + c if wide else 4 + g % 2
                pt = self.bank(bank, rows, Q * S)
                PE.after(*self.since(("pt", bank), A, V))
                for h in range(Q):
                    self.tp(pt[:, h * S:(h + 1) * S], P_sb[:, h, at:at + rows], h == Q - 1)
                lane = A if c == 1 else V
                lane.after(PE, *self.since("values", PE))
                if keepT is not None:
                    self.tt(PT_sb[0:rows, c, :].rearrange("p (h s) -> p h s", h=Q),
                            pt.rearrange("p (h s) -> p h s", h=Q),
                            keepT[0:rows, :].unsqueeze(1).broadcast_to([rows, Q, S]), ALU.mult)
                else:
                    self.copy(PT_sb[0:rows, c, :], pt, lane)
                M[("pt", bank)] = [lane.mark()]
                marks.append(lane.mark())
            M["turn"], M["PT"] = [PE.mark()], marks

        def values(buf, g):
            PE.after(*M["PT"], *self.since("own", V))
            for h in range(Q):
                n = Q * g + h
                if spread:
                    out = self.bank(7, S)[:, h * Q * hd:(h + 1) * Q * hd]
                    vs = [buf["v"][0:r, c, Q * g * hd:Q * (g + 1) * hd] for c, (_, r) in enumerate(chunks)]
                else:
                    out = self.bank(o_banks[n // per_bank], S)[:, (n % per_bank) * hd:(n % per_bank + 1) * hd]
                    vs = [value(buf, n, c) for c in range(len(chunks))]
                self.project(out, [PT_sb[0:r, c, h * S:(h + 1) * S] for c, (_, r) in enumerate(chunks)],
                             vs, h == Q - 1)
            M["values"] = [PE.mark()]
            if spread:
                V.after(PE, *self.since("oread", PE))
                own = self.bank(7, S, 512).rearrange("p (h x) -> p h x", x=hd)
                if Q * (Q + 1) <= 512 // hd:
                    self.copy(o[:, Q * g * hd:Q * (g + 1) * hd].rearrange("p (h d) -> p h d", h=Q),
                              own[:, 0:Q * (Q + 1):Q + 1, :], V)
                else:
                    for h in range(Q):
                        self.copy(o[:, (Q * g + h) * hd:(Q * g + h + 1) * hd], own[:, Q * h + h, :], V)
                M["own"] = [V.mark()]

        def divide(buf, last_exp):
            inv = buf["inv"]
            V.after(*last_exp)
            V.do(nc.vector.reciprocal(inv[:, 0:H], buf["total"][:, 0:H]))
            if share != 1.0:
                V.after(V)
                self.ts(inv[:, 0:H], inv[:, 0:H], share, None, ALU.mult)
            V.after(V, *M["values"], *self.since("oread", PE))
            if spread:
                ov = o.rearrange("p (h d) -> p h d", h=H)
                self.tt(ov, ov, inv[:, 0:H].unsqueeze(2).broadcast_to([S, H, hd]), ALU.mult)
            else:
                each = min(per_bank, H)
                for n in range(0, H, each):
                    ob = self.bank(o_banks[n // per_bank], S, each * hd).rearrange("p (h d) -> p h d", h=each)
                    self.tt(o[:, n * hd:(n + each) * hd].rearrange("p (h d) -> p h d", h=each), ob,
                            inv[:, n:n + each].unsqueeze(2).broadcast_to([S, each, hd]), ALU.mult)
                M["own"] = [V.mark()]
            if plus is not None:
                V.after(V)
                self.tt(o, o, plus(buf), ALU.add)

        def first(buf):
            PE.after(*M["ready"])
            scores(buf, 0)

        M.clear()
        self.row_stats = Region(self.mem, self.small.at, 96)
        for buf in bufs:
            buf["nmax"], buf["total"], buf["inv"] = (self.take_small(16) for _ in range(3))
        for piece in prologue(0, bufs[0]):
            piece()
        M["ready"] = [V.mark(), A.mark(), G.mark()]
        first(bufs[0])
        weigh_group(bufs[0], 0)

        def pair(i):
            M.clear()
            for p in range(2):
                b, buf, other = i * 2 + p, bufs[p], bufs[1 - p]
                pieces = prologue(b + 1, other) + (late(b) if late else [])
                slots = 3 * groups - 1
                each = -(-len(pieces) // slots)

                def side():
                    for _ in range(each):
                        if pieces:
                            pieces.pop(0)()
                            if not pieces:
                                M["ready"] = [V.mark(), A.mark(), G.mark()]
                for g in range(groups):
                    turn(g)
                    side()
                    if g + 1 < groups:
                        scores(buf, g + 1)
                        weigh_group(buf, g + 1)
                        side()
                        values(buf, g)
                        side()
                while pieces:
                    side()
                last_exp = self.since("exp", A)
                values(buf, groups - 1)
                divide(buf, last_exp)
                first(other)
                weigh_group(other, 0)
                epilogue(b, buf)
        self.prog.loop(name, B // 2, pair)

    def out_project(self, o, oT, w):
        tiles = w.shape[1]
        PE, V = self.PE, self.DVE
        PE.after(V)
        for t0 in range(0, tiles, 4):
            n = min(4, tiles - t0)
            src = lambda t: o[:, (t0 + t) * P:(t0 + t + 1) * P]
            self.via_misc(P, n * S,
                          lambda bk: [self.tp(bk[:, t * S:(t + 1) * S], src(t), t == n - 1) for t in range(n)],
                          lambda bk: self.copy(oT[:, t0:t0 + n, :], bk.rearrange("p (t s) -> p t s", t=n), V), V)
        self.marks["oread"] = [PE.mark()]
        PE.after(V)
        self.y_bank = self.next_misc()
        y = self.bank(self.y_bank, S, D)
        self.project(y, [oT[:, t, :] for t in range(tiles)], [w[:, t, :] for t in range(tiles)])
        V.after(PE)
        return y

    def done_y(self):
        self.marks[("misc", self.y_bank)] = [self.DVE.mark()]

    def take_small(self, n):
        return self.row_stats.take(n, parts=S)

    def norm_pieces(self, src, xn, xT, gain=None, shift=None, also=None):
        V, PE = self.DVE, self.PE

        def one():
            V.after(PE)
            self.norm(src, xn)

        def two():
            PE.after(V)

            def evict(bk):
                pt = bk.rearrange("p (k s) -> p k s", k=KD)
                if gain is None:
                    self.copy(xT, pt, V)
                else:
                    for k in range(KD):
                        self.ts(xT[:, k, :], pt[:, k, :], gain[:, k:k + 1], shift[:, k:k + 1], ALU.mult, ALU.add)
                if also is not None:
                    dst, g2, s2 = also
                    for k in range(KD):
                        self.ts(dst[:, k, :], pt[:, k, :], g2[:, k:k + 1], s2[:, k:k + 1], ALU.mult, ALU.add)
            V.after(self.POOL)
            self.via_misc(P, KD * S, lambda bk: [self.tp(bk[:, k * S:(k + 1) * S], xn[:, k * P:(k + 1) * P],
                                                         k == KD - 1) for k in range(KD)], evict, V)
        return [one, two]

    def key_pieces(self, kT, src, w, bias, step=1):
        A, nk = self.ACT, kT.shape[2]

        def piece(t0):
            def fill(bk):
                for t in range(t0, t0 + step):
                    self.project(bk[:, (t - t0) * nk:(t - t0 + 1) * nk],
                                 [w[:, k, t * P:(t + 1) * P] for k in range(len(src))], src, t == t0 + step - 1)

            def evict(bk):
                if bias is None:
                    self.copy(kT[:, t0:t0 + step, :], bk.rearrange("p (t n) -> p t n", t=step), A)
                else:
                    for t in range(t0, t0 + step):
                        self.act(kT[:, t, :], bk[:, (t - t0) * nk:(t - t0 + 1) * nk], ACT.Identity,
                                 bias=bias[:, t:t + 1], scale=1.0)
            self.PE.after(self.DVE)
            self.via_misc(P, step * nk, fill, evict, A)
        return [lambda t0=t0: piece(t0) for t0 in range(0, kT.shape[1], step)]

    def value_pieces(self, v, src, w, bias, chunks):
        V, F = self.DVE, w.shape[2]

        def piece(c, at, rows):
            def evict(bk):
                if bias is None:
                    self.copy(v[0:rows, c, :], bk, V)
                else:
                    self.tt(v[0:rows, c, :], bk, bias[0:rows, :], ALU.add)
            self.via_misc(rows, F, lambda bk: self.project(bk, [s[:, at:at + rows] for s in src],
                                                           [w[:, k, :] for k in range(len(src))]), evict, V)
        return [lambda c=c, a=a, r=r: piece(c, a, r) for c, (a, r) in enumerate(chunks)]

    def query_pieces(self, q, qm, src, w, bias, scale, rows):
        PE, V, G = self.PE, self.DVE, self.POOL
        tiles = w.shape[2] // P

        def one():
            PE.after(V)

            def fill(bk):
                for t in range(tiles):
                    self.project(bk[:, t * S:(t + 1) * S], [w[:, k, t * P:(t + 1) * P] for k in range(KD)],
                                 [src[:, k, :] for k in range(KD)], t == tiles - 1)

            def evict(bk):
                ps = bk.rearrange("p (t s) -> p t s", t=tiles)
                if bias is None:
                    self.ts(q, ps, scale, None, ALU.mult)
                else:
                    self.stt(q, ps, scale, bias.unsqueeze(2).broadcast_to([P, tiles, S]), ALU.mult, ALU.add)
            V.after(G)
            self.via_misc(P, tiles * S, fill, evict, V)

        def two():
            per = rows.shape[1]
            G.after(V, PE)
            for t in range(tiles):
                self.tt(qm[:, t * per:(t + 1) * per, :], q[:, t, :].unsqueeze(1).broadcast_to([P, per, S]),
                        rows.unsqueeze(2).broadcast_to([P, per, S]), ALU.mult, G)
        return [one] if qm is None else [one, two]

    def context_piece(self, b, ctx, which="ctxT"):
        return [lambda: self.load_context(b, ctx, which)]

    CHUNKS = [(c * CR, CR) for c in range(CC)]

    def await_context(self):
        for e in (self.PE, self.ACT, self.DVE):
            e.after(self.CTX)

    def start(self):
        SP, nc = self.SP, self.nc
        self.load_x = Lane(self.prog, "x_landed", nc.sync, 16)
        self.load_x.do(nc.sync.dma_start(self.x[:, 0:B, :], self.ins["x"]))
        c = self.load("consts", self.small)
        self.ident, self.causal, self.upperT, self.spread = c["ident"], c["causal"], c["upperT"], c["spread"]
        self.rows16, self.rows32, self.prefix = c["rows16"], c["rows32"], c["prefix"]
        self.ones, self.turn8 = c["ones"], c["turn8"]
        self.rows64 = c["rows64"]
        self.row_stats = None
        first_done = self.small.take(32, parts=S)
        self.POOL.do(nc.gpsimd.memset(self.minus_half, -0.5))
        self.POOL.do(nc.gpsimd.memset(self.x[:, B, :], 0.0))
        for lane in self.compute:
            lane.after(self.load_x, self.landed["consts"], self.POOL)
        self.tp(self.bank(0, P, P), self.ident)
        self.copy(first_done[:, 0:16], self.ident[0:S, 0:16], self.ACT)
        self.copy(first_done[:, 16:32], self.ident[0:S, 0:16], self.DVE)

    def l0_attn(self):
        nc, PE, A, V, G = self.nc, self.PE, self.ACT, self.DVE, self.POOL
        GT = 8
        w = self.load("l0a", self.A)
        after_pack = self.A.at
        whh = self.A.take(3, 2, KD, GT * P, dt=BF16)
        raw = self.load("l0a_whh", self.A)["whh"]
        bias = self.load("l0a_bias", self.biases)
        x, xnT = self.x, self.xnT
        xW = Region(self.mem, self.Bm.start, 15360).take(2, S, GT, B)
        wk = self.work.rest()
        hs = wk.take(2, KD, B + 1, S)
        G.do(nc.gpsimd.memset(hs[:, :, :, B, :], 0.0))
        G.do(nc.gpsimd.memset(xnT[:, :, B, :], 0.0))
        xn = wk.take(D, parts=S)

        def norm_batch(b):
            self.norm(x[:, b, :], xn)
            V.after(V)
            self.turn_features(xn, xnT[:, :, b, :], 0)
        self.prog.loop("l0_norm", B, norm_batch)

        self.need("l0a_whh", V, A, G)
        for l in range(2):
            self.copy(whh[:, 0, l], raw[:, l], A)
            G.after(A)
            self.tt(raw[:, l], raw[:, l], whh[:, 0, l], ALU.subtract, G)
            A.after(G)
            self.copy(whh[:, 1, l], raw[:, l], A)
            G.after(A, G)
            self.tt(whh[:, 2, l], raw[:, l], whh[:, 1, l], ALU.subtract, G)
        self.need("l0a", PE, V)
        self.need("l0a_bias", PE, A, V)

        PE.after(V)
        def input_gates(half):
            free = [None] * 4
            for n in range(2 * GT):
                l, g = divmod(n, GT)
                ps = self.bank(n % 4, P, HT)
                if free[n % 4]:
                    PE.after(free[n % 4])
                else:
                    PE.after(A, V)
                self.project(ps, [w["wih"][:, l, k, g * P:(g + 1) * P] for k in range(KD)],
                             [xnT[:, k, bass.ds(half * HALF, HALF), :] for k in range(KD)])
                dst = xW[:, l, :, g, bass.ds(half * HALF, HALF)].rearrange("p t b -> p b t")
                src = ps.rearrange("p (b t) -> p b t", b=HALF)
                lane = A if n % 2 else V
                lane.after(PE)
                if lane is A:
                    self.act(dst, src, ACT.Identity, bias=bias["b_lstm"][:, n:n + 1], scale=1.0)
                else:
                    self.ts(dst, src, bias["b_lstm"][:, n:n + 1], None, ALU.add)
                free[n % 4] = lane.mark()
        self.prog.loop("l0_input", 2, input_gates)

        gates = wk.take(2, GT, B)
        cell = wk.take(2, KD, B)
        prod = wk.take(2, 2, KD, B)
        tc = wk.take(2, KD, B)
        h = wk.take(2, KD, B)
        left = wk.take(2, KD, B)
        hp = wk.take(2, 2, 3, KD, B, dt=BF16)
        V.do(nc.vector.memset(cell, 0.0))
        V.do(nc.vector.memset(hp, 0.0))
        UN = 8
        V.after(A, V, G)
        PE.after(A, V, G)
        G.after(V)

        def steps(i):
            hmark = [V.mark(), V.mark()]
            pmark = [G.mark(), G.mark()]
            for u in range(UN):
                t = i * UN + u
                new, old = (u + 1) % 2, u % 2
                for l in range(2):
                    ps = self.bank(l, P, 3 * GT * B).rearrange("p (s g b) -> p s g b", s=3, g=GT)
                    PE.after(hmark[l])
                    for g in range(GT):
                        for k in range(KD):
                            for part in range(3):
                                ins = nc.tensor.matmul(
                                    ps[:, part:3, g, :], whh[:, part, l, k, g * P:(g + 1) * P],
                                    hp[:, old, l, 0:3 - part, k, :],
                                    start=(g == 0 and k == 0 and part == 0), stop=(k == KD - 1 and part == 2),
                                    skip_group_check=True)
                    PE.do(ins)
                    V.after(PE)
                    V.do(nc.vector.tensor_reduce(gates[:, l].rearrange("p g b -> p (g b)"),
                                                 ps.rearrange("p s g b -> p (g b) s"), AX, ALU.add))
                    V.after(V)
                    self.tt(gates[:, l], gates[:, l],
                            xW[:, l, bass.ds(t, 1), :, :].rearrange("p o g b -> p (o g) b"), ALU.add)
                    A.after(V)
                    self.act(gates[:, l, 0:6, :], gates[:, l, 0:6, :], ACT.Sigmoid)
                    m_sig = A.mark()
                    self.act(gates[:, l, 6:8, :], gates[:, l, 6:8, :], ACT.Tanh)
                    m_tanh = A.mark()
                    V.after(m_sig, V)
                    self.tt(prod[:, l, 0], gates[:, l, 2:4, :], cell[:, l], ALU.mult)
                    V.after(m_tanh)
                    self.tt(prod[:, l, 1], gates[:, l, 0:2, :], gates[:, l, 6:8, :], ALU.mult)
                    V.after(V)
                    self.tt(cell[:, l], prod[:, l, 0], prod[:, l, 1], ALU.add)
                    A.after(V)
                    self.act(tc[:, l], cell[:, l], ACT.Tanh)
                    V.after(A, pmark[l])
                    self.tt(hp[:, new, l, 0], gates[:, l, 4:6, :], tc[:, l], ALU.mult)
                    self.tt(h[:, l], gates[:, l, 4:6, :], tc[:, l], ALU.mult)
                    V.after(V)
                    self.tt(hp[:, new, l, 1], h[:, l], hp[:, new, l, 0], ALU.subtract)
                    self.tt(left[:, l], h[:, l], hp[:, new, l, 0], ALU.subtract)
                    V.after(V)
                    self.tt(hp[:, new, l, 2], left[:, l], hp[:, new, l, 1], ALU.subtract)
                    hmark[l] = V.mark()
                    G.after(hmark[l])
                    self.copy(hs[:, l, :, 0:B, bass.ds(t, 1)].rearrange("p k b o -> p k (b o)"), h[:, l], G)
                    pmark[l] = G.mark()
        self.prog.loop("l0_lstm", S // UN, steps)
        self.fetch_l0_l1()

        take = self.buffers(Region(self.mem, self.Bm.start, 5000), Region(self.mem, after_pack, self.A.start + 22528 - after_pack))
        xb, r1 = take(KD, S), take(2, S, parts=64)
        o, oT, P_sb, PT_sb = take(4 * D, parts=S), take(8, S), take(4, S, parts=S), take(1, 4 * S)
        q_mask, bq2m = take(2), take(2, 8)
        bufs = [dict(qm=take(8, 2, S), kT=take(4, S), v=take(D, parts=S)) for _ in range(2)]
        self.settle()
        self.ts(q_mask, self.rows64, 0.125, None, ALU.mult)
        V.after(V)
        for m in range(2):
            self.ts(bq2m[:, m, :], bias["bq2"], q_mask[:, m:m + 1], None, ALU.mult)

        def prologue(b, u):
            def hidden(l, w1, b1):
                def evict(bk):
                    self.ts(r1[:, l, :], bk, bias[b1][0:64, :], 0.0, ALU.add, ALU.max)
                self.via_misc(64, S, lambda bk: self.project(bk, [w[w1][:, k, :] for k in range(KD)],
                                                             [hs[:, l, k, b, :] for k in range(KD)]), evict, V)

            def queries(half):
                PE.after(V)

                def fill(bk):
                    for t in range(4):
                        c = 4 * half + t
                        self.mm(bk[:, t * S:(t + 1) * S], w["wq2"][0:64, c * P:(c + 1) * P], r1[:, 0, :], count=t == 3)

                def evict(bk):
                    ps = bk.rearrange("p (t s) -> p t s", t=4)
                    for m in range(2):
                        self.stt(u["qm"][:, 4 * half:4 * half + 4, m, :], ps, q_mask[:, m:m + 1],
                                 bq2m[:, m, 4 * half:4 * half + 4].unsqueeze(2).broadcast_to([P, 4, S]),
                                 ALU.mult, ALU.add)
                self.via_misc(P, 4 * S, fill, evict, V)

            def keys():
                PE.after(V)

                def fill(bk):
                    for t in range(4):
                        self.mm(bk[:, t * S:(t + 1) * S], w["wk2"][0:64, t * P:(t + 1) * P], r1[:, 1, :], count=t == 3)
                self.via_misc(P, 4 * S, fill, lambda bk: self.tt(
                    u["kT"], bk.rearrange("p (t s) -> p t s", t=4),
                    bias["bk2"].unsqueeze(2).broadcast_to([P, 4, S]), ALU.add), V)

            def stage():
                G.after(PE)
                self.copy(xb, xnT[:, :, b, :], G)
                PE.after(G)
            return ([lambda: hidden(0, "wq1", "bq1"), lambda: hidden(1, "wk1", "bk1"), stage,
                     lambda: queries(0), lambda: queries(1), keys]
                    + self.value_pieces(u["v"].unsqueeze(1), [xb[:, k, :] for k in range(KD)], w["wv"], bias["bv"],
                                        [(0, S)]))

        def epilogue(b, u):
            y = self.out_project(o, oT, w["wo"])
            V.after(V)
            self.tt(x[:, b, :], x[:, b, :], y, ALU.add)
            self.done_y()
        self.attend_all("l0_attn", 16, S, 64, bufs, lambda u, n: [(u["qm"][:, n // 2, n % 2, :], u["kT"][:, n // 4, :])],
                        lambda u, n, c: u["v"][:, 64 * (n // 4):64 * (n // 4) + 64], prologue, epilogue,
                        o=o, P_sb=P_sb, PT_sb=PT_sb, mask=self.causal, o_banks=(6, 7))
        self.fetch_l1_l2()

    def fetch_l0_l1(self):
        upper = Region(self.mem, self.Bm.start + 5000, 15360 - 5000)
        for pack in ("l0x", "l0f", "l1a"):
            self.packs[pack] = self.load(pack, upper, self.compute)

    def fetch_l1_l2(self):
        a = Region(self.mem, self.a_start, 22528)
        for pack in ("l1x", "l1f", "l2a"):
            self.packs[pack] = self.load(pack, a, self.compute)
        self.extra = a.rest()
        self.extra_b = Region(self.mem, self.Bm.start, 5000)

    def settle(self):
        for lane in self.compute:
            lane.after(*self.compute, self.CTX)

    def buffers(self, *regions):
        regions = [r.rest() for r in regions]

        def take(*dims, dt=F32, parts=P):
            n = int(np.prod(dims))
            n = n if dt is not BF16 else (n + 1) // 2
            for r in regions:
                if r.at + n <= r.end:
                    return r.take(*dims, dt=dt, parts=parts)
            raise AssertionError(("no room for", dims))
        return take

    def load_context(self, i, dst, which="ctxT"):
        src = self.ins[which][i] if isinstance(i, int) else \
            self.ins[which][bass.ds(i, 1)].rearrange("o p n -> (o p) n")
        self.SP.after(*(self.compute if isinstance(i, int) else (self.DVE,)))
        self.CTX.do(self.nc.sync.dma_start(dst, src))

    def l0_xattn(self):
        V = self.DVE
        self.settle()
        w, x = self.packs["l0x"], self.x
        take = self.buffers(self.work, self.extra, self.extra_b)
        xn, xT, ctx = take(D, parts=S), take(KD, S), take(CK)
        P_sb, PT_sb, o = take(1, CK, parts=S), take(CC, S), take(D, parts=S)
        bufs = [dict(q=take(KD, S), kT=take(KD, CK), v=take(CC, D)) for _ in range(2)]
        self.load_context(0, ctx)
        self.need("l0x", self.PE, V, self.ACT)

        def prologue(b, u):
            return ([self.await_context] + self.norm_pieces(x[:, b, :], xn, xT)
                    + self.key_pieces(u["kT"], [ctx], w["wk"], w["bk"])
                    + self.value_pieces(u["v"], [ctx], w["wv"], w["bv"], self.CHUNKS)
                    + self.context_piece(b + 1, ctx)
                    + self.query_pieces(u["q"], None, xT, w["wq"], w["bq"], 1.0, None))

        def epilogue(b, u):
            V.after(V)
            self.tt(x[:, b, :], x[:, b, :], o, ALU.add)
        self.attend_all("l0_xattn", 1, CK, D, bufs,
                        lambda u, n: [(u["q"][:, k, :], u["kT"][:, k, :]) for k in range(KD)],
                        lambda u, n, c: u["v"][0:CR, c, :], prologue, epilogue, o=o, P_sb=P_sb, PT_sb=PT_sb)

    def cross(self, name, pack, hd, scale, rows):
        PE, A, V = self.PE, self.ACT, self.DVE
        self.settle()
        w, x = self.packs[pack], self.x
        H, per = D // hd, P // hd
        take = self.buffers(self.work, self.extra, self.extra_b)
        xn, xT, ctx, q = take(D, parts=S), take(KD, S), take(CK), take(KD, S)
        P_sb, PT_sb, o = take(4, CK, parts=S), take(CC, 4 * S), take(D, parts=S)
        oT, y_sb = take(KD, S), take(D, parts=S)
        bufs = [dict(qm=take(H, S), kT=take(KD, CK), v=take(CC, D)) for _ in range(2)]
        self.load_context(0, ctx)
        self.need(pack, PE, V, A)
        bq = w.get("bq")
        if bq is not None:
            bqs = take(KD)
            self.ts(bqs, bq, scale, None, ALU.mult)
            bq = bqs

        def prologue(b, u):
            return ([self.await_context] + self.norm_pieces(x[:, b, :], xn, xT)
                    + self.key_pieces(u["kT"], [ctx], w["wk"], w.get("bk"))
                    + self.value_pieces(u["v"], [ctx], w["wv"], w.get("bv"), self.CHUNKS)
                    + self.context_piece(b + 1, ctx)
                    + self.query_pieces(q, u["qm"], xT, w["wq"], bq, scale, rows))

        def epilogue(b, u):
            y = self.out_project(o, oT, w["wo"])
            if "bo" in w:
                V.after(V)
                self.tt(y_sb, y, w["bo"][0:S, :], ALU.add)
                self.done_y()
                y = y_sb
            V.after(V)
            self.tt(x[:, b, :], x[:, b, :], y, ALU.add)
            if y is not y_sb:
                self.done_y()
        self.attend_all(name, H, CK, hd, bufs, lambda u, n: [(u["qm"][:, n, :], u["kT"][:, n // per, :])],
                        None, prologue, epilogue, o=o, P_sb=P_sb, PT_sb=PT_sb, spread=True)

    def l1_attn(self):
        PE, A, V = self.PE, self.ACT, self.DVE
        self.settle()
        w, x, H, hd = self.packs["l1a"], self.x, 16, 16
        take = self.buffers(self.work, self.extra, self.extra_b)
        xn, xT, q = take(D, parts=S), take(KD, S), take(KD, S)
        P_sb, PT_sb, o, oT = take(4, S, parts=S), take(1, 4 * S), take(D, parts=S), take(KD, S)
        bqs, y_sb = take(KD), take(D, parts=S)
        bufs = [dict(qm=take(H, S), kT=take(KD, S), v=take(1, D, parts=S), near=take(D, parts=S)) for _ in range(2)]
        self.need("l1a", PE, V, A)
        self.ts(bqs, w["bq"], 0.25, None, ALU.mult)

        def prologue(b, u):
            src = [xT[:, k, :] for k in range(KD)]

            def near():
                PE.after(V)
                self.via_misc(S, D, lambda bk: self.mm(bk, self.spread[0:S, :], u["v"][:, 0, :], count=True),
                              lambda bk: self.copy(u["near"], bk, V), V)
            return (self.norm_pieces(x[:, b, :], xn, xT) + self.key_pieces(u["kT"], src, w["wk"], w["bk"], 2)
                    + self.query_pieces(q, u["qm"], xT, w["wq"], bqs, 0.25, self.rows16)
                    + self.value_pieces(u["v"], src, w["wv"], w["bv"], [(0, S)]) + [near])

        def epilogue(b, u):
            y = self.out_project(o, oT, w["wo"])
            V.after(V)
            self.tt(y_sb, y, w["bo"][0:S, :], ALU.add)
            self.done_y()
            V.after(V)
            self.tt(x[:, b, :], x[:, b, :], y_sb, ALU.add)
        self.attend_all("l1_attn", H, S, hd, bufs, lambda u, n: [(u["qm"][:, n, :], u["kT"][:, n // 8, :])],
                        None, prologue, epilogue, o=o, P_sb=P_sb, PT_sb=PT_sb, spread=True,
                        share=0.6, plus=lambda u: u["near"])

    def l1_xattn(self):
        self.cross("l1_xattn", "l1x", 16, 0.25, self.rows16)

    def l3_xattn(self):
        self.cross("l3_xattn", "l3x", 16, 0.25, self.rows16)

    def norm_half(self, half, src, xn2, xT, gain=None, shift=None):
        V = self.DVE
        for j in range(HALF):
            self.norm(src[:, bass.ds(half * HALF + j, 1), :].rearrange("p o d -> p (o d)"), xn2)
            V.after(V)
            self.turn_features(xn2, xT[:, :, j, :], j % 2, gain, shift)

    def tile_stream(self, n, banks, fill, drain, free):
        PE = self.PE
        for u in range(n):
            bk = banks[u % len(banks)]
            if bk in free:
                PE.after(*free[bk])
            fill(u, bk)
            free[bk] = drain(u, bk)

    def gated(self, tiles, xT, wg, wu, h, g_sb, free, scales=None):
        PE, A, V = self.PE, self.ACT, self.DVE
        flat = [xT[:, k].rearrange("p b s -> p (b s)") for k in range(KD)]

        def fill(u, bk):
            for o, wt in ((0, wg), (1, wu)):
                self.project(self.bank(bk + o, P, HT), [wt[:, k, u * P:(u + 1) * P] for k in range(KD)], flat)

        def drain(u, bk):
            A.after(PE, V)
            sg = {} if scales is None else dict(scale=scales[0][:, u:u + 1])
            self.act(g_sb[:, u % 2, :], self.bank(bk, P, HT), ACT.Silu, **sg)
            V.after(A, PE)
            if scales is None:
                self.tt(h[:, u, :], g_sb[:, u % 2, :], self.bank(bk + 1, P, HT), ALU.mult)
            else:
                self.stt(h[:, u, :], self.bank(bk + 1, P, HT), scales[1][:, u:u + 1], g_sb[:, u % 2, :],
                         ALU.mult, ALU.mult)
            return (A.mark(), V.mark())
        self.tile_stream(tiles, (0, 2, 4), fill, drain, free)

    def down(self, half, h, w, free, finish):
        PE, V = self.PE, self.DVE
        PE.after(V)
        tiles = w.shape[1]

        def fill(j, bk):
            self.project(self.bank(bk, S, D), [h[:, t, j * S:(j + 1) * S] for t in range(tiles)],
                         [w[:, t, :] for t in range(tiles)])

        def drain(j, bk):
            V.after(PE)
            finish(j, bass.ds(half * HALF + j, 1), self.bank(bk, S, D))
            return (V.mark(),)
        self.tile_stream(HALF, (6, 7), fill, drain, free)

    def xs(self, a, at):
        return a[:, at, :].rearrange("p o d -> p (o d)")

    def l0_ffn(self):
        PE, A, V, G = self.PE, self.ACT, self.DVE, self.POOL
        self.settle()
        wi, x = self.packs["l0f"], self.x
        take = self.buffers(self.work, self.extra, self.extra_b)
        xn, xT = take(D, parts=S), take(KD, HALF, S)
        h, g_sb = take(6, HT), take(2, HT)
        self.need("l0f", A, V, G)
        w = {}
        for name, lane in (("wg", A), ("wu", V), ("wd", G)):
            w[name] = wi[name].bitcast(F32)
            if lane is A:
                self.act(w[name], wi[name], ACT.Copy, scale=1.0 / 127.0)
            else:
                self.ts(w[name], wi[name], 1.0 / 127.0, None, ALU.mult, lane=lane)
        PE.after(A, V, G)

        def half_turn(i):
            free = {}
            PE.after(V, A)
            self.norm_half(i, x, xn, xT)
            PE.after(V)
            self.gated(6, xT, w["wg"], w["wu"], h, g_sb, free)
            self.down(i, h, w["wd"], free,
                      lambda j, at, y: self.tt(self.xs(x, at), self.xs(x, at), y, ALU.add))
        self.prog.loop("l0_ffn", 2, half_turn)

    def l1_ffn(self):
        nc, PE, A, V, G = self.nc, self.PE, self.ACT, self.DVE, self.POOL
        self.settle()
        self.fetch_l2x()
        w, x, xnT = self.packs["l1f"], self.x, self.xnT
        E, TOP, CAP = 8, 4, 140
        take = self.buffers(self.work, self.extra)
        xn, logits = take(D, parts=S), take(B, E + 1, parts=S)
        free = {}
        self.need("l1f", PE)

        def norm_batch(b):
            PE.after(V)
            self.norm(x[:, b, :], xn)
            V.after(V)
            xb = xb_buf
            self.turn_features(xn, xb, 0)
            PE.after(V)
            self.project(self.bank(1, S, E + 1), [xb[:, k, :] for k in range(KD)],
                         [w["router"][:, k, :] for k in range(KD)])
            V.after(PE, G)
            self.copy(logits[:, b, :], self.bank(1, S, E + 1), V)
            G.after(V)
            self.copy(xnT[:, :, b, :], xb, G)
        xb_buf = take(KD, S)
        self.prog.loop("l1_router", B, norm_batch)

        e3 = lambda: take(B, E, parts=S)
        e1 = lambda: take(B, parts=S)
        wide = lambda a: a.unsqueeze(2).broadcast_to([S, B, E])
        s, rest, t1, t2, t3, pick, rw = logits[:, :, 0:E], e3(), e3(), e3(), e3(), e3(), e3()
        size, prob, cum, a1, first, total = e3(), e1(), e1(), e1(), e1(), e1()
        turn, weight = self.turn8[0:S, :].unsqueeze(1).broadcast_to([S, B, E]), take(B, E + 1, parts=S)

        def do(f, *a, **k):
            V.after(V)
            f(*a, **k)

        def red(out, a, op):
            V.after(V)
            V.do(nc.vector.tensor_reduce(out, a, AX, op))

        def exp(out, a):
            A.after(V)
            self.act(out, a, ACT.Exp)
            V.after(A)
        do(self.copy, rest, s, V)
        do(self.ts, rw, s, 0.0, None, ALU.mult)
        do(self.ts, t1, s, -1.0, None, ALU.mult)
        do(self.tt, size, s, t1, ALU.max)
        for r in range(TOP):
            red(a1, rest, ALU.max)
            if r == 0:
                do(self.copy, first, a1, V)
                do(self.tt, t1, s, wide(first), ALU.subtract)
                exp(t1, t1)
                red(total, t1, ALU.add)
                do(lambda: V.do(nc.vector.reciprocal(total, total)))
            do(self.tt, t1, rest, wide(a1), ALU.is_equal)
            do(self.tt, t1, t1, turn, ALU.mult)
            red(prob, t1, ALU.max)
            do(self.tt, pick, t1, wide(prob), ALU.is_equal)
            do(self.ts, prob, a1, -1.0, None, ALU.mult)
            do(self.tt, prob, prob, a1, ALU.max)
            do(self.tt, t1, size, wide(prob), ALU.max)
            do(self.ts, t1, t1, 0.2, None, ALU.mult)
            do(self.tt, t2, wide(a1), s, ALU.subtract)
            do(self.tt, t2, t2, t1, ALU.is_le)
            do(self.tt, t3, rest, wide(a1), ALU.subtract)
            exp(t3, t3)
            do(self.tt, t3, t3, t2, ALU.mult)
            red(prob, t3, ALU.add)
            do(lambda: V.do(nc.vector.reciprocal(prob, prob)))
            if r:
                do(self.ts, t1[:, :, 0], cum, 0.75, None, ALU.is_lt)
                do(self.tt, prob, prob, t1[:, :, 0], ALU.mult)
            do(self.tt, t1, pick, wide(prob), ALU.mult)
            do(self.tt, rw, rw, t1, ALU.add)
            if r < TOP - 1:
                do(self.ts, t1, pick, MASKED, None, ALU.mult)
                do(self.tt, rest, rest, t1, ALU.add)
                do(self.tt, a1, a1, first, ALU.subtract)
                exp(a1, a1)
                do(self.tt, a1, a1, total, ALU.mult)
                if r:
                    do(self.tt, cum, cum, a1, ALU.add)
                else:
                    do(self.copy, cum, a1, V)
        red(a1, rw, ALU.add)
        do(lambda: V.do(nc.vector.reciprocal(a1, a1)))
        do(self.tt, rw, rw, wide(a1), ALU.mult)
        do(self.ts, t1, rw, 0.0, None, ALU.is_gt)
        PE.after(V)
        flat = t1.rearrange("p b e -> p (b e)")
        self.mm(self.bank(2, S, B * E), self.prefix[0:S, :], flat)
        self.mm(self.bank(3, S, B * E), self.ones[0:S, 0:S], flat, count=True)
        V.after(PE)
        do(self.copy, t2.rearrange("p b e -> p (b e)"), self.bank(2, S, B * E), V)
        do(self.copy, t3.rearrange("p b e -> p (b e)"), self.bank(3, S, B * E), V)
        for b in range(1, B):
            do(self.tt, t2[:, b, :], t2[:, b, :], t3[:, b - 1, :], ALU.add)
            if b < B - 1:
                do(self.tt, t3[:, b, :], t3[:, b, :], t3[:, b - 1, :], ALU.add)
        do(self.ts, t2, t2, float(CAP), None, ALU.is_le)
        do(self.tt, t1, t1, t2, ALU.mult)
        do(self.ts, weight[:, :, 0:E], t1, -1.0, -MASKED, ALU.add, ALU.mult)
        do(self.tt, weight[:, :, 0:E], weight[:, :, 0:E], s, ALU.add)
        do(self.copy, weight[:, :, E:E + 1], logits[:, :, E:E + 1], V)
        red(a1, weight, ALU.max)
        w9 = lambda a: a.unsqueeze(2).broadcast_to([S, B, E + 1])
        do(self.tt, weight, weight, w9(a1), ALU.subtract)
        exp(weight, weight)
        red(a1, weight, ALU.add)
        do(lambda: V.do(nc.vector.reciprocal(a1, a1)))
        do(self.tt, weight, weight, w9(a1), ALU.mult)
        red(a1, weight[:, :, 0:E], ALU.add)
        do(self.tt, rw, rw, wide(a1), ALU.mult)
        do(self.tt, weight[:, :, 0:E], rw, t1, ALU.mult)

        h, g_sb, wt = take(4, HT), take(2, HT), take(HALF, E + 1, parts=S)
        self.settle()

        def experts(i):
            free = {}
            V.after(V)
            self.copy(wt, weight[:, bass.ds(i * HALF, HALF), :], V)
            flat = [xnT[:, k, bass.ds(i * HALF, HALF), :].rearrange("p b s -> p (b s)") for k in range(KD)]
            PE.after(V, A)

            def unit(u, bk):
                wg, wu, c = (w["dg"], w["du"], u) if u < E else (w["sg"], w["su"], u - E)
                for o, ww in ((0, wg), (1, wu)):
                    self.project(self.bank(bk + o, P, HT), [ww[:, k, c * P:(c + 1) * P] for k in range(KD)], flat)

            def activate(u, bk):
                slot = u % 4
                A.after(PE, V)
                self.act(g_sb[:, u % 2, :], self.bank(bk, P, HT), ACT.Silu)
                V.after(A, PE)
                self.tt(h[:, slot, :], g_sb[:, u % 2, :], self.bank(bk + 1, P, HT), ALU.mult)
                return (A.mark(), V.mark())

            def give(e):
                tiles = [e % 4] if e < E else [0, 1, 2, 3]
                dd = [w["dd"][:, e, :]] if e < E else [w["sd"][:, t, :] for t in range(4)]

                def fill(j, bk):
                    self.project(self.bank(bk, S, D), [h[:, t, j * S:(j + 1) * S] for t in tiles], dd)

                def drain(j, bk):
                    V.after(PE, V)
                    xb = self.xs(x, bass.ds(i * HALF + j, 1))
                    self.stt(xb, self.bank(bk, S, D), wt[:, j, e:e + 1], xb, ALU.mult, ALU.add)
                    return (V.mark(),)
                self.tile_stream(HALF, (6, 7), fill, drain, free)
            ready = {}
            for u in range(E + 4 + 1):
                if u < E + 4:
                    self.tile_stream(1, ((0, 2, 4)[u % 3],), lambda _, bk: unit(u, bk),
                                     lambda _, bk: activate(u, bk), free)
                    ready[u] = V.mark()
                if 1 <= u <= E:
                    PE.after(ready[u - 1])
                    give(u - 1)
            PE.after(V)
            give(E)
        self.prog.loop("l1_experts", 2, experts)

    def fetch_l2x(self):
        self.packs["l2x"] = self.load("l2x", Region(self.mem, self.Bm.start, 15360), self.compute)

    def l2_attn(self):
        PE, A, V, G = self.PE, self.ACT, self.DVE, self.POOL
        self.settle()
        w, x, H, KV = self.packs["l2a"], self.x, 8, 4
        take = self.buffers(self.work, self.extra)
        xn, xT, o, oT = take(D, parts=S), take(KD, S), take(H * P, parts=S), take(H, S)
        P_sb, PT_sb, tmp = take(4, S, parts=S), take(1, 4 * S), take(2, 4, S)
        bufs = [dict(q=take(H, S), kT=take(KV, S), v=take(1, KV * P, parts=S)) for _ in range(2)]
        self.need("l2a", PE)
        self.SP.after(*self.compute)
        rb = Region(self.mem, self.biases.start, 2700)
        rope = self.load("rope", rb)
        self.need("rope", V)

        cs = lambda n: rope[n].unsqueeze(1).broadcast_to([P, 4, S])

        def prologue(b, u):
            def rotary(wa, wb, c0, dst, cos, sin, slot):
                def fill(ww):
                    def f(bk):
                        for h in range(4):
                            c = c0 + h
                            self.project(bk[:, h * S:(h + 1) * S], [ww[:, k, c * P:(c + 1) * P] for k in range(KD)],
                                         [xT[:, k, :] for k in range(KD)], h == 3)
                    return f

                def drain(out, factor):
                    return lambda bk: self.tt(out, bk.rearrange("p (h s) -> p h s", h=4), cs(factor), ALU.mult)
                V.after(G)
                self.via_misc(P, 4 * S, fill(w[wa]), drain(dst, cos), V)
                self.via_misc(P, 4 * S, fill(w[wb]), drain(tmp[:, slot], sin), V)
                G.after(V)
                self.tt(dst, dst, tmp[:, slot], ALU.add, G)
            return (self.norm_pieces(x[:, b, :], xn, xT) + [lambda: PE.after(V)]
                    + [lambda: rotary("wk", "wks", 0, u["kT"], "cos", "sin", 0),
                       lambda: rotary("wq", "wqs", 0, u["q"][:, 0:4], "cosq", "sinq", 1),
                       lambda: rotary("wq", "wqs", 4, u["q"][:, 4:8], "cosq", "sinq", 0)]
                    + self.value_pieces(u["v"], [xT[:, k, :] for k in range(KD)], w["wv"], None, [(0, S)]))

        def epilogue(b, u):
            y = self.out_project(o, oT, w["wo"])
            self.tt(x[:, b, :], x[:, b, :], y, ALU.add)
            self.done_y()
        self.attend_all("l2_attn", H, S, P, bufs, lambda u, n: [(u["q"][:, n, :], u["kT"][:, n // 2, :])],
                        lambda u, n, c: u["v"][:, 0, P * (n // 2):P * (n // 2) + P], prologue, epilogue,
                        o=o, P_sb=P_sb, PT_sb=PT_sb, mask=self.causal, o_banks=(6, 7))
        self.fetch_l2f()

    def fetch_l2f(self):
        a = Region(self.mem, self.a_start, 22528)
        self.packs["l2f"] = self.load("l2f", a, self.compute)
        self.a_hi = a.rest()

    def fetch_l2f_rest(self):
        self.packs["l2f2"] = self.load("l2f2", Region(self.mem, self.a_hi.start, 8192), self.compute)

    def fetch_l3(self):
        b = Region(self.mem, self.Bm.start, 15360)
        for pack in ("l3a", "l3x", "l3f"):
            self.packs[pack] = self.load(pack, b, self.compute)
        self.b_hi = b.rest()
        self.extra = self.extra_b = Region(self.mem, self.a_start, 22528)

    def l2_xattn(self):
        PE, A, V, G = self.PE, self.ACT, self.DVE, self.POOL
        self.settle()
        w, x, xnT = self.packs["l2x"], self.x, self.xnT
        H, hd, HT4 = 16, 32, 4
        scale = float(np.float32(hd) ** np.float32(-0.5))
        c = self.load("l2x_rows", Region(self.mem, self.biases.start, 2700), self.compute)
        take = self.buffers(self.work, self.a_hi)
        acc = take(B + 1, D, parts=S)
        V.do(self.nc.vector.memset(acc[:, B, :], 0.0))
        xn, xT, yT, xo = take(D, parts=S), take(KD, S), take(KD, S), take(D, parts=S)
        q, o, oT = take(HT4, S), take(512, parts=S), take(HT4, S)
        P_sb, PT_sb = take(4, S, parts=S), take(1, 4 * S)
        bufs = [dict(xm=take(D, parts=S), qm=take(H, S), kT=take(HT4, S), v=take(1, 512, parts=S)) for _ in range(2)]
        self.need("l2x", PE, V, A)
        self.need("l2x_rows", V, A)
        row = lambda n: c["rows"][0:S, n, :]
        f = c["cols"]

        def col(n, k=KD):
            return f[:, n:n + k]

        def affine(a, g, b):
            self.tt(a, a, row(g), ALU.mult)
            V.after(V)
            self.tt(a, a, row(b), ALU.add)
            V.after(V)

        def close(b, y, base, lib):
            V.after(V)
            self.tt(xo, y, row(lib), ALU.add)
            self.done_y()
            V.after(V)
            self.tt(xo, xo, base, ALU.add)
            V.after(V)
            self.tt(acc[:, b, :], xo, base, ALU.add)

        def late(b, ln3):
            return self.norm_pieces(xo, xl, xnT[:, :, b, :], col(ln3), col(ln3 + 2))

        def settle_late(ln3):
            for piece in late(B, ln3):
                piece()

        def prologue1(b, u):
            def enter():
                V.after(PE)
                self.norm(x[:, b, :], u["xm"])
                V.after(V)
                affine(u["xm"], 0, 1)
            src = [yT[:, k, :] for k in range(KD)]
            return ([enter] + self.norm_pieces(u["xm"], xn, xT, col(0), col(2), (yT, col(4), col(6)))
                    + self.query_pieces(q, u["qm"], xT, w["a1_wq"], None, scale, self.rows32)
                    + self.key_pieces(u["kT"], src, w["a1_wk"], None, 4)
                    + self.value_pieces(u["v"], src, w["a1_wv"], None, [(0, S)]))
        xl = take(D, parts=S)
        V.do(self.nc.vector.memset(xo, 0.0))
        self.attend_all("l2_block1", H, S, hd, bufs, lambda u, n: [(u["qm"][:, n, :], u["kT"][:, n // 4, :])],
                        None, prologue1,
                        lambda b, u: close(b, self.out_project(o, oT, w["a1_li1"]), u["xm"], 4),
                        o=o, P_sb=P_sb, PT_sb=PT_sb, keepT=self.upperT, spread=True, late=lambda b: late(b, 8))
        settle_late(8)
        self.settle()
        self.gelu_block("l2_block1_mlp", w["a1_li2"], w["a1_li3"], f[:, 32:40], row(5), acc, (w, take))

        self.settle()
        take = self.buffers(Region(self.mem, self.work.at + (B + 1) * D, self.work.end - self.work.at - (B + 1) * D), self.a_hi,
                            Region(self.mem, self.Bm.start, 8192))
        xn, xT, xo, xl = take(D, parts=S), take(KD, S), take(D, parts=S), take(D, parts=S)
        q, P_sb, PT_sb = take(HT4, S), take(4, CK, parts=S), take(CC, 4 * S)
        o, oT, ctx, cn, cT = take(512, parts=S), take(HT4, S), take(CC, P), take(P), take(CK)
        bufs = [dict(xm=take(D, parts=S), qm=take(H, S), kT=take(HT4, CK), v=take(CC, 512)) for _ in range(2)]
        cst = take(12)
        flat = ctx[0:CR].rearrange("p c n -> p (c n)")
        self.load_context(0, flat, "ctxN")

        def prologue2(b, u):
            def context(k):
                V.after(V)
                V.do(self.nc.vector.bn_stats(cst[0:CR, 0:6], ctx[0:CR, k, :]))
                V.after(V)
                V.do(self.nc.vector.memset(cst[0:CR, 10:11], 0.0))
                V.do(self.nc.vector.bn_aggr(cst[0:CR, 6:8], cst[0:CR, 0:6]))
                V.after(V)
                self.ts(cst[0:CR, 8:9], cst[0:CR, 7:8], EPS, None, ALU.add)
                G.after(V)
                self.tt(cst[0:CR, 9:10], cst[0:CR, 8:9], self.minus_half[0:CR, :], ALU.pow, G)
                V.after(G, PE)
                self.ts(cn[0:CR, :], ctx[0:CR, k, :], cst[0:CR, 6:7], cst[0:CR, 9:10], ALU.subtract, ALU.mult)
                PE.after(V)
                self.via_misc(P, CR, lambda bk: self.tp(bk, cn[0:CR, :]),
                              lambda bk: self.ts(cT[:, k * CR:(k + 1) * CR], bk, f[:, 20:21], f[:, 21:22],
                                                 ALU.mult, ALU.add), V)

            def enter():
                V.after(V, PE)
                self.norm(acc[:, b, :], u["xm"])
                V.after(V)
                affine(u["xm"], 2, 3)
            return ([self.await_context] + [lambda k=k: context(k) for k in range(CC)]
                    + self.context_piece(b + 1, flat, "ctxN")
                    + self.key_pieces(u["kT"], [cT], w["a2_wk"], None)
                    + self.value_pieces(u["v"], [cT], w["a2_wv"], None, self.CHUNKS)
                    + [enter] + self.norm_pieces(u["xm"], xn, xT, col(12), col(14))
                    + self.query_pieces(q, u["qm"], xT, w["a2_wq"], None, scale, self.rows32))
        V.do(self.nc.vector.memset(xo, 0.0))
        self.attend_all("l2_block2", H, CK, hd, bufs, lambda u, n: [(u["qm"][:, n, :], u["kT"][:, n // 4, :])],
                        None, prologue2,
                        lambda b, u: close(b, self.out_project(o, oT, w["a2_li1"]), u["xm"], 6),
                        o=o, P_sb=P_sb, PT_sb=PT_sb, spread=True, late=lambda b: late(b, 16))
        settle_late(16)
        self.settle()
        for half in range(2):
            self.tt(x[:, half * HALF:(half + 1) * HALF, :], x[:, half * HALF:(half + 1) * HALF, :],
                    acc[:, half * HALF:(half + 1) * HALF, :], ALU.add)
        V.after(V)
        self.gelu_block("l2_block2_mlp", w["a2_li2"], w["a2_li3"], f[:, 40:48], row(7), x, (w, take))

    def gelu_block(self, name, w2, w3, b2, b3, into, _):
        PE, A, V = self.PE, self.ACT, self.DVE
        xnT = self.xnT
        h = Region(self.mem, self.a_hi.start, 8192).take(8, HT)

        def turn(i):
            free = {}
            PE.after(V, A)
            flat = [xnT[:, k, bass.ds(i * HALF + 1, HALF), :].rearrange("p b s -> p (b s)") for k in range(KD)]

            def fill(u, bk):
                self.project(self.bank(bk, P, HT), [w2[:, k, u * P:(u + 1) * P] for k in range(KD)], flat)

            def drain(u, bk):
                A.after(PE)
                self.act(h[:, u, :], self.bank(bk, P, HT), ACT.Gelu, bias=b2[:, u:u + 1], scale=1.0)
                return (A.mark(),)
            self.tile_stream(8, (0, 1, 2, 3), fill, drain, free)
            PE.after(A)

            def finish(j, at, y):
                dst = self.xs(into, at)
                V.after(V)
                self.tt(dst, dst, y, ALU.add)
                V.after(V)
                self.tt(dst, dst, b3, ALU.add)
            self.down(i, h, w3, free, finish)
        self.prog.loop(name, 2, turn)

    def l2_ffn(self):
        PE, A, V, G = self.PE, self.ACT, self.DVE, self.POOL
        self.settle()
        self.fetch_l2f_rest()
        self.fetch_l3()
        w, w2, x = self.packs["l2f"], self.packs["l2f2"], self.x
        s = self.load("l2f_scales", Region(self.mem, self.biases.start, 2700), self.compute)
        take = self.buffers(self.b_hi, self.work)
        h1, h2 = take(8, HT), take(8, HT)
        xT, g_sb, xn = self.xnT[:, :, 0:HALF, :], take(2, HT), take(D, parts=S)
        self.need("l2f", PE)
        self.need("l2f_scales", A, V)

        def turn(i):
            free = {}
            PE.after(V, A)
            self.norm_half(i, x, xn, xT)
            PE.after(V)
            self.gated(8, xT, w["w1"], w["w2"], h1, g_sb, free, (s["s1"], s["s2"]))

            def dense(src, dst, ww, sc):
                PE.after(A, V)

                def fill(u, bk):
                    self.project(self.bank(bk, P, HT), [ww[:, k, u * P:(u + 1) * P] for k in range(8)],
                                 [src[:, k, :] for k in range(8)])

                def drain(u, bk):
                    A.after(PE)
                    self.act(dst[:, u, :], self.bank(bk, P, HT), ACT.Gelu, scale=sc[:, u:u + 1])
                    return (A.mark(),)
                self.tile_stream(8, (0, 1, 2, 3, 4, 5), fill, drain, free)
            dense(h1, h2, w["h1"], s["h1s"])
            self.need("l2f2", PE)
            dense(h2, h1, w2["h2"], s["h2s"])
            PE.after(A)

            def finish(j, at, y):
                V.after(V)
                self.tt(xn, y, s["s3"][0:S, :], ALU.mult)
                V.after(V)
                self.tt(self.xs(x, at), self.xs(x, at), xn, ALU.add)
            self.down(i, h1, w["w3"], free, finish)
        self.prog.loop("l2_ffn", 2, turn)

    def l3_attn(self):
        nc, PE, A, V, G = self.nc, self.PE, self.ACT, self.DVE, self.POOL
        self.settle()
        w, x = self.packs["l3a"], self.x
        H, DEPTH, hd = 8, 5, 32
        R = H * DEPTH
        take = self.buffers(self.work, self.extra)
        xn, xT = take(D, parts=S), take(KD, S)
        P_sb, PT_sb = take(4, S, parts=S), take(1, 4 * S)
        o, oT, bp = take(D, parts=S), take(KD, S), take(1)
        bufs = [dict(left=take(S, parts=65), right=take(R, S, parts=65), v=take(1, D, parts=S)) for _ in range(2)]
        self.need("l3a", PE, V, A)
        self.ts(bp, w["bp"], 0.5, None, ALU.mult)
        for u in bufs:
            V.do(nc.vector.memset(u["left"], 0.0))
            V.do(nc.vector.memset(u["right"], 0.0))
            V.after(V, G)
            V.do(nc.vector.memset(u["left"][64:65, :], 1.0))
            V.do(nc.vector.memset(u["right"][64:65], 0.5))
        V.after(V)

        def prologue(b, u):
            src = [xT[:, k, :] for k in range(KD)]

            def paths():
                PE.after(V)
                self.via_misc(R, S, lambda bk: self.project(bk, [w["wp"][:, k, :] for k in range(KD)], src),
                              lambda bk: self.act(u["left"][0:R, :], bk, ACT.Tanh, bias=bp[0:R, :], scale=0.5), A)

            def spread():
                G.after(A)
                self.tt(u["right"][0:R], u["left"][0:R, :].unsqueeze(1).broadcast_to([R, R, S]),
                        w["half_eye"][0:R, :].unsqueeze(2).broadcast_to([R, R, S]), ALU.mult, G)
            return (self.norm_pieces(x[:, b, :], xn, xT) + [paths, spread]
                    + self.value_pieces(u["v"], src, w["wv"], None, [(0, S)]))

        def fill(u, g, dst):
            for d in range(DEPTH - 1, -1, -1):
                bk = (0, 1, 6)[d % 3]
                PE.after(*self.since(("s", bk), V))
                at = d * H + 4 * g
                self.mm(self.bank(bk, S, 4 * S), u["left"], u["right"][:, at:at + 4, :], count=True)
                V.after(PE, V)
                agree = self.bank(bk, S, 4 * S).rearrange("p (h s) -> p h s", h=4)
                if d == DEPTH - 1:
                    self.copy(dst, agree, V)
                else:
                    self.stt(dst, dst, 1.0, agree, ALU.add, ALU.mult)
                self.marks[("s", bk)] = [V.mark()]
            V.after(V)
            self.stt(dst, dst, 1.0 / DEPTH, self.causal[0:S, :].unsqueeze(1).broadcast_to([S, 4, S]),
                     ALU.mult, ALU.add)

        def epilogue(b, u):
            y = self.out_project(o, oT, w["wo"])
            self.tt(x[:, b, :], x[:, b, :], y, ALU.add)
            self.done_y()
        self.attend_all("l3_attn", H, S, hd, bufs, None, None, prologue, epilogue,
                        o=o, P_sb=P_sb, PT_sb=PT_sb, fill=fill, spread=True)

    def quantize(self, src, gs, dst, y, t, sc, blocks):
        V, nc = self.DVE, self.nc
        p = src.shape[0]
        b3 = lambda a: a.rearrange("p (n k) -> p n k", k=16)
        wide = lambda a: a.unsqueeze(2).broadcast_to([p, blocks, 16])
        top, s8, c8 = sc[:, 0], sc[:, 1], sc[:, 2]
        V.after(V)
        V.do(nc.vector.tensor_reduce(top, b3(src), AX, ALU.max, apply_absolute_value=True))
        V.after(V)
        self.ts(top, top, 1.0 / 6.0, gs, ALU.mult, ALU.mult)
        V.after(V)
        self.ts(top, top, 448.0, None, ALU.min)
        V.after(V)
        self.ts(c8.bitcast(I32), top.bitcast(I32), 0x7F800000, None, ALU.bitwise_and)
        V.after(V)
        self.ts(c8, c8, 2.0 ** -6, 1.5 * 2.0 ** 20, ALU.max, ALU.mult)
        V.after(V)
        self.tt(s8, top, c8, ALU.add)
        V.after(V)
        self.tt(s8, s8, c8, ALU.subtract)
        V.after(V)
        self.ts(c8, s8, 2.0 ** -9, None, ALU.max)
        V.after(V)
        V.do(nc.vector.reciprocal(c8, c8))
        V.after(V)
        self.ts(c8, c8, gs, 1.0 + 2.0 ** -22, ALU.mult, ALU.mult)
        V.after(V)
        self.tt(b3(y), b3(src), wide(c8), ALU.mult)
        V.after(V)
        self.ts(y, y, 6.0, -6.0, ALU.min, ALU.max)
        V.after(V)
        self.ts(t.bitcast(I32), y.bitcast(I32), 0x7F800000, None, ALU.bitwise_and)
        V.after(V)
        self.ts(t, t, 1.0, 1.5 * 2.0 ** 22, ALU.max, ALU.mult)
        V.after(V)
        self.tt(y, y, t, ALU.add)
        V.after(V)
        self.tt(y, y, t, ALU.subtract)
        V.after(V)
        self.tt(b3(dst), b3(y), wide(s8), ALU.mult)

    def tp16(self, src, dst, n, bank, lane):
        PE = self.PE
        rows = src.shape[0]
        PE.after(self.DVE, self.ACT)
        ps = self.banks[:, bank, :].bitcast(BF16)[:, 0:n * rows].rearrange("p (n r) -> p n r", n=n)
        for k in range(n):
            ins = self.nc.tensor.transpose(ps[:, k, :], src[:, k * P:(k + 1) * P], self.ident16[0:rows, 0:rows])
        PE.do(ins)
        lane.after(PE)
        self.copy(dst, ps, lane)

    def l3_ffn(self):
        nc, PE, A, V, G = self.nc, self.PE, self.ACT, self.DVE, self.POOL
        self.settle()
        w, x = self.packs["l3f"], self.x
        take = self.buffers(self.work, self.extra)
        self.ident16 = take(P, dt=BF16)
        self.copy(self.ident16, self.ident, V)
        self.need("l3f", V, A, G)
        HID = 1024
        big, gs = take(3), take(3)
        y, t, sc = take(2048), take(2048), take(3, P)
        wq = take(2048, dt=BF16)
        wT = {"gate": take(KD, HID, dt=BF16), "up": take(KD, HID, dt=BF16), "down": take(8, D, dt=BF16)}
        for n, name in enumerate(("gate", "up", "down")):
            V.do(nc.vector.tensor_reduce(big[:, n:n + 1], w[name].rearrange("p o i -> p (o i)"), AX, ALU.max,
                                         apply_absolute_value=True))
        G.after(V)
        top = take(3)
        G.do(nc.gpsimd.partition_all_reduce(top, big, P, bass.bass_isa.ReduceOp.max))
        V.after(G)
        V.do(nc.vector.reciprocal(gs, top))
        V.after(V)
        self.ts(gs, gs, 448.0 * 6.0, None, ALU.mult)
        inv = take(3)
        V.after(V)
        for n in range(3):
            self.tt(inv[:, n:n + 1], gs[:, n:n + 1], w["s_in"][:, (0, 0, 1)[n]:(0, 0, 1)[n] + 1], ALU.mult)
        V.after(V)
        V.do(nc.vector.reciprocal(inv, inv))
        for n, name in enumerate(("gate", "up", "down")):
            V.after(PE)
            self.quantize(w[name].rearrange("p o i -> p (o i)"), gs[:, n:n + 1], wq, y, t, sc, P)
            it = w[name].shape[2] // P
            for o in range(w[name].shape[1]):
                cols = wq[:, o * it * P:(o + 1) * it * P]
                self.tp16(cols, wT[name][:, :, o * P:(o + 1) * P], it, o % 4, A)
        xn, xq, xT = take(D, parts=S), take(D, dt=BF16, parts=S), take(KD, S, dt=BF16)
        sg, hid, hq = take(HID, parts=S), take(HID, parts=S), take(HID, dt=BF16, parts=S)
        hT, tmp = take(8, S, dt=BF16), take(D, parts=S)
        self.settle()

        def batch(b):
            PE.after(V, A)
            self.norm(x[:, b, :], xn)
            self.quantize(xn, w["s_in"][0:S, 0:1], xq, y[0:S, 0:D], t[0:S, 0:D], sc[0:S, :, 0:D // 16], D // 16)
            self.tp16(xq, xT, KD, 4, V)
            PE.after(V)
            for o, name in ((0, "gate"), (2, "up")):
                for half in range(2):
                    self.project(self.bank(o + half, S), [xT[:, k, :] for k in range(KD)],
                                 [wT[name][:, k, half * 512:(half + 1) * 512] for k in range(KD)])
            A.after(PE, V)
            self.act(sg.rearrange("p (h n) -> p h n", h=2), self.banks[0:S, 0:2, :], ACT.Silu, scale=inv[0:S, 0:1])
            V.after(A, PE)
            self.stt(hid.rearrange("p (h n) -> p h n", h=2), self.banks[0:S, 2:4, :], inv[0:S, 1:2],
                     sg.rearrange("p (h n) -> p h n", h=2), ALU.mult, ALU.mult)
            self.quantize(hid, w["s_in"][0:S, 1:2], hq, y[0:S, 0:HID], t[0:S, 0:HID], sc[0:S, :, 0:HID // 16], HID // 16)
            self.tp16(hq, hT, 8, 5, A)
            PE.after(A)
            self.project(self.bank(6, S, D), [hT[:, k, :] for k in range(8)], [wT["down"][:, k, :] for k in range(8)])
            V.after(PE, V)
            self.stt(x[:, b, :], self.bank(6, S, D), inv[0:S, 2:3], x[:, b, :], ALU.mult, ALU.add)
        self.prog.loop("l3_ffn", B, batch)

SUBLAYERS = (Decoder.l0_attn, Decoder.l0_xattn, Decoder.l0_ffn, Decoder.l1_attn, Decoder.l1_xattn, Decoder.l1_ffn,
             Decoder.l2_attn, Decoder.l2_xattn, Decoder.l2_ffn, Decoder.l3_attn, Decoder.l3_xattn, Decoder.l3_ffn)


def build(nc, ins, layouts, out, per_turn, stages=None):
    from contextlib import ExitStack
    with ExitStack() as stack:
        d = Decoder(nc, stack, ins, layouts, out, per_turn)
        d.start()
        for stage in stages or SUBLAYERS:
            stage(d)
        d.SP.after(*d.compute, d.CTX)
        done = Lane(d.prog, "out_stored", nc.sync, 16)
        done.do(nc.sync.dma_start(out, d.x[:, 0:B, :]))
        nc.sync.wait_ge(done.sem, 16)
        return d.prog.counted


def lay_out(i):
    f = lambda name: np.asarray(i[name])

    def inout(w):
        return w.reshape(-1, P, w.shape[1]).transpose(1, 0, 2)

    def col(b):
        return b.reshape(-1, P).T

    def row(b):
        return np.broadcast_to(b[None, :], (P, b.shape[0]))

    def pad(a):
        return np.concatenate([a, np.zeros((P - a.shape[0],) + a.shape[1:], a.dtype)], 0)

    packs = {}
    iota = np.arange(S)
    dist = iota[:, None] - iota[None, :]
    near = np.where(np.abs(dist) <= 3, np.exp(-(dist.astype(np.float32) ** 2) / np.float32(2.0 * 0.4 ** 2)), 0.0)
    near = near / (near.sum(-1, keepdims=True) + 1e-10)
    c32 = lambda a: np.ascontiguousarray(a, np.float32)
    packs["consts"] = {
        "ident": np.eye(P, dtype=np.float32),
        "causal": pad(c32(np.where(dist >= 0, 0.0, MASKED))),
        "upperT": pad(c32(dist > 0)),
        "rows16": c32(np.arange(P)[:, None] // 16 == np.arange(8)),
        "rows32": c32(np.arange(P)[:, None] // 32 == np.arange(4)),
        "rows64": c32(np.arange(P)[:, None] // 64 == np.arange(2)),
        "prefix": pad(c32(dist.T >= 0)),
        "ones": np.ones((P, S), np.float32),
        "turn8": row(c32(8 - np.arange(8))),
        "spread": pad(c32((1.0 - 0.6) * near.T)),
    }
    order = [0, 1, 3, 2]
    gates = lambda w: w.reshape(4, D, -1)[order].reshape(4 * D, -1)
    both = lambda n: np.stack([inout(gates(f(f"L0_attn_{n}_q")).T), inout(gates(f(f"L0_attn_{n}_k")).T)], 1)
    wk2 = f("L0_attn_Wk2").reshape(4, 64, 64)
    packs["l0a"] = {
        "wih": both("Wih"),
        "wq1": inout(f("L0_attn_Wq1").T), "wk1": inout(f("L0_attn_Wk1").T),
        "wq2": pad(f("L0_attn_Wq2").T),
        "wk2": pad(np.stack([wk2, wk2], 1).reshape(512, 64).T),
        "wv": inout(f("L0_attn_Wv").T), "wo": inout(f("L0_attn_Wo").T),
    }
    bk2 = f("L0_attn_bk2").reshape(4, 64)
    packs["l0a_whh"] = {"whh": both("Whh")}
    packs["l0a_bias"] = {
        "b_lstm": np.concatenate([col(gates(f("L0_attn_b_q"))[:, 0]), col(gates(f("L0_attn_b_k"))[:, 0])], 1),
        "bq1": pad(f("L0_attn_bq1")[:, None]), "bk1": pad(f("L0_attn_bk1")[:, None]),
        "bq2": col(f("L0_attn_bq2")), "bk2": np.concatenate([bk2, bk2], 1).T,
        "bv": row(f("L0_attn_bv")),
    }
    packs["l0x"] = {"wq": inout(f("L0_xattn_Wq")), "wk": inout(f("L0_xattn_Wk")), "wv": inout(f("L0_xattn_Wv")),
                    "bq": col(f("L0_xattn_bq")), "bk": col(f("L0_xattn_bk")), "bv": row(f("L0_xattn_bv"))}
    packs["l0f"] = {"wg": inout(f("L0_ffn_w_gate").T), "wu": inout(f("L0_ffn_w_up").T),
                    "wd": inout(f("L0_ffn_w_down").T)}
    packs["l1a"] = {"wq": inout(f("L1_attn_Wq").T), "wk": inout(f("L1_attn_Wk").T), "wv": inout(f("L1_attn_Wv").T),
                    "wo": inout(f("L1_attn_Wo").T), "bq": col(f("L1_attn_bq")), "bk": col(f("L1_attn_bk")),
                    "bv": row(f("L1_attn_bv")), "bo": row(f("L1_attn_bo"))}
    packs["l1x"] = {"wq": inout(f("L1_xattn_Wq")), "wk": inout(f("L1_xattn_Wk")), "wv": inout(f("L1_xattn_Wv")),
                    "wo": inout(f("L1_xattn_Wo")), "bq": col(f("L1_xattn_bq")), "bk": col(f("L1_xattn_bk")),
                    "bv": row(f("L1_xattn_bv")), "bo": row(f("L1_xattn_bo"))}
    packs["l1f"] = {
        "router": inout(f("L1_ffn_gate_w").T),
        "dg": np.concatenate([inout(w.T) for w in f("L1_ffn_dyn_gate_w")], 2),
        "du": np.concatenate([inout(w.T) for w in f("L1_ffn_dyn_up_w")], 2),
        "dd": np.concatenate([inout(w.T) for w in f("L1_ffn_dyn_down_w")], 1),
        "sg": inout(f("L1_ffn_sh_gate_w")[0].T), "su": inout(f("L1_ffn_sh_up_w")[0].T),
        "sd": inout(f("L1_ffn_sh_down_w")[0].T),
    }
    swap = lambda w: w.reshape(D, -1, 2, 64)[:, :, ::-1].reshape(D, -1)
    packs["l2a"] = {"wq": inout(f("L2_attn_Wq")), "wqs": inout(swap(f("L2_attn_Wq"))),
                    "wk": inout(f("L2_attn_Wk")), "wks": inout(swap(f("L2_attn_Wk"))),
                    "wv": inout(f("L2_attn_Wv")), "wo": inout(f("L2_attn_Wo"))}
    inv_freq = (1.0 / np.float32(10000.0) ** (np.arange(0, P, 2, dtype=np.float32) / np.float32(P))).astype(np.float32)
    angle = np.outer(np.concatenate([inv_freq, inv_freq]), iota.astype(np.float32)).astype(np.float32)
    sign = np.where(np.arange(P) < P // 2, -1.0, 1.0)[:, None]
    unit = 1.0 / np.sqrt(np.float32(P))
    packs["rope"] = {"cosq": c32(np.cos(angle) * unit), "sinq": c32(np.sin(angle) * sign * unit),
                     "cos": c32(np.cos(angle)), "sin": c32(np.sin(angle) * sign)}
    x2 = lambda n: f(f"L2_xattn_{n}")
    heads = lambda w: inout(w.transpose(1, 0, 2).reshape(w.shape[1], -1))
    packs["l2x"] = {"a1_wq": heads(x2("a1_wq")), "a1_wk": heads(x2("a1_wk")), "a1_wv": heads(x2("a1_wv")),
                    "a1_li1": inout(x2("a1_li1_w")), "a1_li2": inout(x2("a1_li2_w")), "a1_li3": inout(x2("a1_li3_w")),
                    "a2_wq": heads(x2("a2_wq")), "a2_wk": heads(x2("a2_wk")), "a2_wv": heads(x2("a2_wv")),
                    "a2_li1": inout(x2("a2_li1_w")), "a2_li2": inout(x2("a2_li2_w")), "a2_li3": inout(x2("a2_li3_w"))}
    cols = [col(x2(n)) for n in ("a1_lnx_g", "a1_lnx_b", "a1_lny_g", "a1_lny_b", "a1_ln3_g", "a1_ln3_b",
                                 "a2_lnx_g", "a2_lnx_b", "a2_ln3_g", "a2_ln3_b", "a2_lny_g", "a2_lny_b")]
    packs["l2x_rows"] = {
        "rows": np.stack([row(x2(n)) for n in ("ln1_g", "ln1_b", "ln2_g", "ln2_b", "a1_li1_b", "a1_li3_b",
                                               "a2_li1_b", "a2_li3_b")], 1),
        "cols": np.concatenate(cols + [np.zeros((P, 10), np.float32), col(x2("a1_li2_b")), col(x2("a2_li2_b"))], 1)}
    l2 = lambda n: f(f"L2_ffn_{n}")
    packs["l2f"] = {"w1": inout(l2("w1_w").T), "w2": inout(l2("w2_w").T), "h1": inout(l2("h1_w").T),
                    "w3": inout(l2("w3_w").T)}
    packs["l2f2"] = {"h2": inout(l2("h2_w").T)}
    packs["l2f_scales"] = {"s1": col(l2("w1_s")), "s2": col(l2("w2_s")), "h1s": col(l2("h1_s")),
                           "h2s": col(l2("h2_s")), "s3": row(l2("w3_s"))}
    by_depth = lambda w: w.reshape(-1, 8, 5).transpose(0, 2, 1).reshape(-1, 40)
    packs["l3a"] = {"wp": inout(by_depth(f("L3_attn_Wp"))), "bp": pad(by_depth(f("L3_attn_bp")[None])[0][:, None]),
                    "half_eye": pad(c32(0.5 * np.eye(40))),
                    "wv": inout(f("L3_attn_Wv")), "wo": inout(f("L3_attn_Wo"))}
    wkv = f("L3_xattn_Wkv")
    packs["l3x"] = {"wq": inout(f("L3_xattn_Wq").T), "wk": inout(wkv[0:D].T), "wv": inout(wkv[D:2 * D].T),
                    "wo": inout(f("L3_xattn_Wo").T)}
    natural = lambda w: w.reshape(-1, P, w.shape[1]).transpose(1, 0, 2)
    packs["l3f"] = {"gate": natural(f("L3_ffn_gate_w")), "up": natural(f("L3_ffn_up_w")),
                    "down": natural(f("L3_ffn_down_w")),
                    "s_in": row(np.concatenate([f("L3_ffn_s_in"), f("L3_ffn_s_in_down")]))}
    arrays = {"x": np.ascontiguousarray(f("x").transpose(1, 0, 2))}
    ctx = f("ctx_512")
    ahead = np.concatenate([ctx, ctx[:2]], 0)
    arrays["ctxT"] = np.ascontiguousarray(ahead.transpose(0, 2, 1))
    arrays["ctxN"] = np.ascontiguousarray(ahead.reshape(B + 2, CC, CR, CD).transpose(0, 2, 1, 3).reshape(B + 2, CR, -1))
    layouts = {}
    for name, pack in packs.items():
        layouts[name] = [(k, a.shape[1:]) for k, a in pack.items()]
        arrays[name] = np.ascontiguousarray(np.concatenate([a.reshape(P, -1) for a in pack.values()], 1))
    return arrays, layouts


def kernel(**inputs):
    import concourse.bacc as bacc
    from concourse.bass_utils import run_bass_kernel_spmd

    arrays, layouts = lay_out(inputs)
    per_turn = {}
    for _ in range(2):
        nc = bacc.Bacc("TRN2", target_bir_lowering=False, num_devices=1)
        ins = {k: nc.dram_tensor(f"in_{k}", a.shape, mybir.dt.from_np(a.dtype), kind="ExternalInput").ap()
               for k, a in arrays.items()}
        out = nc.dram_tensor("out", (S, B, D), F32, kind="ExternalOutput").ap()
        per_turn = build(nc, ins, layouts, out, per_turn)
    r = run_bass_kernel_spmd(nc, [{f"in_{k}": a for k, a in arrays.items()}], core_ids=[0])
    return np.ascontiguousarray(r.results[0]["out"].transpose(1, 0, 2))
```

```python
import numpy as np
import concourse.bass as bass
import concourse.mybir as mybir
from concourse.alu_op_type import AluOpType as ALU

F32 = mybir.dt.float32
BF16 = mybir.dt.bfloat16
I32 = mybir.dt.int32
ACT = mybir.ActivationFunctionType
AX = mybir.AxisListType.X

P = 128
B, S, D = 8, 112, 256
T = B * S
KD = D // P
CK, CD = 375, 128
CC = 3
CR = CK // CC
HALF = B // 2
HT = HALF * S
EPS = 1e-5
MASKED = -1e30


class Lane:

    def __init__(self, prog, name, engine, step=1):
        self.prog, self.name, self.engine, self.step = prog, name, engine, step
        self.sem = prog.stack.enter_context(prog.nc.semaphore(name))
        self.n = 0
        self.base = 0
        self.seen = {}
        prog.lanes.append(self)

    def do(self, ins):
        self.n += self.step
        return ins.then_inc(self.sem, self.step)

    def mark(self):
        return (self, self.n, self.prog.turn)

    def after(self, *points):
        for pt in points:
            lane, k, turn = pt.mark() if isinstance(pt, Lane) else pt
            if self.seen.get((lane.name, turn), -1) >= k:
                continue
            self.seen[(lane.name, turn)] = k
            if turn is None or turn is not self.prog.turn:
                if k:
                    self.engine.wait_ge(lane.sem, k)
            else:
                per = self.prog.per_turn.get((turn.name, lane.name), 0)
                if per:
                    self.engine.wait_ge(lane.sem, turn.i * per + (lane.base + k))
                elif lane.base + k:
                    self.engine.wait_ge(lane.sem, lane.base + k)


class Turn:
    def __init__(self, name, i, times):
        self.name, self.i, self.times = name, i, times


class Prog:

    def __init__(self, nc, stack, per_turn):
        self.nc, self.stack, self.per_turn = nc, stack, per_turn
        self.lanes, self.turn, self.counted = [], None, {}

    def loop(self, name, times, body):
        for lane in self.lanes:
            lane.base, lane.n, lane.seen = lane.n, 0, {}
        with self.nc.Fori(0, times) as i:
            self.turn = Turn(name, i, times)
            body(i)
        for lane in self.lanes:
            self.counted[(name, lane.name)] = lane.n
            lane.n, lane.base, lane.seen = lane.base + times * lane.n, 0, {}
        self.turn = None


class Region:

    def __init__(self, mem, start, words):
        self.mem, self.start, self.at, self.end = mem, start, start, start + words

    def take(self, *dims, dt=F32, parts=P):
        n = int(np.prod(dims))
        words = n if dt in (F32, I32) else (n + 1) // 2
        a = self.mem[0:parts, self.at:self.at + words]
        self.at += words
        assert self.at <= self.end, (self.at, self.end)
        if dt is not F32:
            a = a.bitcast(dt)
        names = "abcde"[:len(dims)]
        if len(dims) > 1:
            a = a.rearrange(f"p ({' '.join(names)}) -> p {' '.join(names)}",
                            **{c: d for c, d in zip(names, dims)})
        return a

    def rest(self):
        return Region(self.mem, self.at, self.end - self.at)


class Decoder:

    def __init__(self, nc, stack, ins, layouts, out, per_turn):
        self.nc, self.ins, self.layouts, self.out = nc, ins, layouts, out
        self.prog = Prog(nc, stack, per_turn)
        lane = lambda name, engine, step=1: Lane(self.prog, name, engine, step)
        self.PE = lane("pe_done", nc.tensor)
        self.ACT = lane("act_done", nc.scalar)
        self.DVE = lane("dve_done", nc.vector)
        self.POOL = lane("pool_done", nc.gpsimd)
        self.SP = lane("sp_done", nc.sync)
        self.CTX = lane("ctx_landed", nc.sync, 16)
        self.compute = (self.PE, self.ACT, self.DVE, self.POOL)
        self.landed = {}

        words = 53100
        mem = stack.enter_context(nc.sbuf_tensor("memory", [P, words], F32))
        self.mem = mem
        ps = stack.enter_context(nc.psum_tensor("banks", [P, 8, 512], F32))
        self.bank = lambda n, parts=P, cols=512: ps[0:parts, n, 0:cols]
        self.banks = ps
        whole = Region(mem, 0, words)
        self.x_all = whole.take(B + 2, D, parts=S)
        self.x = self.x_all[:, 1:, :]
        self.xnT = whole.take(KD, B + 1, S)
        self.small = Region(mem, whole.at, 960)
        whole.at += 960
        self.biases = Region(mem, whole.at, 2700)
        whole.at += 2700
        self.A = Region(mem, whole.at, 22528)
        whole.at += 22528
        self.Bm = Region(mem, whole.at, 15360)
        whole.at += 15360
        self.work = whole.rest()
        self.a_start, self.packs = self.A.start, {}
        self.marks = {}
        self.stats = self.small.take(16, parts=S)
        self.minus_half = self.small.take(1)
        self.stats4 = self.small.take(HALF, 12, parts=S)

    def load(self, pack, region, after=()):
        self.SP.after(*after)
        lane = Lane(self.prog, f"{pack}_landed", self.nc.sync, 16)
        self.landed[pack] = lane
        first, arrays = region.at, {}
        dt = self.ins[pack].dtype
        for name, shape in self.layouts[pack]:
            arrays[name] = region.take(*shape, dt=dt)
        dst = self.mem[:, first:region.at]
        lane.do(self.nc.sync.dma_start(dst if dt is F32 else dst.bitcast(dt), self.ins[pack]))
        return arrays

    def need(self, pack, *lanes):
        for lane in lanes:
            lane.after(self.landed[pack])

    def mm(self, out, lhsT, rhs, start=True, stop=True, count=False):
        ins = self.nc.tensor.matmul(out, lhsT, rhs, start=start, stop=stop)
        if count:
            self.PE.do(ins)

    def project(self, out, weights, acts, count=True):
        n = len(weights)
        for k in range(n):
            self.mm(out, weights[k], acts[k], k == 0, k == n - 1, count and k == n - 1)

    def tp(self, out, in_, count=True):
        n = in_.shape[0]
        ins = self.nc.tensor.transpose(out, in_, self.ident[0:n, 0:n])
        if count:
            self.PE.do(ins)

    def tt(self, out, a, b, op, lane=None):
        lane = lane or self.DVE
        lane.do(lane.engine.tensor_tensor(out, a, b, op))

    def ts(self, out, a, s1, s2, op0, op1=None, lane=None):
        lane = lane or self.DVE
        lane.do(lane.engine.tensor_scalar(out, a, s1, s2, op0, op1) if op1 is not None
                else lane.engine.tensor_scalar(out, a, s1, None, op0))

    def stt(self, out, a, s, b, op0, op1):
        self.DVE.do(self.nc.vector.scalar_tensor_tensor(out=out, in0=a, scalar=s, in1=b, op0=op0, op1=op1))

    def act(self, out, in_, func, **kw):
        self.ACT.do(self.nc.scalar.activation(out, in_, func, **kw))

    def copy(self, out, in_, lane):
        lane.do(lane.engine.copy(out, in_) if lane is self.ACT else lane.engine.tensor_copy(out, in_))

    def norm(self, src, dst):
        self.norm_begin(src)
        self.norm_end(src, dst)

    def norm_begin(self, src):
        DVE, POOL, st = self.DVE, self.POOL, self.stats
        DVE.do(self.nc.vector.bn_stats(st[:, 0:6], src))
        DVE.after(DVE)
        DVE.do(self.nc.vector.memset(st[:, 10:11], 0.0))
        DVE.do(self.nc.vector.bn_aggr(st[:, 6:8], st[:, 0:6]))
        DVE.after(DVE)
        self.ts(st[:, 8:9], st[:, 7:8], EPS, None, ALU.add)
        POOL.after(DVE)
        self.tt(st[:, 9:10], st[:, 8:9], self.minus_half[0:S, :], ALU.pow, POOL)

    def norm_end(self, src, dst):
        DVE, st = self.DVE, self.stats
        DVE.after(self.POOL)
        self.ts(dst, src, st[:, 6:7], st[:, 9:10], ALU.subtract, ALU.mult)

    def turn_features(self, src, dst, bank, gain=None, shift=None):
        PE, DVE = self.PE, self.DVE
        PE.after(DVE)
        pt = self.bank(bank, P, KD * S).rearrange("p (k s) -> p k s", k=KD)
        for k in range(KD):
            self.tp(pt[:, k, :], src[:, k * P:(k + 1) * P], k == KD - 1)
        DVE.after(PE)
        if gain is None:
            self.copy(dst, pt, DVE)
        else:
            for k in range(KD):
                self.ts(dst[:, k, :], pt[:, k, :], gain[:, k:k + 1], shift[:, k:k + 1], ALU.mult, ALU.add)

    def since(self, key, *lanes):
        return self.marks.get(key) or [(lane, 0, self.prog.turn) for lane in lanes]

    def via_misc(self, parts, cols, fill, drain, lane):
        n = self.next_misc()
        bk = self.bank(n, parts, cols)
        fill(bk)
        lane.after(self.PE)
        drain(bk)
        self.marks[("misc", n)] = [lane.mark()]

    def next_misc(self):
        n = self.misc_banks[self.misc_at % len(self.misc_banks)]
        self.misc_at += 1
        self.PE.after(*self.since(("misc", n), self.DVE, self.ACT))
        return n

    def attend_all(self, name, H, nk, hd, bufs, score, value, prologue, epilogue, *, o, take,
                   mask=None, keepT=None, fill=None, spread=False, o_banks=(7,), share=1.0, plus=None,
                   side=None):
        PE, A, V, G, nc, M = self.PE, self.ACT, self.DVE, self.POOL, self.nc, self.marks
        Q = min(4, H)
        groups = H // Q
        wide = nk > S
        chunks = self.CHUNKS if wide else [(0, nk)]
        per_bank = 512 // hd
        P_both = [take(Q, nk, parts=S) for _ in range(2)]
        PT_both = [take(len(chunks), Q * S) for _ in range(2)]
        odd = lambda buf, g: (bufs.index(buf) * groups + g) % 2
        in_scores, in_turn = (Q - 1 if wide else 4 if fill else 1), len(chunks)
        PLACES, spare = in_scores + in_turn + 2, in_scores + 1
        self.side = lambda: None
        ring = lambda buf, n: (bufs.index(buf) * H + n) % 3
        self.misc_banks, self.misc_at = side or ((3,) if wide and H > 1 else (1, 2, 3) if wide else (2, 3)), 0

        def scores(buf, g):
            if fill is not None:
                return
            for h in range(Q):
                n = Q * g + h
                if wide:
                    out = self.bank(ring(buf, n), S, nk)
                    PE.after(*self.since(("s", ring(buf, n)), A))
                else:
                    out = self.bank(g % 2, S, Q * nk)[:, h * nk:(h + 1) * nk]
                    if h == 0:
                        PE.after(*self.since(("s", g % 2), A, V))
                pairs = score(buf, n)
                self.project(out, [q for q, _ in pairs], [k for _, k in pairs])
                M[("sc", h)] = [PE.mark()]
                if wide:
                    weigh(buf, n, h, out)
                if h < Q - 1 and (wide or h == Q // 2 - 1):
                    self.side()

        def weigh(buf, n, h, src):
            o_ = odd(buf, n // Q)
            P_sb = P_both[o_]
            V.after(*M[("sc", h)])
            V.do(nc.vector.tensor_reduce(buf["nmax"][:, n:n + 1], src, AX, ALU.max, negate=True))
            A.after(V, *self.since(("turn", o_), PE))
            self.act(P_sb[:, h, :], src, ACT.Exp, bias=buf["nmax"][:, n:n + 1], scale=1.0,
                     accum_out=buf["total"][:, n:n + 1])
            M[("s", ring(buf, n))] = [A.mark()]
            M[("exp", o_)] = [A.mark()]

        def weigh_group(buf, g):
            if wide:
                return
            o_ = odd(buf, g)
            P_sb = P_both[o_]
            src = self.bank(g % 2, S, Q * nk).rearrange("p (h k) -> p h k", h=Q)
            if fill is not None:
                V.after(*self.since(("turn", o_), PE))
                fill(buf, g, P_sb)
                src = P_sb
            else:
                V.after(*M[("sc", Q - 1)])
                if mask is not None:
                    V.after(*self.since(("turn", o_), PE))
                    self.tt(P_sb, src, mask[0:S, :].unsqueeze(1).broadcast_to([S, Q, nk]), ALU.add)
                    M[("s", g % 2)] = [V.mark()]
                    src = P_sb
            V.after(V)
            n = Q * g
            V.do(nc.vector.tensor_reduce(buf["nmax"][:, n:n + Q], src, AX, ALU.max, negate=True))
            A.after(V, *self.since(("turn", o_), PE))
            for h in range(Q):
                self.act(P_sb[:, h, :], src[:, h, :], ACT.Exp, bias=buf["nmax"][:, n + h:n + h + 1],
                         scale=1.0, accum_out=buf["total"][:, n + h:n + h + 1])
            if src is not P_sb:
                M[("s", g % 2)] = [A.mark()]
            M[("exp", o_)] = [A.mark()]

        def turn(buf, g):
            o_ = odd(buf, g)
            P_sb, PT_sb = P_both[o_], PT_both[o_]
            PE.after(*self.since(("exp", o_), A))
            marks = []
            for c, (at, rows) in enumerate(chunks):
                bank = 4 + c if wide else 4 + g % 2
                pt = self.bank(bank, rows, Q * S)
                PE.after(*self.since(("pt", bank), A, V))
                for h in range(Q):
                    self.tp(pt[:, h * S:(h + 1) * S], P_sb[:, h, at:at + rows], h == Q - 1)
                lane = A if c == 1 else V
                lane.after(PE, *self.since(("values", o_), PE))
                if keepT is not None:
                    self.tt(PT_sb[0:rows, c, :].rearrange("p (h s) -> p h s", h=Q),
                            pt.rearrange("p (h s) -> p h s", h=Q),
                            keepT[0:rows, :].unsqueeze(1).broadcast_to([rows, Q, S]), ALU.mult)
                else:
                    self.copy(PT_sb[0:rows, c, :], pt, lane)
                M[("pt", bank)] = [lane.mark()]
                marks.append(lane.mark())
                self.side()
            M[("turn", o_)], M[("PT", o_)] = [PE.mark()], marks

        def values(buf, g):
            o_ = odd(buf, g)
            PT_sb = PT_both[o_]
            PE.after(*M[("PT", o_)], *self.since("own", V))
            for h in range(Q):
                n = Q * g + h
                if spread:
                    out = self.bank(7, S)[:, h * Q * hd:(h + 1) * Q * hd]
                    vs = [buf["v"][0:r, c, Q * g * hd:Q * (g + 1) * hd] for c, (_, r) in enumerate(chunks)]
                else:
                    out = self.bank(o_banks[n // per_bank], S)[:, (n % per_bank) * hd:(n % per_bank + 1) * hd]
                    vs = [value(buf, n, c) for c in range(len(chunks))]
                self.project(out, [PT_sb[0:r, c, h * S:(h + 1) * S] for c, (_, r) in enumerate(chunks)],
                             vs, h == Q - 1)
            M[("values", o_)] = M["summed"] = [PE.mark()]
            if spread:
                V.after(PE, *self.since("oread", PE))
                own = self.bank(7, S, 512).rearrange("p (h x) -> p h x", x=hd)
                if Q * (Q + 1) <= 512 // hd:
                    self.copy(o[:, Q * g * hd:Q * (g + 1) * hd].rearrange("p (h d) -> p h d", h=Q),
                              own[:, 0:Q * (Q + 1):Q + 1, :], V)
                else:
                    for h in range(Q):
                        self.copy(o[:, (Q * g + h) * hd:(Q * g + h + 1) * hd], own[:, Q * h + h, :], V)
                M["own"] = [V.mark()]

        def divide(buf, last_exp):
            inv = buf["inv"]
            V.after(*last_exp)
            V.do(nc.vector.reciprocal(inv[:, 0:H], buf["total"][:, 0:H]))
            if share != 1.0:
                V.after(V)
                self.ts(inv[:, 0:H], inv[:, 0:H], share, None, ALU.mult)
            V.after(V, *M["summed"], *self.since("oread", PE))
            if spread:
                ov = o.rearrange("p (h d) -> p h d", h=H)
                self.tt(ov, ov, inv[:, 0:H].unsqueeze(2).broadcast_to([S, H, hd]), ALU.mult)
            else:
                each = min(per_bank, H)
                for n in range(0, H, each):
                    ob = self.bank(o_banks[n // per_bank], S, each * hd).rearrange("p (h d) -> p h d", h=each)
                    self.tt(o[:, n * hd:(n + each) * hd].rearrange("p (h d) -> p h d", h=each), ob,
                            inv[:, n:n + each].unsqueeze(2).broadcast_to([S, each, hd]), ALU.mult)
                M["own"] = [V.mark()]
            if plus is not None:
                V.after(V)
                self.tt(o, o, plus(buf), ALU.add)
            M["o"] = [V.mark()]

        def first(buf):
            PE.after(*M["ready"])
            scores(buf, 0)

        M.clear()
        self.row_stats = Region(self.mem, self.small.at, 96)
        for buf in bufs:
            buf["nmax"], buf["total"], buf["inv"] = (self.take_small(16) for _ in range(3))
        V.do(nc.vector.memset(o, 0.0))
        for piece in prologue(0, bufs[0]):
            piece()
        M["ready"] = [V.mark(), A.mark(), G.mark()]
        first(bufs[0])
        weigh_group(bufs[0], 0)

        def pair(i):
            M.clear()
            for p in range(2):
                b, buf, other = i * 2 + p, bufs[p], bufs[1 - p]
                pieces = epilogue(b, other) + prologue(b + 1, other)
                total, places, at = len(pieces), PLACES * groups - spare, [0]

                def side(flush=False):
                    at[0] += 1
                    while pieces and (flush or (total - len(pieces)) * places < at[0] * total):
                        pieces.pop(0)()
                        if not pieces:
                            M["ready"] = [V.mark(), A.mark(), G.mark()]
                self.side = side
                for g in range(groups):
                    if g + 1 < groups:
                        scores(buf, g + 1)
                        weigh_group(buf, g + 1)
                        side()
                    last_exp = self.since(("exp", odd(buf, g)), A)
                    turn(buf, g)
                    if g:
                        values(buf, g - 1)
                    side()
                self.side = lambda: None
                side(flush=True)
                first(other)
                weigh_group(other, 0)
                values(buf, groups - 1)
                divide(buf, last_exp)
        self.prog.loop(name, B // 2, pair)
        self.settle()
        M.clear()
        for piece in epilogue(B, bufs[1]):
            piece()

    def output_pieces(self, o, oT, w, finish):
        tiles = w.shape[1]
        PE, V = self.PE, self.DVE

        def transposes(t0, n):
            PE.after(*self.since("o", V))
            src = lambda t: o[:, (t0 + t) * P:(t0 + t + 1) * P]
            self.via_misc(P, n * S,
                          lambda bk: [self.tp(bk[:, t * S:(t + 1) * S], src(t), t == n - 1) for t in range(n)],
                          lambda bk: self.copy(oT[:, t0:t0 + n, :], bk.rearrange("p (t s) -> p t s", t=n), V), V)
            self.marks["oread"] = [PE.mark()]
            self.marks["oT"] = [V.mark()]

        def product():
            PE.after(*self.marks["oT"])
            self.via_misc(S, D, lambda bk: self.project(bk, [oT[:, t, :] for t in range(tiles)],
                                                        [w[:, t, :] for t in range(tiles)]), finish, V)
        return [lambda t0=t0: transposes(t0, min(4, tiles - t0)) for t0 in range(0, tiles, 4)] + [product]

    def take_small(self, n):
        return self.row_stats.take(n, parts=S)

    def norm_pieces(self, src, xn, xT, gain=None, shift=None, also=None):
        V, PE = self.DVE, self.PE

        def begin():
            V.after(V)
            self.norm_begin(src)

        def end():
            self.norm_end(src, xn)

        def turn():
            PE.after(V)

            def evict(bk):
                pt = bk.rearrange("p (k s) -> p k s", k=KD)
                if gain is None:
                    self.copy(xT, pt, V)
                else:
                    for k in range(KD):
                        self.ts(xT[:, k, :], pt[:, k, :], gain[:, k:k + 1], shift[:, k:k + 1], ALU.mult, ALU.add)
                if also is not None:
                    dst, g2, s2 = also
                    for k in range(KD):
                        self.ts(dst[:, k, :], pt[:, k, :], g2[:, k:k + 1], s2[:, k:k + 1], ALU.mult, ALU.add)
                self.marks["source"] = [V.mark()]
            self.via_misc(P, KD * S, lambda bk: [self.tp(bk[:, k * S:(k + 1) * S], xn[:, k * P:(k + 1) * P],
                                                         k == KD - 1) for k in range(KD)], evict, V)
        return [begin, end, turn]

    def key_pieces(self, kT, src, w, bias, step=1):
        A, nk = self.ACT, kT.shape[2]

        def piece(t0):
            def fill(bk):
                for t in range(t0, t0 + step):
                    self.project(bk[:, (t - t0) * nk:(t - t0 + 1) * nk],
                                 [w[:, k, t * P:(t + 1) * P] for k in range(len(src))], src, t == t0 + step - 1)

            def evict(bk):
                if bias is None:
                    self.copy(kT[:, t0:t0 + step, :], bk.rearrange("p (t n) -> p t n", t=step), A)
                else:
                    for t in range(t0, t0 + step):
                        self.act(kT[:, t, :], bk[:, (t - t0) * nk:(t - t0 + 1) * nk], ACT.Identity,
                                 bias=bias[:, t:t + 1], scale=1.0)
            self.PE.after(*self.since("source", self.DVE))
            self.via_misc(P, step * nk, fill, evict, A)
        return [lambda t0=t0: piece(t0) for t0 in range(0, kT.shape[1], step)]

    def value_pieces(self, v, src, w, bias, chunks):
        V, F = self.DVE, w.shape[2]

        def piece(c, at, rows):
            def evict(bk):
                if bias is None:
                    self.copy(v[0:rows, c, :], bk, V)
                else:
                    self.tt(v[0:rows, c, :], bk, bias[0:rows, :], ALU.add)
            self.via_misc(rows, F, lambda bk: self.project(bk, [s[:, at:at + rows] for s in src],
                                                           [w[:, k, :] for k in range(len(src))]), evict, V)
        return [lambda c=c, a=a, r=r: piece(c, a, r) for c, (a, r) in enumerate(chunks)]

    def query_pieces(self, q, qm, src, w, bias, scale, rows):
        PE, V, G = self.PE, self.DVE, self.POOL
        tiles = w.shape[2] // P

        def one():
            PE.after(*self.since("source", V))

            def fill(bk):
                for t in range(tiles):
                    self.project(bk[:, t * S:(t + 1) * S], [w[:, k, t * P:(t + 1) * P] for k in range(KD)],
                                 [src[:, k, :] for k in range(KD)], t == tiles - 1)

            def evict(bk):
                ps = bk.rearrange("p (t s) -> p t s", t=tiles)
                if bias is None:
                    self.ts(q, ps, scale, None, ALU.mult)
                else:
                    self.stt(q, ps, scale, bias.unsqueeze(2).broadcast_to([P, tiles, S]), ALU.mult, ALU.add)
            V.after(G)
            self.via_misc(P, tiles * S, fill, evict, V)

        def two():
            per = rows.shape[1]
            G.after(V)
            for t in range(tiles):
                self.tt(qm[:, t * per:(t + 1) * per, :], q[:, t, :].unsqueeze(1).broadcast_to([P, per, S]),
                        rows.unsqueeze(2).broadcast_to([P, per, S]), ALU.mult, G)
        return [one] if qm is None else [one, two]

    def context_piece(self, b, ctx, which="ctxT"):
        return [lambda: self.load_context(b, ctx, which)]

    CHUNKS = [(c * CR, CR) for c in range(CC)]

    def await_context(self):
        for e in (self.PE, self.ACT, self.DVE):
            e.after(self.CTX)

    def start(self):
        SP, nc = self.SP, self.nc
        self.load_x = Lane(self.prog, "x_landed", nc.sync, 16)
        self.load_x.do(nc.sync.dma_start(self.x[:, 0:B, :], self.ins["x"]))
        c = self.load("consts", self.small)
        self.ident, self.causal, self.upperT, self.spread = c["ident"], c["causal"], c["upperT"], c["spread"]
        self.rows16, self.rows32, self.prefix = c["rows16"], c["rows32"], c["prefix"]
        self.ones, self.turn8 = c["ones"], c["turn8"]
        self.rows64 = c["rows64"]
        self.row_stats = None
        first_done = self.small.take(32, parts=S)
        self.POOL.do(nc.gpsimd.memset(self.minus_half, -0.5))
        self.POOL.do(nc.gpsimd.memset(self.x_all[:, 0, :], 0.0))
        self.POOL.do(nc.gpsimd.memset(self.x_all[:, B + 1, :], 0.0))
        for lane in self.compute:
            lane.after(self.load_x, self.landed["consts"], self.POOL)
        self.tp(self.bank(0, P, P), self.ident)
        self.copy(first_done[:, 0:16], self.ident[0:S, 0:16], self.ACT)
        self.copy(first_done[:, 16:32], self.ident[0:S, 0:16], self.DVE)

    def l0_attn(self):
        nc, PE, A, V, G = self.nc, self.PE, self.ACT, self.DVE, self.POOL
        GT = 8
        w = self.load("l0a", self.A)
        after_pack = self.A.at
        whh = self.A.take(3, 2, KD, GT * P, dt=BF16)
        raw = self.load("l0a_whh", self.A)["whh"]
        bias = self.load("l0a_bias", self.biases)
        x, xnT = self.x, self.xnT
        xW = Region(self.mem, self.Bm.start, 15360).take(2, S, GT, B)
        wk = self.work.rest()
        hs = wk.take(2, KD, B + 1, S)
        G.do(nc.gpsimd.memset(hs[:, :, :, B, :], 0.0))
        G.do(nc.gpsimd.memset(xnT[:, :, B, :], 0.0))
        xn = wk.take(HALF, D, parts=S)

        for half in range(2):
            self.norm_half(half, x, xn, xnT[:, :, half * HALF:(half + 1) * HALF, :])

        self.need("l0a_whh", V, A, G)
        for l in range(2):
            self.copy(whh[:, 0, l], raw[:, l], A)
            G.after(A)
            self.tt(raw[:, l], raw[:, l], whh[:, 0, l], ALU.subtract, G)
            A.after(G)
            self.copy(whh[:, 1, l], raw[:, l], A)
            G.after(A, G)
            self.tt(whh[:, 2, l], raw[:, l], whh[:, 1, l], ALU.subtract, G)
        self.need("l0a", PE, V)
        self.need("l0a_bias", PE, A, V)

        PE.after(V)
        def input_gates(half):
            free = [V.mark()] * 4
            for n in range(2 * GT):
                l, g = divmod(n, GT)
                ps = self.bank(n % 4, P, HT)
                PE.after(free[n % 4])
                self.project(ps, [w["wih"][:, l, k, g * P:(g + 1) * P] for k in range(KD)],
                             [xnT[:, k, bass.ds(half * HALF, HALF), :] for k in range(KD)])
                dst = xW[:, l, :, g, bass.ds(half * HALF, HALF)].rearrange("p t b -> p b t")
                src = ps.rearrange("p (b t) -> p b t", b=HALF)
                V.after(PE)
                self.ts(dst, src, bias["b_lstm"][:, n:n + 1], None, ALU.add)
                free[n % 4] = V.mark()
        self.prog.loop("l0_input", 2, input_gates)

        gates = wk.take(2, GT, B)
        cell = wk.take(2, KD, B)
        prod = wk.take(2, 2, KD, B)
        tc = wk.take(2, KD, B)
        h = wk.take(2, KD, B)
        left = wk.take(2, KD, B)
        hp = wk.take(2, 2, 3, KD, B, dt=BF16)
        V.do(nc.vector.memset(cell, 0.0))
        V.do(nc.vector.memset(hp, 0.0))
        UN = 8
        V.after(A, V, G)
        PE.after(A, V, G)
        G.after(V)

        def steps(i):
            hmark = [V.mark(), V.mark()]
            pmark = [G.mark(), G.mark()]

            def recur(u, l):
                ps = self.bank(l, P, 3 * GT * B).rearrange("p (s g b) -> p s g b", s=3, g=GT)
                PE.after(hmark[l])
                for g in range(GT):
                    for k in range(KD):
                        for part in range(3):
                            ins = nc.tensor.matmul(
                                ps[:, part:3, g, :], whh[:, part, l, k, g * P:(g + 1) * P],
                                hp[:, u % 2, l, 0:3 - part, k, :],
                                start=(g == 0 and k == 0 and part == 0), stop=(k == KD - 1 and part == 2),
                                skip_group_check=True)
                PE.do(ins)
                return PE.mark()

            def total(l):
                ps = self.bank(l, P, 3 * GT * B).rearrange("p (s g b) -> p s g b", s=3, g=GT)
                V.after(rmark[l])
                V.do(nc.vector.tensor_reduce(gates[:, l].rearrange("p g b -> p (g b)"),
                                             ps.rearrange("p s g b -> p (g b) s"), AX, ALU.add))
                return V.mark()

            def gate(u, l, m_sum):
                t = i * UN + u
                V.after(m_sum)
                self.tt(gates[:, l], gates[:, l],
                        xW[:, l, bass.ds(t, 1), :, :].rearrange("p o g b -> p (o g) b"), ALU.add)
                A.after(V)
                self.act(gates[:, l, 0:6, :], gates[:, l, 0:6, :], ACT.Sigmoid)
                m_sig = A.mark()
                self.act(gates[:, l, 6:8, :], gates[:, l, 6:8, :], ACT.Tanh)
                return m_sig, A.mark()

            def cells(l, m_sig, m_tanh):
                V.after(m_sig, V)
                self.tt(prod[:, l, 0], gates[:, l, 2:4, :], cell[:, l], ALU.mult)
                V.after(m_tanh)
                self.tt(prod[:, l, 1], gates[:, l, 0:2, :], gates[:, l, 6:8, :], ALU.mult)
                V.after(V)
                self.tt(cell[:, l], prod[:, l, 0], prod[:, l, 1], ALU.add)
                A.after(V)
                self.act(tc[:, l], cell[:, l], ACT.Tanh)
                return A.mark()

            def state(u, l, m_tc):
                t, new = i * UN + u, (u + 1) % 2
                V.after(m_tc, pmark[l])
                self.tt(hp[:, new, l, 0], gates[:, l, 4:6, :], tc[:, l], ALU.mult)
                self.tt(h[:, l], gates[:, l, 4:6, :], tc[:, l], ALU.mult)
                V.after(V)
                self.tt(hp[:, new, l, 1], h[:, l], hp[:, new, l, 0], ALU.subtract)
                self.tt(left[:, l], h[:, l], hp[:, new, l, 0], ALU.subtract)
                V.after(V)
                self.tt(hp[:, new, l, 2], left[:, l], hp[:, new, l, 1], ALU.subtract)
                hmark[l] = V.mark()
                G.after(hmark[l])
                self.copy(hs[:, l, :, 0:B, bass.ds(t, 1)].rearrange("p k b o -> p k (b o)"), h[:, l], G)
                pmark[l] = G.mark()

            rmark = [None, None]
            for u in range(UN):
                rmark[0] = recur(u, 0)
                rmark[1] = recur(u, 1)
                m_tc = cells(0, *gate(u, 0, total(0)))
                second_gates = gate(u, 1, total(1))
                state(u, 0, m_tc)
                m_tc = cells(1, *second_gates)
                state(u, 1, m_tc)
        self.prog.loop("l0_lstm", S // UN, steps)
        self.fetch_l0_l1()

        take = self.buffers(Region(self.mem, self.Bm.start, 5000), Region(self.mem, after_pack, self.A.start + 22528 - after_pack))
        xb, r1 = take(KD, S), take(2, S, parts=64)
        o, oT = take(4 * D, parts=S), take(8, S)
        q_mask, bq2m = take(2), take(2, 8)
        bufs = [dict(qm=take(8, 2, S), kT=take(4, S), v=take(D, parts=S)) for _ in range(2)]
        self.settle()
        self.ts(q_mask, self.rows64, 0.125, None, ALU.mult)
        V.after(V)
        for m in range(2):
            self.ts(bq2m[:, m, :], bias["bq2"], q_mask[:, m:m + 1], None, ALU.mult)

        def prologue(b, u):
            def hidden(l, w1, b1):
                def evict(bk):
                    self.ts(r1[:, l, :], bk, bias[b1][0:64, :], 0.0, ALU.add, ALU.max)
                self.via_misc(64, S, lambda bk: self.project(bk, [w[w1][:, k, :] for k in range(KD)],
                                                             [hs[:, l, k, b, :] for k in range(KD)]), evict, V)

            def queries(half):
                PE.after(V)

                def fill(bk):
                    for t in range(4):
                        c = 4 * half + t
                        self.mm(bk[:, t * S:(t + 1) * S], w["wq2"][0:64, c * P:(c + 1) * P], r1[:, 0, :], count=t == 3)

                def evict(bk):
                    ps = bk.rearrange("p (t s) -> p t s", t=4)
                    for m in range(2):
                        self.stt(u["qm"][:, 4 * half:4 * half + 4, m, :], ps, q_mask[:, m:m + 1],
                                 bq2m[:, m, 4 * half:4 * half + 4].unsqueeze(2).broadcast_to([P, 4, S]),
                                 ALU.mult, ALU.add)
                self.via_misc(P, 4 * S, fill, evict, V)

            def keys():
                PE.after(V)

                def fill(bk):
                    for t in range(4):
                        self.mm(bk[:, t * S:(t + 1) * S], w["wk2"][0:64, t * P:(t + 1) * P], r1[:, 1, :], count=t == 3)
                self.via_misc(P, 4 * S, fill, lambda bk: self.tt(
                    u["kT"], bk.rearrange("p (t s) -> p t s", t=4),
                    bias["bk2"].unsqueeze(2).broadcast_to([P, 4, S]), ALU.add), V)

            def stage():
                G.after(PE)
                self.copy(xb, xnT[:, :, b, :], G)
                PE.after(G)
            return ([lambda: hidden(0, "wq1", "bq1"), lambda: hidden(1, "wk1", "bk1"), stage,
                     lambda: queries(0), lambda: queries(1), keys]
                    + self.value_pieces(u["v"].unsqueeze(1), [xb[:, k, :] for k in range(KD)], w["wv"], bias["bv"],
                                        [(0, S)]))

        def epilogue(slot, u):
            xb = self.x_all[:, slot, :]
            return self.output_pieces(o, oT, w["wo"], lambda y: self.tt(xb, xb, y, ALU.add))
        self.attend_all("l0_attn", 16, S, 64, bufs, lambda u, n: [(u["qm"][:, n // 2, n % 2, :], u["kT"][:, n // 4, :])],
                        lambda u, n, c: u["v"][:, 64 * (n // 4):64 * (n // 4) + 64], prologue, epilogue,
                        o=o, take=take, mask=self.causal, o_banks=(6, 7))
        self.fetch_l1_l2()

    def fetch_l0_l1(self):
        upper = Region(self.mem, self.Bm.start + 5000, 15360 - 5000)
        for pack in ("l0x", "l0f", "l1a"):
            self.packs[pack] = self.load(pack, upper, self.compute)
            if pack == "l0f":
                self.layer0_end = upper.at

    def fetch_l1_l2(self):
        a = Region(self.mem, self.a_start, 22528)
        for pack in ("l1x", "l1f", "l2a"):
            self.packs[pack] = self.load(pack, a, self.compute)
        self.extra = a.rest()
        self.extra_b = Region(self.mem, self.Bm.start, 5000)

    def settle(self):
        for lane in self.compute:
            lane.after(*self.compute, self.CTX)

    def buffers(self, *regions):
        regions = [r.rest() for r in regions]

        def take(*dims, dt=F32, parts=P):
            n = int(np.prod(dims))
            n = n if dt is not BF16 else (n + 1) // 2
            for r in regions:
                if r.at + n <= r.end:
                    return r.take(*dims, dt=dt, parts=parts)
            raise AssertionError(("no room for", dims))
        return take

    def load_context(self, i, dst, which="ctxT"):
        src = self.ins[which][i] if isinstance(i, int) else \
            self.ins[which][bass.ds(i, 1)].rearrange("o p n -> (o p) n")
        self.SP.after(*(self.compute if isinstance(i, int) else (self.DVE,)))
        self.CTX.do(self.nc.sync.dma_start(dst, src))

    def l0_xattn(self):
        V = self.DVE
        self.settle()
        w, x = self.packs["l0x"], self.x
        take = self.buffers(self.work, self.extra, self.extra_b)
        xn, xT, ctx = take(D, parts=S), take(KD, S), take(CK)
        o = take(D, parts=S)
        bufs = [dict(q=take(KD, S), kT=take(KD, CK), v=take(CC, D)) for _ in range(2)]
        self.load_context(0, ctx)
        self.need("l0x", self.PE, V, self.ACT)

        def prologue(b, u):
            return ([self.await_context] + self.norm_pieces(x[:, b, :], xn, xT)
                    + self.key_pieces(u["kT"], [ctx], w["wk"], w["bk"])
                    + self.value_pieces(u["v"], [ctx], w["wv"], w["bv"], self.CHUNKS)
                    + self.context_piece(b + 1, ctx)
                    + self.query_pieces(u["q"], None, xT, w["wq"], w["bq"], 1.0, None))

        def epilogue(slot, u):
            def add():
                V.after(V)
                self.tt(self.x_all[:, slot, :], self.x_all[:, slot, :], o, ALU.add)
            return [add]
        self.attend_all("l0_xattn", 1, CK, D, bufs,
                        lambda u, n: [(u["q"][:, k, :], u["kT"][:, k, :]) for k in range(KD)],
                        lambda u, n, c: u["v"][0:CR, c, :], prologue, epilogue, o=o, take=take)

    def cross(self, name, pack, hd, scale, rows):
        PE, A, V = self.PE, self.ACT, self.DVE
        self.settle()
        w, x = self.packs[pack], self.x
        H, per = D // hd, P // hd
        take = self.buffers(self.work, self.extra, self.extra_b)
        xn, xT, ctx, q = take(D, parts=S), take(KD, S), take(CK), take(KD, S)
        o = take(D, parts=S)
        oT, y_sb = take(KD, S), take(D, parts=S)
        bufs = [dict(qm=take(H, S), kT=take(KD, CK), v=take(CC, D)) for _ in range(2)]
        self.load_context(0, ctx)
        self.need(pack, PE, V, A)
        bq = w.get("bq")
        if bq is not None:
            bqs = take(KD)
            self.ts(bqs, bq, scale, None, ALU.mult)
            bq = bqs

        def prologue(b, u):
            return (self.norm_pieces(x[:, b, :], xn, xT)
                    + self.query_pieces(q, u["qm"], xT, w["wq"], bq, scale, rows)
                    + [self.await_context] + self.key_pieces(u["kT"], [ctx], w["wk"], w.get("bk"))
                    + self.value_pieces(u["v"], [ctx], w["wv"], w.get("bv"), self.CHUNKS)
                    + self.context_piece(b + 1, ctx))

        def epilogue(slot, u):
            xb = self.x_all[:, slot, :]

            def finish(y):
                if "bo" in w:
                    V.after(V)
                    self.tt(y_sb, y, w["bo"][0:S, :], ALU.add)
                    V.after(V)
                self.tt(xb, xb, y_sb if "bo" in w else y, ALU.add)
            return self.output_pieces(o, oT, w["wo"], finish)
        self.attend_all(name, H, CK, hd, bufs, lambda u, n: [(u["qm"][:, n, :], u["kT"][:, n // per, :])],
                        None, prologue, epilogue, o=o, take=take, spread=True)

    def l1_attn(self):
        PE, A, V = self.PE, self.ACT, self.DVE
        self.settle()
        w, x, H, hd = self.packs["l1a"], self.x, 16, 16
        take = self.buffers(self.work, self.extra, self.extra_b)
        xn, xT, q = take(D, parts=S), take(KD, S), take(KD, S)
        o, oT = take(D, parts=S), take(KD, S)
        bqs, y_sb = take(KD), take(D, parts=S)
        bufs = [dict(qm=take(H, S), kT=take(KD, S), v=take(1, D, parts=S), near=take(D, parts=S)) for _ in range(2)]
        self.need("l1a", PE, V, A)
        self.ts(bqs, w["bq"], 0.25, None, ALU.mult)

        def prologue(b, u):
            src = [xT[:, k, :] for k in range(KD)]

            def near():
                PE.after(V)
                self.via_misc(S, D, lambda bk: self.mm(bk, self.spread[0:S, :], u["v"][:, 0, :], count=True),
                              lambda bk: self.copy(u["near"], bk, V), V)
            return (self.norm_pieces(x[:, b, :], xn, xT) + self.key_pieces(u["kT"], src, w["wk"], w["bk"], 2)
                    + self.query_pieces(q, u["qm"], xT, w["wq"], bqs, 0.25, self.rows16)
                    + self.value_pieces(u["v"], src, w["wv"], w["bv"], [(0, S)]) + [near])

        def epilogue(slot, u):
            xb = self.x_all[:, slot, :]

            def finish(y):
                V.after(V)
                self.tt(y_sb, y, w["bo"][0:S, :], ALU.add)
                V.after(V)
                self.tt(xb, xb, y_sb, ALU.add)
            return self.output_pieces(o, oT, w["wo"], finish)
        self.attend_all("l1_attn", H, S, hd, bufs, lambda u, n: [(u["qm"][:, n, :], u["kT"][:, n // 8, :])],
                        None, prologue, epilogue, o=o, take=take, spread=True,
                        share=0.6, plus=lambda u: u["near"])

    def l1_xattn(self):
        self.cross("l1_xattn", "l1x", 16, 0.25, self.rows16)

    def l3_xattn(self):
        self.cross("l3_xattn", "l3x", 16, 0.25, self.rows16)

    def norm_half(self, half, src, xn, xT):
        V, G, PE, st, nc = self.DVE, self.POOL, self.PE, self.stats4, self.nc
        batch = lambda j: src[:, bass.ds(half * HALF + j, 1), :].rearrange("p o d -> p (o d)")
        V.after(V)
        for j in range(HALF):
            V.do(nc.vector.bn_stats(st[:, j, 0:6], batch(j)))
        V.after(V)
        V.do(nc.vector.memset(st[:, 0, 10:11], 0.0))
        for j in range(HALF):
            V.do(nc.vector.bn_aggr(st[:, j, 6:8], st[:, j, 0:6]))
        V.after(V)
        self.ts(st[:, :, 8], st[:, :, 7], EPS, None, ALU.add)
        G.after(V)
        self.tt(st[:, :, 9], st[:, :, 8], self.minus_half[0:S, :].broadcast_to([S, HALF]), ALU.pow, G)
        V.after(G)
        ready = []
        for j in range(HALF):
            self.ts(xn[:, j, :], batch(j), st[:, j, 6:7], st[:, j, 9:10], ALU.subtract, ALU.mult)
            ready.append(V.mark())
        banks = [self.bank(j, P, 2 * KD * S) for j in range(HALF // 2)]
        for j in range(HALF):
            PE.after(ready[j])
            for k in range(KD):
                at = ((j % 2) * KD + k) * S
                self.tp(banks[j // 2][:, at:at + S], xn[:, j, k * P:(k + 1) * P], k == KD - 1 and j % 2 == 1)
            if j % 2:
                V.after(PE)
                self.copy(xT[:, :, j - 1:j + 1, :], banks[j // 2].rearrange("p (j k s) -> p k j s", j=2, k=KD), V)

    def tile_stream(self, n, banks, fill, drain, free):
        PE = self.PE
        for u in range(n):
            bk = banks[u % len(banks)]
            if bk in free:
                PE.after(*free[bk])
            fill(u, bk)
            free[bk] = drain(u, bk)

    def gated(self, tiles, xT, wg, wu, h, g_sb, free, scales=None):
        PE, A, V = self.PE, self.ACT, self.DVE
        flat = [xT[:, k].rearrange("p b s -> p (b s)") for k in range(KD)]

        def fill(u, bk):
            for o, wt in ((0, wg), (1, wu)):
                self.project(self.bank(bk + o, P, HT), [wt[:, k, u * P:(u + 1) * P] for k in range(KD)], flat)

        def drain(u, bk):
            A.after(PE, V)
            sg = {} if scales is None else dict(scale=scales[0][:, u:u + 1])
            self.act(g_sb[:, u % 2, :], self.bank(bk, P, HT), ACT.Silu, **sg)
            V.after(A, PE)
            if scales is None:
                self.tt(h[:, u, :], g_sb[:, u % 2, :], self.bank(bk + 1, P, HT), ALU.mult)
            else:
                self.stt(h[:, u, :], self.bank(bk + 1, P, HT), scales[1][:, u:u + 1], g_sb[:, u % 2, :],
                         ALU.mult, ALU.mult)
            return (A.mark(), V.mark())
        self.tile_stream(tiles, (0, 2, 4), fill, drain, free)

    def down(self, half, h, w, free, finish):
        PE, V = self.PE, self.DVE
        PE.after(V)
        tiles = w.shape[1]

        def fill(j, bk):
            self.project(self.bank(bk, S, D), [h[:, t, j * S:(j + 1) * S] for t in range(tiles)],
                         [w[:, t, :] for t in range(tiles)])

        def drain(j, bk):
            V.after(PE)
            finish(j, bass.ds(half * HALF + j, 1), self.bank(bk, S, D))
            return (V.mark(),)
        self.tile_stream(HALF, (6, 7), fill, drain, free)

    def xs(self, a, at):
        return a[:, at, :].rearrange("p o d -> p (o d)")

    def l0_ffn(self):
        PE, A, V, G = self.PE, self.ACT, self.DVE, self.POOL
        self.settle()
        wi, x = self.packs["l0f"], self.x
        take = self.buffers(self.work, self.extra, self.extra_b)
        xn, xT = take(HALF, D, parts=S), take(KD, HALF, S)
        h, g_sb = take(6, HT), take(2, HT)
        self.need("l0f", A, V, G)
        w = {}
        for name, lane in (("wg", A), ("wu", V), ("wd", G)):
            w[name] = wi[name].bitcast(F32)
            if lane is A:
                self.act(w[name], wi[name], ACT.Copy, scale=1.0 / 127.0)
            else:
                self.ts(w[name], wi[name], 1.0 / 127.0, None, ALU.mult, lane=lane)
        PE.after(A, V, G)

        def half_turn(i):
            free = {}
            PE.after(V, A)
            self.norm_half(i, x, xn, xT)
            PE.after(V)
            self.gated(6, xT, w["wg"], w["wu"], h, g_sb, free)
            self.down(i, h, w["wd"], free,
                      lambda j, at, y: self.tt(self.xs(x, at), self.xs(x, at), y, ALU.add))
        self.prog.loop("l0_ffn", 2, half_turn)
        self.free_layer0()

    def free_layer0(self):
        self.extra_b = Region(self.mem, self.Bm.start, self.layer0_end - self.Bm.start)

    def l1_ffn(self):
        nc, PE, A, V, G = self.nc, self.PE, self.ACT, self.DVE, self.POOL
        self.settle()
        self.fetch_l2x()
        w, x, xnT = self.packs["l1f"], self.x, self.xnT
        E, TOP, CAP = 8, 4, 140
        take = self.buffers(self.work, self.extra)
        xn, xh, logits = take(HALF, D, parts=S), take(KD, HALF, S), take(B, E + 1, parts=S)
        free = {}
        self.need("l1f", PE)

        def route(i):
            PE.after(V, A)
            V.after(PE, G)
            self.norm_half(i, x, xn, xh)
            PE.after(V)
            for j in range(HALF):
                self.project(self.bank(4, S, HALF * (E + 1))[:, j * (E + 1):(j + 1) * (E + 1)],
                             [xh[:, k, j, :] for k in range(KD)], [w["router"][:, k, :] for k in range(KD)], j == HALF - 1)
            V.after(PE)
            self.copy(logits[:, bass.ds(i * HALF, HALF), :],
                      self.bank(4, S, HALF * (E + 1)).rearrange("p (j e) -> p j e", j=HALF), V)
            G.after(V)
            self.copy(xnT[:, :, bass.ds(i * HALF, HALF), :], xh, G)
            V.after(G)
        self.prog.loop("l1_router", 2, route)

        e3 = lambda: take(B, E, parts=S)
        e1 = lambda: take(B, parts=S)
        wide = lambda a: a.unsqueeze(2).broadcast_to([S, B, E])
        s, rest, t1, t2, t3, pick, rw = logits[:, :, 0:E], e3(), e3(), e3(), e3(), e3(), e3()
        size, prob, cum, a1, first, total = e3(), e1(), e1(), e1(), e1(), e1()
        turn, weight = self.turn8[0:S, :].unsqueeze(1).broadcast_to([S, B, E]), take(B, E + 1, parts=S)

        def do(f, *a, **k):
            V.after(V)
            f(*a, **k)

        def red(out, a, op):
            V.after(V)
            V.do(nc.vector.tensor_reduce(out, a, AX, op))

        def exp(out, a):
            A.after(V)
            self.act(out, a, ACT.Exp)
            V.after(A)
        do(self.copy, rest, s, V)
        do(self.ts, rw, s, 0.0, None, ALU.mult)
        do(self.ts, t1, s, -1.0, None, ALU.mult)
        do(self.tt, size, s, t1, ALU.max)
        for r in range(TOP):
            red(a1, rest, ALU.max)
            if r == 0:
                do(self.copy, first, a1, V)
                do(self.tt, t1, s, wide(first), ALU.subtract)
                exp(t1, t1)
                red(total, t1, ALU.add)
                do(lambda: V.do(nc.vector.reciprocal(total, total)))
            do(self.tt, t1, rest, wide(a1), ALU.is_equal)
            do(self.tt, t1, t1, turn, ALU.mult)
            red(prob, t1, ALU.max)
            do(self.tt, pick, t1, wide(prob), ALU.is_equal)
            do(self.ts, prob, a1, -1.0, None, ALU.mult)
            do(self.tt, prob, prob, a1, ALU.max)
            do(self.tt, t1, size, wide(prob), ALU.max)
            do(self.ts, t1, t1, 0.2, None, ALU.mult)
            do(self.tt, t2, wide(a1), s, ALU.subtract)
            do(self.tt, t2, t2, t1, ALU.is_le)
            do(self.tt, t3, rest, wide(a1), ALU.subtract)
            exp(t3, t3)
            do(self.tt, t3, t3, t2, ALU.mult)
            red(prob, t3, ALU.add)
            do(lambda: V.do(nc.vector.reciprocal(prob, prob)))
            if r:
                do(self.ts, t1[:, :, 0], cum, 0.75, None, ALU.is_lt)
                do(self.tt, prob, prob, t1[:, :, 0], ALU.mult)
            do(self.tt, t1, pick, wide(prob), ALU.mult)
            do(self.tt, rw, rw, t1, ALU.add)
            if r < TOP - 1:
                do(self.ts, t1, pick, MASKED, None, ALU.mult)
                do(self.tt, rest, rest, t1, ALU.add)
                do(self.tt, a1, a1, first, ALU.subtract)
                exp(a1, a1)
                do(self.tt, a1, a1, total, ALU.mult)
                if r:
                    do(self.tt, cum, cum, a1, ALU.add)
                else:
                    do(self.copy, cum, a1, V)
        red(a1, rw, ALU.add)
        do(lambda: V.do(nc.vector.reciprocal(a1, a1)))
        do(self.tt, rw, rw, wide(a1), ALU.mult)
        do(self.ts, t1, rw, 0.0, None, ALU.is_gt)
        PE.after(V)
        flat = t1.rearrange("p b e -> p (b e)")
        self.mm(self.bank(2, S, B * E), self.prefix[0:S, :], flat)
        self.mm(self.bank(3, S, B * E), self.ones[0:S, 0:S], flat, count=True)
        V.after(PE)
        do(self.copy, t2.rearrange("p b e -> p (b e)"), self.bank(2, S, B * E), V)
        do(self.copy, t3.rearrange("p b e -> p (b e)"), self.bank(3, S, B * E), V)
        for b in range(1, B):
            do(self.tt, t2[:, b, :], t2[:, b, :], t3[:, b - 1, :], ALU.add)
            if b < B - 1:
                do(self.tt, t3[:, b, :], t3[:, b, :], t3[:, b - 1, :], ALU.add)
        do(self.ts, t2, t2, float(CAP), None, ALU.is_le)
        do(self.tt, t1, t1, t2, ALU.mult)
        do(self.ts, weight[:, :, 0:E], t1, -1.0, -MASKED, ALU.add, ALU.mult)
        do(self.tt, weight[:, :, 0:E], weight[:, :, 0:E], s, ALU.add)
        do(self.copy, weight[:, :, E:E + 1], logits[:, :, E:E + 1], V)
        red(a1, weight, ALU.max)
        w9 = lambda a: a.unsqueeze(2).broadcast_to([S, B, E + 1])
        do(self.tt, weight, weight, w9(a1), ALU.subtract)
        exp(weight, weight)
        red(a1, weight, ALU.add)
        do(lambda: V.do(nc.vector.reciprocal(a1, a1)))
        do(self.tt, weight, weight, w9(a1), ALU.mult)
        red(a1, weight[:, :, 0:E], ALU.add)
        do(self.tt, rw, rw, wide(a1), ALU.mult)
        do(self.tt, weight[:, :, 0:E], rw, t1, ALU.mult)

        h, g_sb, wt = take(4, HT), take(2, HT), take(HALF, E + 1, parts=S)
        self.settle()

        def experts(i):
            free = {}
            V.after(V)
            self.copy(wt, weight[:, bass.ds(i * HALF, HALF), :], V)
            flat = [xnT[:, k, bass.ds(i * HALF, HALF), :].rearrange("p b s -> p (b s)") for k in range(KD)]
            PE.after(V, A)

            def unit(u, bk):
                wg, wu, c = (w["dg"], w["du"], u) if u < E else (w["sg"], w["su"], u - E)
                for o, ww in ((0, wg), (1, wu)):
                    self.project(self.bank(bk + o, P, HT), [ww[:, k, c * P:(c + 1) * P] for k in range(KD)], flat)

            def activate(u, bk):
                slot = u % 4
                A.after(PE, V)
                self.act(g_sb[:, u % 2, :], self.bank(bk, P, HT), ACT.Silu)
                V.after(A, PE)
                self.tt(h[:, slot, :], g_sb[:, u % 2, :], self.bank(bk + 1, P, HT), ALU.mult)
                return (A.mark(), V.mark())

            def give(e):
                tiles = [e % 4] if e < E else [0, 1, 2, 3]
                dd = [w["dd"][:, e, :]] if e < E else [w["sd"][:, t, :] for t in range(4)]

                def fill(j, bk):
                    self.project(self.bank(bk, S, D), [h[:, t, j * S:(j + 1) * S] for t in tiles], dd)

                def drain(j, bk):
                    V.after(PE, V)
                    xb = self.xs(x, bass.ds(i * HALF + j, 1))
                    self.stt(xb, self.bank(bk, S, D), wt[:, j, e:e + 1], xb, ALU.mult, ALU.add)
                    return (V.mark(),)
                self.tile_stream(HALF, (6, 7), fill, drain, free)
            ready = {}
            for u in range(E + 4 + 1):
                if u < E + 4:
                    self.tile_stream(1, ((0, 2, 4)[u % 3],), lambda _, bk: unit(u, bk),
                                     lambda _, bk: activate(u, bk), free)
                    ready[u] = V.mark()
                if 1 <= u <= E:
                    PE.after(ready[u - 1])
                    give(u - 1)
            PE.after(V)
            give(E)
        self.prog.loop("l1_experts", 2, experts)

    def fetch_l2x(self):
        self.packs["l2x"] = self.load("l2x", Region(self.mem, self.Bm.start, 15360), self.compute)

    def l2_attn(self):
        PE, A, V, G = self.PE, self.ACT, self.DVE, self.POOL
        self.settle()
        w, x, H, KV = self.packs["l2a"], self.x, 8, 4
        take = self.buffers(self.work, self.extra)
        xn, xT, o, oT = take(D, parts=S), take(KD, S), take(H * P, parts=S), take(H, S)
        tmp = take(2, 4, S)
        bufs = [dict(q=take(H, S), kT=take(KV, S), v=take(1, KV * P, parts=S)) for _ in range(2)]
        self.need("l2a", PE)
        self.SP.after(*self.compute)
        rb = Region(self.mem, self.biases.start, 2700)
        rope = self.load("rope", rb)
        self.need("rope", V)

        cs = lambda n: rope[n].unsqueeze(1).broadcast_to([P, 4, S])

        def prologue(b, u):
            def rotary(ww, c0, dst, cos, sin, slot):
                def fill(bk):
                    for h in range(4):
                        c = c0 + h
                        self.project(bk[:, h * S:(h + 1) * S], [ww[:, k, c * P:(c + 1) * P] for k in range(KD)],
                                     [xT[:, k, :] for k in range(KD)], h == 3)

                def drain(bk):
                    z = bk.rearrange("p (h s) -> p h s", h=4)
                    half = P // 2
                    for to, at in ((0, half), (half, 0)):
                        self.tt(tmp[to:to + half, slot], z[at:at + half],
                                rope[sin][at:at + half, :].unsqueeze(1).broadcast_to([half, 4, S]), ALU.mult)
                    self.tt(dst, z, cs(cos), ALU.mult)
                V.after(*self.since(("tmp", slot), G))
                self.via_misc(P, 4 * S, fill, drain, V)
                G.after(V)
                self.tt(dst, dst, tmp[:, slot], ALU.add, G)
                self.marks[("tmp", slot)] = [G.mark()]
            return (self.norm_pieces(x[:, b, :], xn, xT) + [lambda: PE.after(V)]
                    + [lambda: rotary(w["wq"], 0, u["q"][:, 0:4], "cosq", "sinq", 1),
                       lambda: rotary(w["wq"], 4, u["q"][:, 4:8], "cosq", "sinq", 0),
                       lambda: rotary(w["wk"], 0, u["kT"], "cos", "sin", 1)]
                    + self.value_pieces(u["v"], [xT[:, k, :] for k in range(KD)], w["wv"], None, [(0, S)]))

        def epilogue(slot, u):
            xb = self.x_all[:, slot, :]
            return self.output_pieces(o, oT, w["wo"], lambda y: self.tt(xb, xb, y, ALU.add))
        self.attend_all("l2_attn", H, S, P, bufs, lambda u, n: [(u["q"][:, n, :], u["kT"][:, n // 2, :])],
                        lambda u, n, c: u["v"][:, 0, P * (n // 2):P * (n // 2) + P], prologue, epilogue,
                        o=o, take=take, mask=self.causal, o_banks=(6, 7))
        self.fetch_l2f()

    def fetch_l2f(self):
        a = Region(self.mem, self.a_start, 22528)
        self.packs["l2f"] = self.load("l2f", a, self.compute)
        self.a_hi = a.rest()

    def fetch_l2f_rest(self):
        self.packs["l2f2"] = self.load("l2f2", Region(self.mem, self.a_hi.start, 8192), self.compute)

    def fetch_l3(self):
        b = Region(self.mem, self.Bm.start, 15360)
        for pack in ("l3a", "l3x", "l3f"):
            self.packs[pack] = self.load(pack, b, self.compute)
        self.b_hi = b.rest()
        self.extra = self.extra_b = Region(self.mem, self.a_start, 22528)

    def l2_xattn(self):
        PE, A, V, G = self.PE, self.ACT, self.DVE, self.POOL
        self.settle()
        w, x, xnT = self.packs["l2x"], self.x, self.xnT
        H, hd, HT4 = 16, 32, 4
        scale = float(np.float32(hd) ** np.float32(-0.5))
        c = self.load("l2x_rows", Region(self.mem, self.biases.start, 2700), self.compute)
        take = self.buffers(self.work, self.a_hi)
        acc_all = take(B + 2, D, parts=S)
        acc = acc_all[:, 1:, :]
        V.do(self.nc.vector.memset(acc[:, B, :], 0.0))
        xn, xT, yT, xo = take(D, parts=S), take(KD, S), take(KD, S), take(D, parts=S)
        q, o, oT = take(HT4, S), take(512, parts=S), take(HT4, S)
        bufs = [dict(xm=take(D, parts=S), qm=take(H, S), kT=take(HT4, S), v=take(1, 512, parts=S)) for _ in range(2)]
        self.need("l2x", PE, V, A)
        self.need("l2x_rows", V, A)
        row = lambda n: c["rows"][0:S, n, :]
        f = c["cols"]

        def col(n, k=KD):
            return f[:, n:n + k]

        def affine(a, g, b):
            self.tt(a, a, row(g), ALU.mult)
            V.after(V)
            self.tt(a, a, row(b), ALU.add)
            V.after(V)

        def close(slot, w1, base, lib, ln3):
            def finish(y):
                V.after(V)
                self.tt(xo, y, row(lib), ALU.add)
                V.after(V)
                self.tt(xo, xo, base, ALU.add)
                V.after(V)
                self.tt(acc_all[:, slot, :], xo, base, ALU.add)
            return (self.output_pieces(o, oT, w1, finish)
                    + self.norm_pieces(xo, xl, xnT[:, :, slot, :], col(ln3), col(ln3 + 2)))

        def clear(bufs):
            V.do(self.nc.vector.memset(bufs[1]["xm"], 0.0))
            V.after(V)

        def enter(src, dst, g, b):
            def begin():
                V.after(V)
                self.norm_begin(src)

            def end():
                self.norm_end(src, dst)
                V.after(V)
                affine(dst, g, b)
            return [begin, end]

        def prologue1(b, u):
            src = [yT[:, k, :] for k in range(KD)]
            return (enter(x[:, b, :], u["xm"], 0, 1) + self.norm_pieces(u["xm"], xn, xT, col(0), col(2), (yT, col(4), col(6)))
                    + self.query_pieces(q, u["qm"], xT, w["a1_wq"], None, scale, self.rows32)
                    + self.key_pieces(u["kT"], src, w["a1_wk"], None, 4)
                    + self.value_pieces(u["v"], src, w["a1_wv"], None, [(0, S)]))
        xl = take(D, parts=S)
        clear(bufs)
        self.attend_all("l2_block1", H, S, hd, bufs, lambda u, n: [(u["qm"][:, n, :], u["kT"][:, n // 4, :])],
                        None, prologue1, lambda slot, u: close(slot, w["a1_li1"], u["xm"], 4, 8),
                        o=o, take=take, keepT=self.upperT, spread=True)
        self.settle()
        self.gelu_block("l2_block1_mlp", w["a1_li2"], w["a1_li3"], f[:, 32:40], row(5), acc, (w, take))

        self.settle()
        take = self.buffers(Region(self.mem, self.work.at + (B + 2) * D, self.work.end - self.work.at - (B + 2) * D), self.a_hi,
                            Region(self.mem, self.Bm.start, 8192))
        xn, xT, xo, xl = take(D, parts=S), take(KD, S), take(D, parts=S), take(D, parts=S)
        q = take(HT4, S)
        o, oT, ctx, cn, cT = take(512, parts=S), take(HT4, S), take(CC, P), take(CC, P), take(CK)
        bufs = [dict(xm=take(D, parts=S), qm=take(H, S), kT=take(HT4, CK), v=take(CC, 512)) for _ in range(2)]
        cst = take(CC, 12)
        flat = ctx[0:CR].rearrange("p c n -> p (c n)")
        self.load_context(0, flat, "ctxN")

        def prologue2(b, u):
            def context_stats():
                V.after(V)
                for k in range(CC):
                    V.do(self.nc.vector.bn_stats(cst[0:CR, k, 0:6], ctx[0:CR, k, :]))
                V.after(V)
                V.do(self.nc.vector.memset(cst[0:CR, 0, 10:11], 0.0))
                for k in range(CC):
                    V.do(self.nc.vector.bn_aggr(cst[0:CR, k, 6:8], cst[0:CR, k, 0:6]))
                V.after(V)
                self.ts(cst[0:CR, :, 8], cst[0:CR, :, 7], EPS, None, ALU.add)
                G.after(V)
                self.tt(cst[0:CR, :, 9], cst[0:CR, :, 8], self.minus_half[0:CR, :].broadcast_to([CR, CC]), ALU.pow, G)

            def context_norm():
                V.after(G)
                for k in range(CC):
                    self.ts(cn[0:CR, k, :], ctx[0:CR, k, :], cst[0:CR, k, 6:7], cst[0:CR, k, 9:10],
                            ALU.subtract, ALU.mult)

            def context_turn():
                PE.after(V)
                self.via_misc(P, CK, lambda bk: [self.tp(bk[:, k * CR:(k + 1) * CR], cn[0:CR, k, :], k == CC - 1)
                                                 for k in range(CC)],
                              lambda bk: self.ts(cT, bk, f[:, 20:21], f[:, 21:22], ALU.mult, ALU.add), V)
                self.marks["source"] = [V.mark()]
            return (enter(acc[:, b, :], u["xm"], 2, 3)
                    + [self.await_context, context_stats] + self.norm_pieces(u["xm"], xn, xT, col(12), col(14))
                    + [context_norm, context_turn]
                    + self.query_pieces(q, u["qm"], xT, w["a2_wq"], None, scale, self.rows32)
                    + self.context_piece(b + 1, flat, "ctxN")
                    + self.key_pieces(u["kT"], [cT], w["a2_wk"], None)
                    + self.value_pieces(u["v"], [cT], w["a2_wv"], None, self.CHUNKS))
        clear(bufs)
        self.attend_all("l2_block2", H, CK, hd, bufs, lambda u, n: [(u["qm"][:, n, :], u["kT"][:, n // 4, :])],
                        None, prologue2, lambda slot, u: close(slot, w["a2_li1"], u["xm"], 6, 16),
                        o=o, take=take, spread=True)
        self.settle()
        for half in range(2):
            self.tt(x[:, half * HALF:(half + 1) * HALF, :], x[:, half * HALF:(half + 1) * HALF, :],
                    acc[:, half * HALF:(half + 1) * HALF, :], ALU.add)
        V.after(V)
        self.gelu_block("l2_block2_mlp", w["a2_li2"], w["a2_li3"], f[:, 40:48], row(7), x, (w, take))

    def gelu_block(self, name, w2, w3, b2, b3, into, _):
        PE, A, V = self.PE, self.ACT, self.DVE
        xnT = self.xnT
        h = Region(self.mem, self.a_hi.start, 8192).take(8, HT)

        def turn(i):
            free = {}
            PE.after(V, A)
            flat = [xnT[:, k, bass.ds(i * HALF + 1, HALF), :].rearrange("p b s -> p (b s)") for k in range(KD)]

            def fill(u, bk):
                self.project(self.bank(bk, P, HT), [w2[:, k, u * P:(u + 1) * P] for k in range(KD)], flat)

            def drain(u, bk):
                A.after(PE)
                self.act(h[:, u, :], self.bank(bk, P, HT), ACT.Gelu, bias=b2[:, u:u + 1], scale=1.0)
                return (A.mark(),)
            self.tile_stream(8, (0, 1, 2, 3), fill, drain, free)
            PE.after(A)

            def finish(j, at, y):
                dst = self.xs(into, at)
                V.after(V)
                self.tt(dst, dst, y, ALU.add)
                V.after(V)
                self.tt(dst, dst, b3, ALU.add)
            self.down(i, h, w3, free, finish)
        self.prog.loop(name, 2, turn)

    def l2_ffn(self):
        PE, A, V, G = self.PE, self.ACT, self.DVE, self.POOL
        self.settle()
        self.fetch_l2f_rest()
        self.fetch_l3()
        w, w2, x = self.packs["l2f"], self.packs["l2f2"], self.x
        s = self.load("l2f_scales", Region(self.mem, self.biases.start, 2700), self.compute)
        take = self.buffers(self.b_hi, self.work)
        h1, h2 = take(8, HT), take(8, HT)
        xT, g_sb, xn = self.xnT[:, :, 0:HALF, :], take(2, HT), take(HALF, D, parts=S)
        self.need("l2f", PE)
        self.need("l2f_scales", A, V)

        def turn(i):
            free = {}
            PE.after(V, A)
            self.norm_half(i, x, xn, xT)
            PE.after(V)
            self.gated(8, xT, w["w1"], w["w2"], h1, g_sb, free, (s["s1"], s["s2"]))

            def dense(src, dst, ww, sc):
                PE.after(A, V)

                def fill(u, bk):
                    self.project(self.bank(bk, P, HT), [ww[:, k, u * P:(u + 1) * P] for k in range(8)],
                                 [src[:, k, :] for k in range(8)])

                def drain(u, bk):
                    A.after(PE)
                    self.act(dst[:, u, :], self.bank(bk, P, HT), ACT.Gelu, scale=sc[:, u:u + 1])
                    return (A.mark(),)
                self.tile_stream(8, (0, 1, 2, 3, 4, 5), fill, drain, free)
            dense(h1, h2, w["h1"], s["h1s"])
            self.need("l2f2", PE)
            dense(h2, h1, w2["h2"], s["h2s"])
            PE.after(A)

            def finish(j, at, y):
                V.after(V)
                self.tt(xn[:, 0, :], y, s["s3"][0:S, :], ALU.mult)
                V.after(V)
                self.tt(self.xs(x, at), self.xs(x, at), xn[:, 0, :], ALU.add)
            self.down(i, h1, w["w3"], free, finish)
        self.prog.loop("l2_ffn", 2, turn)

    def l3_attn(self):
        nc, PE, A, V, G = self.nc, self.PE, self.ACT, self.DVE, self.POOL
        self.settle()
        w, x = self.packs["l3a"], self.x
        H, DEPTH, hd = 8, 5, 32
        R = H * DEPTH
        take = self.buffers(self.work, self.extra)
        xn, xT = take(D, parts=S), take(KD, S)
        o, oT, bp = take(D, parts=S), take(KD, S), take(1)
        bufs = [dict(left=take(S), right=take(R, S), v=take(1, D, parts=S)) for _ in range(2)]
        self.need("l3a", PE, V, A)
        self.ts(bp, w["bp"], 0.5, None, ALU.mult)
        for u in bufs:
            V.do(nc.vector.memset(u["left"], 0.0))
            V.do(nc.vector.memset(u["right"], 0.0))
            V.after(V, G)
            V.do(nc.vector.memset(u["left"][64:65, :], 1.0))
            V.do(nc.vector.memset(u["right"][64:65], 0.5))
        V.after(V)

        def prologue(b, u):
            src = [xT[:, k, :] for k in range(KD)]

            def paths():
                PE.after(V)
                self.via_misc(R, S, lambda bk: self.project(bk, [w["wp"][:, k, :] for k in range(KD)], src),
                              lambda bk: self.act(u["left"][0:R, :], bk, ACT.Tanh, bias=bp[0:R, :], scale=0.5), A)

            def spread():
                scored = V.mark()
                for g, lane in ((0, V), (1, G)):
                    lane.after(A, scored)
                    for d in range(DEPTH):
                        at = d * H + 4 * g
                        self.tt(u["right"][0:R, at:at + 4, :],
                                u["left"][0:R, :].unsqueeze(1).broadcast_to([R, 4, S]),
                                w["half_eye"][0:R, at:at + 4].unsqueeze(2).broadcast_to([R, 4, S]), ALU.mult, lane)
            return (self.norm_pieces(x[:, b, :], xn, xT) + [paths, spread]
                    + self.value_pieces(u["v"], src, w["wv"], None, [(0, S)]))

        def fill(u, g, dst):
            for d in range(DEPTH - 1, -1, -1):
                bk = (0, 1, 6)[d % 3]
                if self.marks.get("ready"):
                    PE.after(*self.marks["ready"])
                PE.after(*self.since(("s", bk), V))
                at = d * H + 4 * g
                self.mm(self.bank(bk, S, 4 * S), u["left"], u["right"][:, at:at + 4, :], count=True)
                V.after(PE, V)
                agree = self.bank(bk, S, 4 * S).rearrange("p (h s) -> p h s", h=4)
                if d == DEPTH - 1:
                    self.copy(dst, agree, V)
                else:
                    self.stt(dst, dst, 1.0, agree, ALU.add, ALU.mult)
                self.marks[("s", bk)] = [V.mark()]
                if d:
                    self.side()
            V.after(V)
            self.stt(dst, dst, 1.0 / DEPTH, self.causal[0:S, :].unsqueeze(1).broadcast_to([S, 4, S]),
                     ALU.mult, ALU.add)

        def epilogue(slot, u):
            xb = self.x_all[:, slot, :]
            return self.output_pieces(o, oT, w["wo"], lambda y: self.tt(xb, xb, y, ALU.add))
        self.attend_all("l3_attn", H, S, hd, bufs, None, None, prologue, epilogue,
                        o=o, take=take, fill=fill, spread=True)

    def quantize(self, src, gs, dst, y, t, sc, blocks):
        V, nc = self.DVE, self.nc
        p = src.shape[0]
        b3 = lambda a: a.rearrange("p (n k) -> p n k", k=16)
        wide = lambda a: a.unsqueeze(2).broadcast_to([p, blocks, 16])
        top, s8, c8 = sc[:, 0], sc[:, 1], sc[:, 2]
        V.after(V)
        V.do(nc.vector.tensor_reduce(top, b3(src), AX, ALU.max, apply_absolute_value=True))
        V.after(V)
        self.ts(top, top, 1.0 / 6.0, gs, ALU.mult, ALU.mult)
        V.after(V)
        self.ts(top, top, 448.0, None, ALU.min)
        V.after(V)
        self.ts(c8.bitcast(I32), top.bitcast(I32), 0x7F800000, None, ALU.bitwise_and)
        V.after(V)
        self.ts(c8, c8, 2.0 ** -6, 1.5 * 2.0 ** 20, ALU.max, ALU.mult)
        V.after(V)
        self.tt(s8, top, c8, ALU.add)
        V.after(V)
        self.tt(s8, s8, c8, ALU.subtract)
        V.after(V)
        self.ts(c8, s8, 2.0 ** -9, None, ALU.max)
        V.after(V)
        V.do(nc.vector.reciprocal(c8, c8))
        V.after(V)
        self.ts(c8, c8, gs, 1.0 + 2.0 ** -22, ALU.mult, ALU.mult)
        V.after(V)
        self.tt(b3(y), b3(src), wide(c8), ALU.mult)
        V.after(V)
        self.ts(y, y, 6.0, -6.0, ALU.min, ALU.max)
        V.after(V)
        self.ts(t.bitcast(I32), y.bitcast(I32), 0x7F800000, None, ALU.bitwise_and)
        V.after(V)
        self.ts(t, t, 1.0, 1.5 * 2.0 ** 22, ALU.max, ALU.mult)
        V.after(V)
        self.tt(y, y, t, ALU.add)
        V.after(V)
        self.tt(y, y, t, ALU.subtract)
        V.after(V)
        self.tt(b3(dst), b3(y), wide(s8), ALU.mult)

    def tp16(self, src, dst, n, bank, lane):
        PE = self.PE
        rows = src.shape[0]
        PE.after(self.DVE, self.ACT)
        ps = self.banks[:, bank, :].bitcast(BF16)[:, 0:n * rows].rearrange("p (n r) -> p n r", n=n)
        for k in range(n):
            ins = self.nc.tensor.transpose(ps[:, k, :], src[:, k * P:(k + 1) * P], self.ident16[0:rows, 0:rows])
        PE.do(ins)
        lane.after(PE)
        self.copy(dst, ps, lane)

    def l3_ffn(self):
        nc, PE, A, V, G = self.nc, self.PE, self.ACT, self.DVE, self.POOL
        self.settle()
        w, x = self.packs["l3f"], self.x
        take = self.buffers(self.work, self.extra)
        self.ident16 = take(P, dt=BF16)
        self.copy(self.ident16, self.ident, V)
        self.need("l3f", V, A, G)
        HID = 1024
        big, gs = take(3), take(3)
        y, t, sc = take(2048), take(2048), take(3, P)
        wq = take(2048, dt=BF16)
        wT = {"gate": take(KD, HID, dt=BF16), "up": take(KD, HID, dt=BF16), "down": take(8, D, dt=BF16)}
        for n, name in enumerate(("gate", "up", "down")):
            V.do(nc.vector.tensor_reduce(big[:, n:n + 1], w[name].rearrange("p o i -> p (o i)"), AX, ALU.max,
                                         apply_absolute_value=True))
        G.after(V)
        top = take(3)
        G.do(nc.gpsimd.partition_all_reduce(top, big, P, bass.bass_isa.ReduceOp.max))
        V.after(G)
        V.do(nc.vector.reciprocal(gs, top))
        V.after(V)
        self.ts(gs, gs, 448.0 * 6.0, None, ALU.mult)
        inv = take(3)
        V.after(V)
        for n in range(3):
            self.tt(inv[:, n:n + 1], gs[:, n:n + 1], w["s_in"][:, (0, 0, 1)[n]:(0, 0, 1)[n] + 1], ALU.mult)
        V.after(V)
        V.do(nc.vector.reciprocal(inv, inv))
        for n, name in enumerate(("gate", "up", "down")):
            V.after(PE)
            self.quantize(w[name].rearrange("p o i -> p (o i)"), gs[:, n:n + 1], wq, y, t, sc, P)
            it = w[name].shape[2] // P
            for o in range(w[name].shape[1]):
                cols = wq[:, o * it * P:(o + 1) * it * P]
                self.tp16(cols, wT[name][:, :, o * P:(o + 1) * P], it, o % 4, A)
        xn, xq, xT = take(D, parts=S), take(D, dt=BF16, parts=S), take(KD, S, dt=BF16)
        sg, hids, hq = take(HID, parts=S), take(2, HID, parts=S), take(HID, dt=BF16, parts=S)
        hT = take(8, S, dt=BF16)
        self.settle()

        def enter(b):
            self.norm(x[:, b, :], xn)
            self.quantize(xn, w["s_in"][0:S, 0:1], xq, y[0:S, 0:D], t[0:S, 0:D], sc[0:S, :, 0:D // 16], D // 16)
            self.tp16(xq, xT, KD, 4, V)
            PE.after(V, A)
            for o, name in ((0, "gate"), (2, "up")):
                for half in range(2):
                    self.project(self.bank(o + half, S), [xT[:, k, :] for k in range(KD)],
                                 [wT[name][:, k, half * 512:(half + 1) * 512] for k in range(KD)])
            return PE.mark()

        def activate(hid, products):
            A.after(products, V)
            self.act(sg.rearrange("p (h n) -> p h n", h=2), self.banks[0:S, 0:2, :], ACT.Silu, scale=inv[0:S, 0:1])
            V.after(A, products)
            self.stt(hid.rearrange("p (h n) -> p h n", h=2), self.banks[0:S, 2:4, :], inv[0:S, 1:2],
                     sg.rearrange("p (h n) -> p h n", h=2), ALU.mult, ALU.mult)
        activate(hids[:, 0, :], enter(0))

        def pair(i):
            for p in range(2):
                b = i * 2 + p
                products = enter(b + 1)
                self.quantize(hids[:, p, :], w["s_in"][0:S, 1:2], hq, y[0:S, 0:HID], t[0:S, 0:HID],
                              sc[0:S, :, 0:HID // 16], HID // 16)
                self.tp16(hq, hT, 8, 5, A)
                PE.after(A)
                self.project(self.bank(6, S, D), [hT[:, k, :] for k in range(8)], [wT["down"][:, k, :] for k in range(8)])
                down = PE.mark()
                activate(hids[:, 1 - p, :], products)
                V.after(down)
                self.stt(x[:, b, :], self.bank(6, S, D), inv[0:S, 2:3], x[:, b, :], ALU.mult, ALU.add)
        self.prog.loop("l3_ffn", B // 2, pair)

SUBLAYERS = (Decoder.l0_attn, Decoder.l0_xattn, Decoder.l0_ffn, Decoder.l1_attn, Decoder.l1_xattn, Decoder.l1_ffn,
             Decoder.l2_attn, Decoder.l2_xattn, Decoder.l2_ffn, Decoder.l3_attn, Decoder.l3_xattn, Decoder.l3_ffn)


def build(nc, ins, layouts, out, per_turn, stages=None):
    from contextlib import ExitStack
    with ExitStack() as stack:
        d = Decoder(nc, stack, ins, layouts, out, per_turn)
        d.start()
        for stage in stages or SUBLAYERS:
            stage(d)
        d.SP.after(*d.compute, d.CTX)
        done = Lane(d.prog, "out_stored", nc.sync, 16)
        done.do(nc.sync.dma_start(out, d.x[:, 0:B, :]))
        nc.sync.wait_ge(done.sem, 16)
        return d.prog.counted


def lay_out(i):
    f = lambda name: np.asarray(i[name])

    def inout(w):
        return w.reshape(-1, P, w.shape[1]).transpose(1, 0, 2)

    def col(b):
        return b.reshape(-1, P).T

    def row(b):
        return np.broadcast_to(b[None, :], (P, b.shape[0]))

    def pad(a):
        return np.concatenate([a, np.zeros((P - a.shape[0],) + a.shape[1:], a.dtype)], 0)

    packs = {}
    iota = np.arange(S)
    dist = iota[:, None] - iota[None, :]
    near = np.where(np.abs(dist) <= 3, np.exp(-(dist.astype(np.float32) ** 2) / np.float32(2.0 * 0.4 ** 2)), 0.0)
    near = near / (near.sum(-1, keepdims=True) + 1e-10)
    c32 = lambda a: np.ascontiguousarray(a, np.float32)
    packs["consts"] = {
        "ident": np.eye(P, dtype=np.float32),
        "causal": pad(c32(np.where(dist >= 0, 0.0, MASKED))),
        "upperT": pad(c32(dist > 0)),
        "rows16": c32(np.arange(P)[:, None] // 16 == np.arange(8)),
        "rows32": c32(np.arange(P)[:, None] // 32 == np.arange(4)),
        "rows64": c32(np.arange(P)[:, None] // 64 == np.arange(2)),
        "prefix": pad(c32(dist.T >= 0)),
        "ones": np.ones((P, S), np.float32),
        "turn8": row(c32(8 - np.arange(8))),
        "spread": pad(c32((1.0 - 0.6) * near.T)),
    }
    order = [0, 1, 3, 2]
    gates = lambda w: w.reshape(4, D, -1)[order].reshape(4 * D, -1)
    both = lambda n: np.stack([inout(gates(f(f"L0_attn_{n}_q")).T), inout(gates(f(f"L0_attn_{n}_k")).T)], 1)
    wk2 = f("L0_attn_Wk2").reshape(4, 64, 64)
    packs["l0a"] = {
        "wih": both("Wih"),
        "wq1": inout(f("L0_attn_Wq1").T), "wk1": inout(f("L0_attn_Wk1").T),
        "wq2": pad(f("L0_attn_Wq2").T),
        "wk2": pad(np.stack([wk2, wk2], 1).reshape(512, 64).T),
        "wv": inout(f("L0_attn_Wv").T), "wo": inout(f("L0_attn_Wo").T),
    }
    bk2 = f("L0_attn_bk2").reshape(4, 64)
    packs["l0a_whh"] = {"whh": both("Whh")}
    packs["l0a_bias"] = {
        "b_lstm": np.concatenate([col(gates(f("L0_attn_b_q"))[:, 0]), col(gates(f("L0_attn_b_k"))[:, 0])], 1),
        "bq1": pad(f("L0_attn_bq1")[:, None]), "bk1": pad(f("L0_attn_bk1")[:, None]),
        "bq2": col(f("L0_attn_bq2")), "bk2": np.concatenate([bk2, bk2], 1).T,
        "bv": row(f("L0_attn_bv")),
    }
    packs["l0x"] = {"wq": inout(f("L0_xattn_Wq")), "wk": inout(f("L0_xattn_Wk")), "wv": inout(f("L0_xattn_Wv")),
                    "bq": col(f("L0_xattn_bq")), "bk": col(f("L0_xattn_bk")), "bv": row(f("L0_xattn_bv"))}
    packs["l0f"] = {"wg": inout(f("L0_ffn_w_gate").T), "wu": inout(f("L0_ffn_w_up").T),
                    "wd": inout(f("L0_ffn_w_down").T)}
    packs["l1a"] = {"wq": inout(f("L1_attn_Wq").T), "wk": inout(f("L1_attn_Wk").T), "wv": inout(f("L1_attn_Wv").T),
                    "wo": inout(f("L1_attn_Wo").T), "bq": col(f("L1_attn_bq")), "bk": col(f("L1_attn_bk")),
                    "bv": row(f("L1_attn_bv")), "bo": row(f("L1_attn_bo"))}
    packs["l1x"] = {"wq": inout(f("L1_xattn_Wq")), "wk": inout(f("L1_xattn_Wk")), "wv": inout(f("L1_xattn_Wv")),
                    "wo": inout(f("L1_xattn_Wo")), "bq": col(f("L1_xattn_bq")), "bk": col(f("L1_xattn_bk")),
                    "bv": row(f("L1_xattn_bv")), "bo": row(f("L1_xattn_bo"))}
    packs["l1f"] = {
        "router": inout(f("L1_ffn_gate_w").T),
        "dg": np.concatenate([inout(w.T) for w in f("L1_ffn_dyn_gate_w")], 2),
        "du": np.concatenate([inout(w.T) for w in f("L1_ffn_dyn_up_w")], 2),
        "dd": np.concatenate([inout(w.T) for w in f("L1_ffn_dyn_down_w")], 1),
        "sg": inout(f("L1_ffn_sh_gate_w")[0].T), "su": inout(f("L1_ffn_sh_up_w")[0].T),
        "sd": inout(f("L1_ffn_sh_down_w")[0].T),
    }
    packs["l2a"] = {"wq": inout(f("L2_attn_Wq")), "wk": inout(f("L2_attn_Wk")),
                    "wv": inout(f("L2_attn_Wv")), "wo": inout(f("L2_attn_Wo"))}
    inv_freq = (1.0 / np.float32(10000.0) ** (np.arange(0, P, 2, dtype=np.float32) / np.float32(P))).astype(np.float32)
    angle = np.outer(np.concatenate([inv_freq, inv_freq]), iota.astype(np.float32)).astype(np.float32)
    sign = np.where(np.arange(P) < P // 2, 1.0, -1.0)[:, None]
    unit = 1.0 / np.sqrt(np.float32(P))
    packs["rope"] = {"cosq": c32(np.cos(angle) * unit), "sinq": c32(np.sin(angle) * sign * unit),
                     "cos": c32(np.cos(angle)), "sin": c32(np.sin(angle) * sign)}
    x2 = lambda n: f(f"L2_xattn_{n}")
    heads = lambda w: inout(w.transpose(1, 0, 2).reshape(w.shape[1], -1))
    packs["l2x"] = {"a1_wq": heads(x2("a1_wq")), "a1_wk": heads(x2("a1_wk")), "a1_wv": heads(x2("a1_wv")),
                    "a1_li1": inout(x2("a1_li1_w")), "a1_li2": inout(x2("a1_li2_w")), "a1_li3": inout(x2("a1_li3_w")),
                    "a2_wq": heads(x2("a2_wq")), "a2_wk": heads(x2("a2_wk")), "a2_wv": heads(x2("a2_wv")),
                    "a2_li1": inout(x2("a2_li1_w")), "a2_li2": inout(x2("a2_li2_w")), "a2_li3": inout(x2("a2_li3_w"))}
    cols = [col(x2(n)) for n in ("a1_lnx_g", "a1_lnx_b", "a1_lny_g", "a1_lny_b", "a1_ln3_g", "a1_ln3_b",
                                 "a2_lnx_g", "a2_lnx_b", "a2_ln3_g", "a2_ln3_b", "a2_lny_g", "a2_lny_b")]
    packs["l2x_rows"] = {
        "rows": np.stack([row(x2(n)) for n in ("ln1_g", "ln1_b", "ln2_g", "ln2_b", "a1_li1_b", "a1_li3_b",
                                               "a2_li1_b", "a2_li3_b")], 1),
        "cols": np.concatenate(cols + [np.zeros((P, 10), np.float32), col(x2("a1_li2_b")), col(x2("a2_li2_b"))], 1)}
    l2 = lambda n: f(f"L2_ffn_{n}")
    packs["l2f"] = {"w1": inout(l2("w1_w").T), "w2": inout(l2("w2_w").T), "h1": inout(l2("h1_w").T),
                    "w3": inout(l2("w3_w").T)}
    packs["l2f2"] = {"h2": inout(l2("h2_w").T)}
    packs["l2f_scales"] = {"s1": col(l2("w1_s")), "s2": col(l2("w2_s")), "h1s": col(l2("h1_s")),
                           "h2s": col(l2("h2_s")), "s3": row(l2("w3_s"))}
    by_depth = lambda w: w.reshape(-1, 8, 5).transpose(0, 2, 1).reshape(-1, 40)
    packs["l3a"] = {"wp": inout(by_depth(f("L3_attn_Wp"))), "bp": pad(by_depth(f("L3_attn_bp")[None])[0][:, None]),
                    "half_eye": pad(c32(0.5 * np.eye(40))),
                    "wv": inout(f("L3_attn_Wv")), "wo": inout(f("L3_attn_Wo"))}
    wkv = f("L3_xattn_Wkv")
    packs["l3x"] = {"wq": inout(f("L3_xattn_Wq").T), "wk": inout(wkv[0:D].T), "wv": inout(wkv[D:2 * D].T),
                    "wo": inout(f("L3_xattn_Wo").T)}
    natural = lambda w: w.reshape(-1, P, w.shape[1]).transpose(1, 0, 2)
    packs["l3f"] = {"gate": natural(f("L3_ffn_gate_w")), "up": natural(f("L3_ffn_up_w")),
                    "down": natural(f("L3_ffn_down_w")),
                    "s_in": row(np.concatenate([f("L3_ffn_s_in"), f("L3_ffn_s_in_down")]))}
    arrays = {"x": np.ascontiguousarray(f("x").transpose(1, 0, 2))}
    ctx = f("ctx_512")
    ahead = np.concatenate([ctx, ctx[:2]], 0)
    arrays["ctxT"] = np.ascontiguousarray(ahead.transpose(0, 2, 1))
    arrays["ctxN"] = np.ascontiguousarray(ahead.reshape(B + 2, CC, CR, CD).transpose(0, 2, 1, 3).reshape(B + 2, CR, -1))
    layouts = {}
    for name, pack in packs.items():
        layouts[name] = [(k, a.shape[1:]) for k, a in pack.items()]
        arrays[name] = np.ascontiguousarray(np.concatenate([a.reshape(P, -1) for a in pack.values()], 1))
    return arrays, layouts


def kernel(**inputs):
    import concourse.bacc as bacc
    from concourse.bass_utils import run_bass_kernel_spmd

    arrays, layouts = lay_out(inputs)
    per_turn = {}
    for _ in range(2):
        nc = bacc.Bacc("TRN2", target_bir_lowering=False, num_devices=1)
        ins = {k: nc.dram_tensor(f"in_{k}", a.shape, mybir.dt.from_np(a.dtype), kind="ExternalInput").ap()
               for k, a in arrays.items()}
        out = nc.dram_tensor("out", (S, B, D), F32, kind="ExternalOutput").ap()
        per_turn = build(nc, ins, layouts, out, per_turn)
    r = run_bass_kernel_spmd(nc, [{f"in_{k}": a for k, a in arrays.items()}], core_ids=[0])
    return np.ascontiguousarray(r.results[0]["out"].transpose(1, 0, 2))
```
